# Optimizing a Trainium2 kernel written in Bass

```python
import numpy as np
import jax
import jax.numpy as jnp

def _softmax(x, axis=-1):
    return jax.nn.softmax(x, axis=axis)

def _gelu(x):
    return jax.nn.gelu(x, approximate=True)

def _silu(x):
    return jax.nn.silu(x)

def _sigmoid(x):
    return jax.nn.sigmoid(x)

def _layernorm(x, axis=-1, eps=1e-05):
    m = jnp.mean(x, axis=axis, keepdims=True)
    v = jnp.var(x, axis=axis, keepdims=True)
    return (x - m) / jnp.sqrt(v + eps)

def _scatter_add(tgt, idx, src, axis=0):
    return tgt.at[idx].add(src)

def _segment_sum(src, seg, n):
    return jax.ops.segment_sum(src, seg, n)
kernel_name = 'mk_decoder_preln_d2_seqx_r4_f46232'

def setup_inputs(seed: int=0):
    np.random.seed(seed)
    _w = jnp.asarray

    def _rec_inputs():
        import jax
        import jax.numpy as jnp
        _rk = jax.random.key(seed)
        x = -0.0002928 + 1 * jax.random.normal(jax.random.fold_in(_rk, 1), (16, 128, 256), jnp.float32)
        _lenS = 128 - jax.random.randint(jax.random.fold_in(_rk, 7), (16,), 0, max(1, 128 // 4) + 1, jnp.int32)
        _lenS2 = 128 - jax.random.randint(jax.random.fold_in(_rk, 8), (16,), 0, max(1, 128 // 4) + 1, jnp.int32)
        _ctx_1024P = jax.random.normal(jax.random.fold_in(_rk, 11), (16, 16, 256), jnp.float32)
        _ctx_1024c = jax.random.dirichlet(jax.random.fold_in(_rk, 511), 0.3 * jnp.ones((16,), jnp.float32), (16, 128))
        _ctx_1024t = jnp.einsum('bsk,bkd->bsd', _ctx_1024c, _ctx_1024P)
        _ctx_1024t = _ctx_1024t * jax.lax.rsqrt(jnp.mean(jnp.square(_ctx_1024t)) + 1e-12) * 0.953939
        ctx_1024 = -1.39393e-06 + 0.999914 * (_ctx_1024t + 0.3 * jax.random.normal(jax.random.fold_in(_rk, 611), (16, 128, 256), jnp.float32))
        _validS = jnp.arange(128)[None, :] < _lenS[:, None]
        _validS2 = jnp.arange(128)[None, :] < _lenS2[:, None]
        _causal = jnp.tril(jnp.ones((128, 128), dtype=bool))
        mask_SxS2_fk0 = jnp.where(jnp.broadcast_to(_validS2[0:1, :], (128, 128)), -1000000000.0, 0.0).astype(jnp.float32)
        mask_BxS2_bf0 = jnp.logical_not(jnp.ones((16, 128), dtype=bool))
        return (x, ctx_1024, mask_SxS2_fk0, mask_BxS2_bf0)
    x, ctx_1024, mask_SxS2_fk0, mask_BxS2_bf0 = _rec_inputs()

    def _L0_attn_setup():
        import jax, jax.numpy as jnp
        import numpy as np
        B, L = (2, 256)
        D_MODEL = 256
        D_STATE = 16
        K = 3
        EXPAND = 1
        D_INNER = D_MODEL * EXPAND

        def _silu(v):
            return v * jax.nn.sigmoid(v)

        def _mamba_fwd(x, W_in, conv_w, W_B, W_C, W_delta, delta_base, W_tau, A_log, W_out):
            residual = x
            z = x @ W_in
            val, gate = jnp.split(z, 2, axis=-1)
            v = jnp.transpose(val, (0, 2, 1))
            v = jax.lax.conv_general_dilated(v, conv_w, window_strides=(1,), padding=[((K - 1) // 2, (K - 1) // 2)], dimension_numbers=('NCH', 'OIH', 'NCH'), feature_group_count=D_INNER)
            val = jnp.transpose(_silu(v), (0, 2, 1))
            B_proj = val @ W_B
            C_proj = val @ W_C
            combined_delta = val @ W_delta + delta_base
            Delta = jax.nn.softplus(combined_delta @ W_tau)
            A = -jnp.exp(A_log)
            dA = Delta[..., None] * A
            A_bar = jnp.exp(dA)
            B_bar = jnp.expm1(dA) / (dA + 1e-06) * Delta[..., None] * B_proj[:, :, None, :]

            def step(h, inp):
                a_t, b_t, c_t, u_t = inp
                h = a_t * h + b_t * u_t[..., None]
                y_t = jnp.sum(h * c_t[:, None, :], axis=-1)
                return (h, y_t)
            h0 = jnp.zeros((x.shape[0], D_INNER, D_STATE), dtype=x.dtype)
            xs = (jnp.moveaxis(A_bar, 1, 0), jnp.moveaxis(B_bar, 1, 0), jnp.moveaxis(C_proj, 1, 0), jnp.moveaxis(val, 1, 0))
            _, ys = jax.lax.scan(step, h0, xs)
            y = jnp.moveaxis(ys, 0, 1)
            out = y * _silu(gate) @ W_out + residual
            return out
        key = jax.random.key(seed)
        ks = jax.random.split(key, 10)
        s = 0.02
        x = jax.random.normal(ks[0], (B, L, D_MODEL), dtype=jnp.float32)
        W_in = jax.random.normal(ks[1], (D_MODEL, 2 * D_INNER), dtype=jnp.float32) * s
        conv_w = jax.random.normal(ks[2], (D_INNER, 1, K), dtype=jnp.float32) * s
        W_B = jax.random.normal(ks[3], (D_INNER, D_STATE), dtype=jnp.float32) * s
        W_C = jax.random.normal(ks[4], (D_INNER, D_STATE), dtype=jnp.float32) * s
        W_delta = jax.random.normal(ks[5], (D_INNER, D_MODEL), dtype=jnp.float32) * s
        delta_base = jax.random.normal(ks[6], (D_MODEL,), dtype=jnp.float32)
        W_tau = jax.random.normal(ks[7], (D_MODEL, D_MODEL), dtype=jnp.float32) * s
        A_log = jnp.tile(jnp.log(jnp.arange(1, D_STATE + 1, dtype=jnp.float32)), (D_MODEL, 1))
        W_out = jax.random.normal(ks[8], (D_INNER, D_MODEL), dtype=jnp.float32) * s
        return {'x': x, 'W_in': W_in, 'conv_w': conv_w, 'W_B': W_B, 'W_C': W_C, 'W_delta': W_delta, 'delta_base': delta_base, 'W_tau': W_tau, 'A_log': A_log, 'W_out': W_out}
    _L0_attn_all = _L0_attn_setup()
    _L0_attn_in = {k: v for k, v in _L0_attn_all.items() if k in ('W_in', 'conv_w', 'W_B', 'W_C', 'W_delta', 'delta_base', 'W_tau', 'A_log', 'W_out')}
    del _L0_attn_all

    def _L0_xattn_setup():
        import jax, jax.numpy as jnp
        import numpy as np
        D_MODEL = 256
        NUM_HEADS = 16
        D_K = D_MODEL // NUM_HEADS

        def _split_heads(x, B, S):
            return x.reshape(B, S, NUM_HEADS, D_K).transpose(0, 2, 1, 3)
        key = jax.random.key(seed)
        ks = jax.random.split(key, 12)
        B, S, D = (2, 512, D_MODEL)
        s = 1.0 / np.sqrt(D)
        inp = {'Q': jax.random.normal(ks[0], (B, S, D), jnp.float32), 'K': jax.random.normal(ks[1], (B, S, D), jnp.float32), 'V': jax.random.normal(ks[2], (B, S, D), jnp.float32), 'Wq': jax.random.normal(ks[3], (D, D), jnp.float32) * s, 'bq': jax.random.normal(ks[4], (D,), jnp.float32) * s, 'Wk': jax.random.normal(ks[5], (D, D), jnp.float32) * s, 'bk': jax.random.normal(ks[6], (D,), jnp.float32) * s, 'Wv': jax.random.normal(ks[7], (D, D), jnp.float32) * s, 'bv': jax.random.normal(ks[8], (D,), jnp.float32) * s, 'Wo': jax.random.normal(ks[9], (D, D), jnp.float32) * s, 'bo': jax.random.normal(ks[10], (D,), jnp.float32) * s}
        return inp
    _L0_xattn_all = _L0_xattn_setup()
    _L0_xattn_in = {k: v for k, v in _L0_xattn_all.items() if k in ('Wq', 'bq', 'Wk', 'bk', 'Wv', 'bv', 'Wo', 'bo')}
    del _L0_xattn_all

    def _L0_ffn_setup():
        import jax, jax.numpy as jnp
        import numpy as np
        B, S, D, F, O = (4, 512, 256, 1024, 256)
        E, NS, K = (4, 2, 2)
        key = jax.random.key(seed)
        ks = jax.random.split(key, 6)

        def w(k, shape, fan_in):
            return jax.random.normal(k, shape, jnp.float32) * fan_in ** (-0.5)
        return {'x': jax.random.normal(ks[0], (B, S, D), jnp.float32), 'gate_w': w(ks[1], (D, E), D), 'gate_b': jnp.zeros((E,), jnp.float32), 'sw1': w(ks[2], (NS, D, F), D), 'sb1': jnp.zeros((NS, F), jnp.float32), 'sw2': w(ks[3], (NS, F, O), F), 'sb2': jnp.zeros((NS, O), jnp.float32), 'rw1': w(ks[4], (E, D, F), D), 'rb1': jnp.zeros((E, F), jnp.float32), 'rw2': w(ks[5], (E, F, O), F), 'rb2': jnp.zeros((E, O), jnp.float32)}
    _L0_ffn_all = _L0_ffn_setup()
    _L0_ffn_in = {k: v for k, v in _L0_ffn_all.items() if k in ('gate_w', 'gate_b', 'sw1', 'sb1', 'sw2', 'sb2', 'rw1', 'rb1', 'rw2', 'rb2')}
    del _L0_ffn_all

    def _L1_attn_setup():
        import jax, jax.numpy as jnp
        import numpy as np
        EPS = 1e-06
        HEADS = 8
        DIM_HEAD = 64
        SCALE = 16.0
        DIM = 256
        INNER = HEADS * DIM_HEAD

        def _l2norm(t):
            return t / jnp.clip(jnp.linalg.norm(t, axis=-1, keepdims=True), 1e-12)
        key = jax.random.key(seed)
        k1, k2, k3, k4 = jax.random.split(key, 4)
        b, n = (2, 1024)
        x = jax.random.normal(k1, (b, n, DIM), dtype=jnp.float32)
        Wq = jax.random.normal(k2, (DIM, INNER), dtype=jnp.float32) * 0.02
        Wkv = jax.random.normal(k3, (DIM, 2 * INNER), dtype=jnp.float32) * 0.02
        Wo = jax.random.normal(k4, (INNER, DIM), dtype=jnp.float32) * 0.02
        return {'x': x, 'Wq': Wq, 'Wkv': Wkv, 'Wo': Wo}
    _L1_attn_all = _L1_attn_setup()
    _L1_attn_in = {k: v for k, v in _L1_attn_all.items() if k in ('Wq', 'Wkv', 'Wo')}
    del _L1_attn_all

    def _L1_xattn_setup():
        import jax, jax.numpy as jnp
        import numpy as np
        B, S, E, H = (2, 512, 256, 16)
        D = E // H
        NEG = -1000000000.0
        key = jax.random.key(seed)
        ks = jax.random.split(key, 12)

        def xavier(k, shape):
            fan_in, fan_out = (shape[1], shape[0])
            lim = jnp.sqrt(6.0 / (fan_in + fan_out))
            return jax.random.uniform(k, shape, jnp.float32, -lim, lim)
        inp = {'Q_input': jax.random.normal(ks[0], (B, S, E), jnp.float32), 'K_input': jax.random.normal(ks[1], (B, S, E), jnp.float32), 'V_input': jax.random.normal(ks[2], (B, S, E), jnp.float32), 'causal_mask': jnp.where(jnp.tril(jnp.ones((S, S), bool)), 0.0, NEG).astype(jnp.float32), 'padding_mask': jnp.zeros((B, S), bool), 'W_q': xavier(ks[3], (E, E)), 'b_q': jnp.zeros((E,), jnp.float32), 'W_k': xavier(ks[4], (E, E)), 'b_k': jnp.zeros((E,), jnp.float32), 'W_v': xavier(ks[5], (E, E)), 'b_v': jnp.zeros((E,), jnp.float32), 'W_o': xavier(ks[6], (E, E)), 'b_o': jnp.zeros((E,), jnp.float32)}
        return inp
    _L1_xattn_all = _L1_xattn_setup()
    _L1_xattn_in = {k: v for k, v in _L1_xattn_all.items() if k in ('W_q', 'b_q', 'W_k', 'b_k', 'W_v', 'b_v', 'W_o', 'b_o')}
    del _L1_xattn_all

    def _L1_ffn_setup():
        import jax, jax.numpy as jnp
        import numpy as np
        B, S, D, F, E = (2, 512, 256, 1024, 8)
        LN_EPS = 1e-05

        def _layer_norm(x, gamma, beta):
            mu = jnp.mean(x, axis=-1, keepdims=True)
            var = jnp.mean(jnp.square(x - mu), axis=-1, keepdims=True)
            return (x - mu) * jax.lax.rsqrt(var + LN_EPS) * gamma + beta
        key = jax.random.key(seed)
        ks = jax.random.split(key, 8)

        def xavier(k, shape):
            fan_in, fan_out = (shape[-1], shape[-2])
            a = jnp.sqrt(6.0 / (fan_in + fan_out))
            return jax.random.uniform(k, shape, jnp.float32, -a, a)
        return {'tgt': jax.random.normal(ks[0], (B, S, D), jnp.float32), 'Wr': xavier(ks[1], (E, D)), 'br': jnp.zeros((E,), jnp.float32), 'W1': xavier(ks[2], (E, F, D)), 'b1': jnp.zeros((E, F), jnp.float32), 'W2': xavier(ks[3], (E, D, F)), 'b2': jnp.zeros((E, D), jnp.float32), 'gamma': jnp.ones((D,), jnp.float32), 'beta': jnp.zeros((D,), jnp.float32)}
    _L1_ffn_all = _L1_ffn_setup()
    _L1_ffn_in = {k: v for k, v in _L1_ffn_all.items() if k in ('Wr', 'br', 'W1', 'b1', 'W2', 'b2', 'gamma', 'beta')}
    del _L1_ffn_all
    return {'x': x, 'ctx_1024': ctx_1024, 'mask_SxS2_fk0': mask_SxS2_fk0, 'mask_BxS2_bf0': mask_BxS2_bf0, 'L0_attn_W_in': _L0_attn_in['W_in'], 'L0_attn_conv_w': _L0_attn_in['conv_w'], 'L0_attn_W_B': _L0_attn_in['W_B'], 'L0_attn_W_C': _L0_attn_in['W_C'], 'L0_attn_W_delta': _L0_attn_in['W_delta'], 'L0_attn_delta_base': _L0_attn_in['delta_base'], 'L0_attn_W_tau': _L0_attn_in['W_tau'], 'L0_attn_A_log': _L0_attn_in['A_log'], 'L0_attn_W_out': _L0_attn_in['W_out'], 'L0_xattn_Wq': _L0_xattn_in['Wq'], 'L0_xattn_bq': _L0_xattn_in['bq'], 'L0_xattn_Wk': _L0_xattn_in['Wk'], 'L0_xattn_bk': _L0_xattn_in['bk'], 'L0_xattn_Wv': _L0_xattn_in['Wv'], 'L0_xattn_bv': _L0_xattn_in['bv'], 'L0_xattn_Wo': _L0_xattn_in['Wo'], 'L0_xattn_bo': _L0_xattn_in['bo'], 'L0_ffn_gate_w': _L0_ffn_in['gate_w'], 'L0_ffn_gate_b': _L0_ffn_in['gate_b'], 'L0_ffn_sw1': _L0_ffn_in['sw1'], 'L0_ffn_sb1': _L0_ffn_in['sb1'], 'L0_ffn_sw2': _L0_ffn_in['sw2'], 'L0_ffn_sb2': _L0_ffn_in['sb2'], 'L0_ffn_rw1': _L0_ffn_in['rw1'], 'L0_ffn_rb1': _L0_ffn_in['rb1'], 'L0_ffn_rw2': _L0_ffn_in['rw2'], 'L0_ffn_rb2': _L0_ffn_in['rb2'], 'L1_attn_Wq': _L1_attn_in['Wq'], 'L1_attn_Wkv': _L1_attn_in['Wkv'], 'L1_attn_Wo': _L1_attn_in['Wo'], 'L1_xattn_W_q': _L1_xattn_in['W_q'], 'L1_xattn_b_q': _L1_xattn_in['b_q'], 'L1_xattn_W_k': _L1_xattn_in['W_k'], 'L1_xattn_b_k': _L1_xattn_in['b_k'], 'L1_xattn_W_v': _L1_xattn_in['W_v'], 'L1_xattn_b_v': _L1_xattn_in['b_v'], 'L1_xattn_W_o': _L1_xattn_in['W_o'], 'L1_xattn_b_o': _L1_xattn_in['b_o'], 'L1_ffn_Wr': _L1_ffn_in['Wr'], 'L1_ffn_br': _L1_ffn_in['br'], 'L1_ffn_W1': _L1_ffn_in['W1'], 'L1_ffn_b1': _L1_ffn_in['b1'], 'L1_ffn_W2': _L1_ffn_in['W2'], 'L1_ffn_b2': _L1_ffn_in['b2'], 'L1_ffn_gamma': _L1_ffn_in['gamma'], 'L1_ffn_beta': _L1_ffn_in['beta']}

def reference(x, ctx_1024, mask_SxS2_fk0, mask_BxS2_bf0, L0_attn_W_in, L0_attn_conv_w, L0_attn_W_B, L0_attn_W_C, L0_attn_W_delta, L0_attn_delta_base, L0_attn_W_tau, L0_attn_A_log, L0_attn_W_out, L0_xattn_Wq, L0_xattn_bq, L0_xattn_Wk, L0_xattn_bk, L0_xattn_Wv, L0_xattn_bv, L0_xattn_Wo, L0_xattn_bo, L0_ffn_gate_w, L0_ffn_gate_b, L0_ffn_sw1, L0_ffn_sb1, L0_ffn_sw2, L0_ffn_sb2, L0_ffn_rw1, L0_ffn_rb1, L0_ffn_rw2, L0_ffn_rb2, L1_attn_Wq, L1_attn_Wkv, L1_attn_Wo, L1_xattn_W_q, L1_xattn_b_q, L1_xattn_W_k, L1_xattn_b_k, L1_xattn_W_v, L1_xattn_b_v, L1_xattn_W_o, L1_xattn_b_o, L1_ffn_Wr, L1_ffn_br, L1_ffn_W1, L1_ffn_b1, L1_ffn_W2, L1_ffn_b2, L1_ffn_gamma, L1_ffn_beta):
    import jax
    import jax.numpy as jnp

    def _L0_attn_ref(x, W_in, conv_w, W_B, W_C, W_delta, delta_base, W_tau, A_log, W_out):
        import jax, jax.numpy as jnp
        import numpy as np
        B, L = (2, 256)
        D_MODEL = 256
        D_STATE = 16
        K = 3
        EXPAND = 1
        D_INNER = D_MODEL * EXPAND

        def _silu(v):
            return v * jax.nn.sigmoid(v)

        def _mamba_fwd(x, W_in, conv_w, W_B, W_C, W_delta, delta_base, W_tau, A_log, W_out):
            residual = x
            z = x @ W_in
            val, gate = jnp.split(z, 2, axis=-1)
            v = jnp.transpose(val, (0, 2, 1))
            v = jax.lax.conv_general_dilated(v, conv_w, window_strides=(1,), padding=[((K - 1) // 2, (K - 1) // 2)], dimension_numbers=('NCH', 'OIH', 'NCH'), feature_group_count=D_INNER)
            val = jnp.transpose(_silu(v), (0, 2, 1))
            B_proj = val @ W_B
            C_proj = val @ W_C
            combined_delta = val @ W_delta + delta_base
            Delta = jax.nn.softplus(combined_delta @ W_tau)
            A = -jnp.exp(A_log)
            dA = Delta[..., None] * A
            A_bar = jnp.exp(dA)
            B_bar = jnp.expm1(dA) / (dA + 1e-06) * Delta[..., None] * B_proj[:, :, None, :]

            def step(h, inp):
                a_t, b_t, c_t, u_t = inp
                h = a_t * h + b_t * u_t[..., None]
                y_t = jnp.sum(h * c_t[:, None, :], axis=-1)
                return (h, y_t)
            h0 = jnp.zeros((x.shape[0], D_INNER, D_STATE), dtype=x.dtype)
            xs = (jnp.moveaxis(A_bar, 1, 0), jnp.moveaxis(B_bar, 1, 0), jnp.moveaxis(C_proj, 1, 0), jnp.moveaxis(val, 1, 0))
            _, ys = jax.lax.scan(step, h0, xs)
            y = jnp.moveaxis(ys, 0, 1)
            out = y * _silu(gate) @ W_out + residual
            return out
        return _mamba_fwd(x, W_in, conv_w, W_B, W_C, W_delta, delta_base, W_tau, A_log, W_out)

    def _L0_xattn_ref(Q, K, V, Wq, bq, Wk, bk, Wv, bv, Wo, bo):
        import jax, jax.numpy as jnp
        import numpy as np
        D_MODEL = 256
        NUM_HEADS = 16
        D_K = D_MODEL // NUM_HEADS

        def _split_heads(x, B, S):
            return x.reshape(B, S, NUM_HEADS, D_K).transpose(0, 2, 1, 3)
        B, S, D = Q.shape
        q = _split_heads(Q @ Wq.T + bq, B, S)
        k = _split_heads(K @ Wk.T + bk, B, S)
        v = _split_heads(V @ Wv.T + bv, B, S)
        scale = 1.0 / np.sqrt(D_K).astype(np.float32)
        scores = jnp.einsum('bhqd,bhkd->bhqk', q, k) * scale
        probs = jax.nn.softmax(scores, axis=-1)
        out = jnp.einsum('bhqk,bhkd->bhqd', probs, v)
        out = out.transpose(0, 2, 1, 3).reshape(B, S, D)
        return out @ Wo.T + bo

    def _L0_ffn_ref(x, gate_w, gate_b, sw1, sb1, sw2, sb2, rw1, rb1, rw2, rb2):
        import jax, jax.numpy as jnp
        import numpy as np
        B, S, D, F, O = (4, 512, 256, 1024, 256)
        E, NS, K = (4, 2, 2)
        weights = jax.nn.softmax(x @ gate_w + gate_b, axis=-1)
        topk_w, topk_i = jax.lax.top_k(weights, K)
        sh = jax.nn.relu(jnp.einsum('bsd,ndf->bsnf', x, sw1) + sb1)
        shared = (jnp.einsum('bsnf,nfo->bsno', sh, sw2) + sb2).sum(axis=2) / NS
        rh = jax.nn.relu(jnp.einsum('bsd,edf->bsef', x, rw1) + rb1)
        eo = jnp.einsum('bsef,efo->bseo', rh, rw2) + rb2
        gathered = jnp.take_along_axis(eo, topk_i[..., None], axis=2)
        routed = (gathered * topk_w[..., None]).sum(axis=2)
        return shared + routed

    def _L1_attn_ref(x, Wq, Wkv, Wo):
        import jax, jax.numpy as jnp
        import numpy as np
        EPS = 1e-06
        HEADS = 8
        DIM_HEAD = 64
        SCALE = 16.0
        DIM = 256
        INNER = HEADS * DIM_HEAD

        def _l2norm(t):
            return t / jnp.clip(jnp.linalg.norm(t, axis=-1, keepdims=True), 1e-12)
        b, n, _ = x.shape
        q = (x @ Wq).reshape(b, n, HEADS, DIM_HEAD).transpose(0, 2, 1, 3)
        kv = x @ Wkv
        k = kv[..., :INNER].reshape(b, n, HEADS, DIM_HEAD).transpose(0, 2, 1, 3)
        v = kv[..., INNER:].reshape(b, n, HEADS, DIM_HEAD).transpose(0, 2, 1, 3)
        q = _l2norm(q)
        k = _l2norm(k)
        logits = jnp.einsum('bhid,bhjd->bhij', q, k) * SCALE - SCALE
        p = jnp.exp(logits)
        row_sums = jnp.clip(p.sum(axis=-1, keepdims=True), EPS)
        out = jnp.einsum('bhij,bhjd->bhid', p, v) / row_sums
        out = out.transpose(0, 2, 1, 3).reshape(b, n, INNER)
        return out @ Wo

    def _L1_xattn_ref(Q_input, K_input, V_input, causal_mask, padding_mask, W_q, b_q, W_k, b_k, W_v, b_v, W_o, b_o):
        import jax, jax.numpy as jnp
        import numpy as np
        B, S, E, H = (2, 512, 256, 16)
        D = E // H
        NEG = -1000000000.0
        b = Q_input.shape[0]

        def proj(x, W, bias):
            y = x @ W.T + bias
            return y.reshape(b, -1, H, D).transpose(0, 2, 1, 3)
        Q = proj(Q_input, W_q, b_q)
        K = proj(K_input, W_k, b_k)
        V = proj(V_input, W_v, b_v)
        scale = 1.0 / jnp.sqrt(jnp.float32(D))
        scores = jnp.einsum('bhqd,bhkd->bhqk', Q, K) * scale
        scores = jnp.where(padding_mask[:, None, None, :], NEG, scores)
        scores = scores + causal_mask
        attn = jax.nn.softmax(scores, axis=-1)
        ctx = jnp.einsum('bhqk,bhkd->bhqd', attn, V)
        ctx = ctx.transpose(0, 2, 1, 3).reshape(b, -1, E)
        return ctx @ W_o.T + b_o

    def _L1_ffn_ref(tgt, Wr, br, W1, b1, W2, b2, gamma, beta):
        import jax, jax.numpy as jnp
        import numpy as np
        B, S, D, F, E = (2, 512, 256, 1024, 8)
        LN_EPS = 1e-05

        def _layer_norm(x, gamma, beta):
            mu = jnp.mean(x, axis=-1, keepdims=True)
            var = jnp.mean(jnp.square(x - mu), axis=-1, keepdims=True)
            return (x - mu) * jax.lax.rsqrt(var + LN_EPS) * gamma + beta
        logits = jnp.einsum('bsd,ed->bse', tgt, Wr) + br
        top_v, top_i = jax.lax.top_k(logits, 2)
        top_w = jax.nn.softmax(top_v, axis=-1)
        n_exp = logits.shape[-1]
        router_w = jnp.sum(jax.nn.one_hot(top_i, n_exp, dtype=top_w.dtype) * top_w[..., None], axis=-2)
        h = jnp.einsum('bsd,efd->bsef', tgt, W1) + b1
        h = jax.nn.relu(h)
        o = jnp.einsum('bsef,edf->bsed', h, W2) + b2
        tgt2 = jnp.einsum('bsed,bse->bsd', o, router_w)
        return _layer_norm(tgt + tgt2, gamma, beta)
    x = x + _L0_attn_ref(_layernorm(x, axis=-1), L0_attn_W_in, L0_attn_conv_w, L0_attn_W_B, L0_attn_W_C, L0_attn_W_delta, L0_attn_delta_base, L0_attn_W_tau, L0_attn_A_log, L0_attn_W_out)
    x = x + _L0_xattn_ref(_layernorm(x, axis=-1), ctx_1024, ctx_1024, L0_xattn_Wq, L0_xattn_bq, L0_xattn_Wk, L0_xattn_bk, L0_xattn_Wv, L0_xattn_bv, L0_xattn_Wo, L0_xattn_bo)
    x = x + _L0_ffn_ref(_layernorm(x, axis=-1), L0_ffn_gate_w, L0_ffn_gate_b, L0_ffn_sw1, L0_ffn_sb1, L0_ffn_sw2, L0_ffn_sb2, L0_ffn_rw1, L0_ffn_rb1, L0_ffn_rw2, L0_ffn_rb2)
    x = x + _L1_attn_ref(_layernorm(x, axis=-1), L1_attn_Wq, L1_attn_Wkv, L1_attn_Wo)
    x = x + _L1_xattn_ref(_layernorm(x, axis=-1), ctx_1024, ctx_1024, mask_SxS2_fk0, mask_BxS2_bf0, L1_xattn_W_q, L1_xattn_b_q, L1_xattn_W_k, L1_xattn_b_k, L1_xattn_W_v, L1_xattn_b_v, L1_xattn_W_o, L1_xattn_b_o)
    x = x + _L1_ffn_ref(_layernorm(x, axis=-1), L1_ffn_Wr, L1_ffn_br, L1_ffn_W1, L1_ffn_b1, L1_ffn_W2, L1_ffn_b2, L1_ffn_gamma, L1_ffn_beta)
    return x

_drawn_inputs = setup_inputs


def setup_inputs(seed=0):
    import zlib

    import numpy as np

    out = dict(_drawn_inputs(seed))
    spreads = {'mask_SxS2_fk0': (-1000000000.0, 0.2),
     'L0_ffn_gate_b': (0.0, 0.27),
     'L0_ffn_sb1': (0.0, 0.318),
     'L0_ffn_sb2': (0.0, 0.287),
     'L0_ffn_rb1': (0.0, 0.372),
     'L0_ffn_rb2': (0.0, 0.268),
     'L1_xattn_b_q': (0.0, 0.1),
     'L1_xattn_b_k': (0.0, 0.1),
     'L1_xattn_b_v': (0.0, 0.1),
     'L1_xattn_b_o': (0.0, 0.1),
     'L1_ffn_br': (0.0, 0.379),
     'L1_ffn_b1': (0.0, 0.413),
     'L1_ffn_b2': (0.0, 0.372),
     'L1_ffn_gamma': (1.0, 0.2),
     'L1_ffn_beta': (0.0, 0.282)}
    factors = {'L0_attn_W_in': 8.0,
     'L0_attn_conv_w': 8.0,
     'L0_attn_W_B': 8.0,
     'L0_attn_W_C': 8.0,
     'L0_attn_delta_base': 8.0,
     'L0_attn_W_tau': 8.0,
     'L0_attn_A_log': 8.0,
     'L0_attn_W_out': 8.0,
     'L0_xattn_bq': 5.345,
     'L0_xattn_bk': 200.0,
     'L1_attn_Wq': 30.141,
     'L0_attn_W_delta': 2.707}
    for name, (base, spread) in spreads.items():
        noise = np.random.default_rng([zlib.crc32(name.encode()), seed]).standard_normal(out[name].shape)
        drawn = base * np.exp(spread * noise) if base else spread * noise
        out[name] = jnp.asarray(drawn.astype(out[name].dtype))
    for name, factor in factors.items():
        out[name] = (out[name] * factor).astype(out[name].dtype)
    return out
```

```python
from contextlib import ExitStack

import numpy as np

import concourse.bass as bass
from concourse import mybir

ALU = mybir.AluOpType
ACT = mybir.ActivationFunctionType
AX = mybir.AxisListType
F32 = mybir.dt.float32
F32R = mybir.dt.float32r
U8 = mybir.dt.uint8

P = 128
BATCH, SEQ, DM = 16, 128, 256
TILES = BATCH
KT = DM // P
GB = 4
GROUPS = TILES // GB
GT = GB * SEQ
LN_EPS = 1e-5


class Chain:

    def __init__(self, engine, sem):
        self.engine, self.sem = engine, sem
        self.done, self.base, self.inside = 0, 0, None

    def link(self, instruction):
        instruction.then_inc(self.sem, 1)
        self.done += 1
        self.engine.wait_ge(self.sem, self.base + self.done)

    def enter(self, turn, links):
        self.before, self.links = self.done, links
        self.base, self.done = turn * links + self.before, 0

    def leave(self, turns):
        assert self.done == self.links, (self.done, self.links)
        self.base, self.done = 0, self.before + turns * self.links


class Core:

    def __init__(self, nc, ctx):
        self.nc, self.ctx = nc, ctx

    def sem(self, name):
        return self.ctx.enter_context(self.nc.semaphore(name))

    def stage_sems(self, prefix, names):
        return {n: self.nc.alloc_semaphore(prefix + n) for n in names.split()}

    def retire(self, sems):
        nc, handles = self.nc, list(sems.values())
        numbers = sorted(h.num for h in handles)
        with nc.Block() as block:
            @block.sync
            def _(sp):
                at = 0
                while at < len(numbers):
                    end = at
                    while end + 1 < len(numbers) and numbers[end + 1] == numbers[end] + 1:
                        end += 1
                    sp.sem_clear(range(numbers[at], numbers[end] + 1))
                    at = end + 1
        for h in handles:
            nc.release_semaphore(h)

    def keep(self, name, shape, dt=F32):
        return self.ctx.enter_context(self.nc.sbuf_tensor(name, shape, dt))


def product(nc, out, lhs, rhs, first, last, skip=False):
    (lh, ll), (rh, rl) = lhs, rhs
    nc.tensor.matmul(out, lh, rl, start=first, stop=False, skip_group_check=skip)
    nc.tensor.matmul(out, ll, rh, start=False, stop=False, skip_group_check=skip)
    return nc.tensor.matmul(out, lh, rh, start=False, stop=last, skip_group_check=skip)


def variance(core, dve, chain, variance_ready):
    nc, st, ln = core.nc, core.stats, core.ln
    mean, var, diff = ln[:, 0, :], ln[:, 1, :], ln[:, 2, :]
    nc.vector.tensor_tensor(diff, st[:, :, 1], st[:, :, 4], ALU.subtract)
    nc.vector.tensor_tensor(mean, st[:, :, 1], st[:, :, 4], ALU.add)
    chain.link(nc.vector.tensor_tensor(var, st[:, :, 2], st[:, :, 5], ALU.add))
    nc.vector.tensor_scalar(mean, mean, 0.5, None, ALU.mult)
    nc.vector.tensor_scalar(var, var, 1.0 / DM, LN_EPS, ALU.mult, ALU.add)
    chain.link(nc.vector.tensor_tensor(diff, diff, diff, ALU.mult))
    nc.vector.scalar_tensor_tensor(out=var, in0=diff, scalar=0.25, in1=var,
                                   op0=ALU.mult, op1=ALU.add).then_inc(variance_ready, 1)


def inverse_deviation(core, pool, variance_ready, scale_ready):
    pool.wait_ge(variance_ready, 1)
    core.nc.gpsimd.tensor_tensor(core.ln[:, 3, :], core.ln[:, 1, :], core.minus_half[:],
                                 ALU.pow).then_inc(scale_ready, 1)


def normalise(core, out, tile):
    return core.nc.vector.tensor_scalar(out, core.x[:, tile, :], core.ln[:, 0, tile:tile + 1],
                                        core.ln[:, 3, tile:tile + 1], ALU.subtract, ALU.mult)


def load(core, w):
    nc = core.nc
    x_in, st = core.sem("x_in"), core.stats
    ident_set = core.sem("ident_set")
    with nc.Block() as block:
        @block.sync
        def _(sp):
            sp.dma_start(core.x[:], w["x"]).then_inc(x_in, 16)

        @block.gpsimd
        def _(pool):
            nc.gpsimd.memset(core.minus_half[:], -0.5)
            nc.gpsimd.memset(core.ident[:], 0.0).then_inc(ident_set, 1)
            pool.wait_ge(ident_set, 1)
            nc.gpsimd.affine_select(out=core.ident[:], in_=core.ident[:], compare_op=ALU.not_equal,
                                    fill=1.0, base=0, pattern=[[-1, P]], channel_multiplier=1)

        @block.vector
        def _(dve):
            dve.wait_ge(x_in, 16)
            for t in range(TILES):
                nc.vector.bn_stats(st[:, t, :], core.x[:, t, :])


def state_space(core, w):
    nc, x, ident = core.nc, core.x, core.ident
    STATE = w["A_log"].shape[2]
    PAIRS = STATE // 2
    PAD = SEQ + 2
    EPS_DA = 1e-6
    LEAST_A = -1e16

    with ExitStack() as ctx:
        def sb(name, shape, dt=F32):
            return ctx.enter_context(nc.sbuf_tensor("m_" + name, shape, dt))

        def ps(name, shape):
            return ctx.enter_context(nc.psum_tensor("m_" + name, shape, F32))

        w_in = sb("w_in", [P, KT, 2 * DM])
        w_bc = sb("w_bc", [P, KT, P])
        w_delta, w_tau, w_out = (sb(n, [P, KT, DM]) for n in ("w_delta", "w_tau", "w_out"))
        raw = [w_in, w_bc, w_delta, w_tau, w_out]
        split = [(sb(f"hi{i}", t.shape, F32R), sb(f"lo{i}", t.shape, F32R)) for i, t in enumerate(raw)]
        s_in, s_bc, s_delta, s_tau, s_out = split
        conv = sb("conv", [P, KT, 3])
        base = sb("base", [P, KT])
        a_log = sb("a_log", [P, KT, STATE])
        rate = sb("rate", [P, KT, STATE])
        half_rate = sb("half_rate", [P, KT, STATE])
        rate_kept = sb("rate_kept", [P, KT, STATE])
        pick = sb("pick", [2 * 2 * STATE, 2 * STATE])
        pick_r = sb("pick_r", [2 * 2 * STATE, 2 * STATE], F32R)

        xnt = (sb("xnt_hi", [P, KT, GT], F32R), sb("xnt_lo", [P, KT, GT], F32R))
        padded = sb("padded", [P, KT, GB, PAD])
        half_v = sb("half_v", [P, KT, GT])
        tanh_v = sb("tanh_v", [P, KT, GT])
        u = sb("u", [P, KT, GT])
        half_g = sb("half_g", [P, KT, GT])
        gate = sb("gate", [P, KT, GT])
        act = (sb("act_hi", [P, KT, GT], F32R), sb("act_lo", [P, KT, GT], F32R))
        bc = sb("bc", [4 * STATE, GT], F32R)
        delta = sb("delta", [P, KT, GT])
        du = sb("du", [P, KT, GT])
        y = sb("y", [P, KT, GT])
        xn = y[:].rearrange("p k (b d) -> p (k b) d", d=DM)
        den = sb("den", [P, 2, 2, KT, GT])
        inv_pair = sb("inv_pair", [P, 2, KT, GT])
        mult_pair = sb("mult_pair", [P, KT, GT])
        decay = sb("decay", [P, 2, 2, KT, GT])
        em = sb("em", [P, 2, 2, KT, GT])
        inv = sb("inv", [P, 2, KT, GT])
        wb = sb("wb", [P, 2, KT, GT])
        h = sb("h", [P, 2, KT, GT])
        bcs = sb("bcs", [P, 2, 2, GT])

        ps_t = [ps(f"t{i}", [P, GT]) for i in range(2)]
        ps_z = [ps(f"z{i}", [P, GT]) for i in range(2)]
        ps_b = [ps(f"b{i}", [P, GT]) for i in range(4)]

        names = ("w_loaded w_high w_low small_set pick_ready rate_exp rate_set variance_ready scale_ready "
                 "xn_ready xnt_moved xnt_high xnt_low xn_added z_ready z_taken conv_ready tanh_ready u_ready "
                 "u_high u_low bc_ready bc_high bc_low z1_ready z1_high z1_low z2_ready exp_ready one_plus_ready "
                 "ln_ready delta_ready spread_ready spread_taken den_ready pair_inverted inverse_ready em_ready "
                 "ratio_ready weighted_b input_ready state_ready weighted_c y_ready y_high y_low out_ready "
                 "x_updated act_chain chain")
        s = core.stage_sems("m_", names)

        with nc.Block() as block:
            @block.sync
            def _(sp):
                sp.dma_start(w_in[:], w["W_in"]).then_inc(s["w_loaded"], 16)
                sp.dma_start(conv[:], w["conv_w"]).then_inc(s["w_loaded"], 16)
                for r in range(2):
                    for j, name in enumerate(("W_B", "W_C")):
                        at = (2 * r + j) * STATE
                        sp.dma_start(w_bc[:, :, at:at + STATE],
                                     w[name]).then_inc(s["w_loaded"], 16)
                sp.dma_start(w_delta[:], w["W_delta"]).then_inc(s["w_loaded"], 16)
                sp.dma_start(w_tau[:], w["W_tau"]).then_inc(s["w_loaded"], 16)
                sp.dma_start(w_out[:], w["W_out"]).then_inc(s["w_loaded"], 16)
                sp.dma_start(base[:], w["delta_base"]).then_inc(s["w_loaded"], 16)
                sp.dma_start(a_log[:], w["A_log"]).then_inc(s["w_loaded"], 16)
            LOADS = 11

            @block.gpsimd
            def _(pool):
                nc.gpsimd.memset(w_bc[:, :, 4 * STATE:], 0.0).then_inc(s["small_set"], 1)
                nc.gpsimd.memset(padded[:, :, :, 0:PAD:PAD - 1], 0.0).then_inc(s["small_set"], 1)
                nc.gpsimd.memset(pick[:], 0.0).then_inc(s["small_set"], 1)
                pool.wait_ge(s["small_set"], 3)
                for half in range(2):
                    at = pick[:]
                    nc.gpsimd.affine_select(out=at, in_=at, compare_op=ALU.not_equal, fill=1.0,
                                            base=-2 * STATE * half, pattern=[[-1, 2 * STATE]],
                                            channel_multiplier=1).then_inc(s["pick_ready"], 1)
                    pool.wait_ge(s["pick_ready"], half + 1)
                inverse_deviation(core, pool, s["variance_ready"], s["scale_ready"])
                pool.wait_ge(s["w_loaded"], 16 * LOADS)
                for i, (t, (hi, lo)) in enumerate(zip(raw, split)):
                    pool.wait_ge(s["w_high"], i + 1)
                    nc.gpsimd.tensor_tensor(lo[:], t[:], hi[:].bitcast(F32), ALU.subtract).then_inc(s["w_low"], 1)


                pool.sem_inc(s["inverse_ready"], 4)
                pool.sem_inc(s["weighted_b"], 2)
                pool.sem_inc(s["weighted_c"], 1)
                with pool.Fori(0, GROUPS) as g:
                    pool.wait_ge(s["xn_ready"], g + 1)
                    xg = x[:, bass.ds(g * GB, GB), :]
                    nc.gpsimd.tensor_tensor(xg, xg, xn, ALU.add).then_inc(s["xn_added"], 1)
                    pool.wait_ge(s["delta_ready"], g + 1)

                    def weigh_c(p):
                        pool.wait_ge(s["state_ready"], 2 + g * PAIRS + p + 1)
                        pool.wait_ge(s["spread_taken"], 4 + 4 * (g * PAIRS + p) + 4)
                        for k in range(2):
                            c_all = bcs[:, 1, k, :].unsqueeze(1).to_broadcast([P, KT, GT])
                            last = nc.gpsimd.tensor_tensor(h[:, k], h[:, k], c_all, ALU.mult)
                        last.then_inc(s["weighted_c"], 1)

                    for p in range(PAIRS):
                        i = g * PAIRS + p
                        pool.wait_ge(s["pair_inverted"], i + 1)
                        pool.wait_ge(s["ratio_ready"], i + 1)
                        for k in range(2):
                            nc.gpsimd.tensor_tensor(inv[:, k], den[:, p % 2, 1 - k], inv_pair[:, p % 2],
                                                    ALU.mult).then_inc(s["inverse_ready"], 1)
                        pool.wait_ge(s["spread_taken"], 4 + 4 * i + 2)
                        pool.wait_ge(s["input_ready"], i + 1)
                        for k in range(2):
                            b_all = bcs[:, 0, k, :].unsqueeze(1).to_broadcast([P, KT, GT])
                            nc.gpsimd.tensor_tensor(wb[:, k], du[:], b_all, ALU.mult).then_inc(s["weighted_b"], 1)
                        if p:
                            weigh_c(p - 1)
                    weigh_c(PAIRS - 1)

            @block.tensor
            def _(pe):
                pe.wait_ge(s["w_low"], len(raw))
                pe.wait_ge(s["rate_set"], 1)
                with pe.Fori(0, GROUPS) as g:
                    pe.wait_ge(s["xn_ready"], g + 1)
                    for k in range(KT):
                        for t in range(GB):
                            last = nc.tensor.transpose(ps_t[k][:, t * P:(t + 1) * P],
                                                       xn[:, t, k * P:(k + 1) * P], ident[:])
                        last.then_inc(s["xnt_moved"], 1)
                    pe.wait_ge(s["xnt_low"], KT * g + KT)
                    for m in range(2 * KT):
                        if m >= 2:
                            pe.wait_ge(s["z_taken"], 4 * g + m - 1)
                        for k in range(KT):
                            last = product(nc, ps_z[m % 2][:], [a[:, k, m * P:(m + 1) * P] for a in s_in],
                                           [a[:, k, :] for a in xnt], k == 0, k == KT - 1)
                        last.then_inc(s["z_ready"], 1)
                    pe.wait_ge(s["u_low"], g + 1)
                    for k in range(KT):
                        last = product(nc, ps_t[0][:], [a[:, k, :] for a in s_bc],
                                       [a[:, k, :] for a in act], k == 0, k == KT - 1)
                    last.then_inc(s["bc_ready"], 1)
                    for m in range(KT):
                        pe.wait_ge(s["z_taken"], 4 * g + 3 + m)
                        for k in range(KT):
                            last = product(nc, ps_z[m][:], [a[:, k, m * P:(m + 1) * P] for a in s_delta],
                                           [a[:, k, :] for a in act], k == 0, k == KT - 1)
                        last.then_inc(s["z1_ready"], 1)
                    pe.wait_ge(s["z1_low"], KT * g + KT)
                    for m in range(KT):
                        for k in range(KT):
                            last = product(nc, ps_z[m][:], [a[:, k, m * P:(m + 1) * P] for a in s_tau],
                                           [a[:, k, :] for a in xnt], k == 0, k == KT - 1)
                        last.then_inc(s["z2_ready"], 1)
                    pe.wait_ge(s["bc_low"], g + 1)
                    for p in range(PAIRS):
                        for j in range(4):
                            row = (j // 2) * STATE + 2 * p + j % 2
                            if j == 0:
                                pe.wait_ge(s["spread_taken"], 4 * (g * PAIRS + p) + 4)
                            nc.tensor.matmul(ps_b[j][:], pick_r[:, row:row + 1].to_broadcast([4 * STATE, P]), bc[:],
                                             start=True, stop=True).then_inc(s["spread_ready"], 1)
                    pe.wait_ge(s["y_low"], g + 1)
                    for t in range(GB):
                        for k in range(KT):
                            last = product(nc, ps_t[t // 2][:, (t % 2) * DM:(t % 2 + 1) * DM],
                                           [a[:, k, t * P:(t + 1) * P] for a in act],
                                           [a[:, k, :] for a in s_out], k == 0, k == KT - 1)
                        if t % 2:
                            last.then_inc(s["out_ready"], 1)

            @block.scalar
            def _(ac):
                ac.wait_ge(s["w_loaded"], 16 * LOADS)
                ac.wait_ge(s["small_set"], 1)
                for i, (t, (hi, lo)) in enumerate(zip(raw, split)):
                    nc.scalar.activation(hi[:], t[:], ACT.Copy).then_inc(s["w_high"], 1)
                nc.scalar.activation(rate[:], a_log[:], ACT.Exp).then_inc(s["rate_exp"], 1)
                ac.sem_inc(s["spread_taken"], 4)
                ac.wait_ge(s["rate_set"], 1)
                chain = Chain(ac, s["act_chain"])
                with ac.Fori(0, GROUPS) as g:
                    chain.enter(g, KT)
                    for k in range(KT):
                        ac.wait_ge(s["xnt_moved"], KT * g + k + 1)
                        nc.scalar.activation(xnt[0][:, k, :], ps_t[k][:], ACT.Copy).then_inc(s["xnt_high"], 1)
                    for m in range(KT):
                        ac.wait_ge(s["z_ready"], 4 * g + m + 1)
                        nc.scalar.activation(padded[:, m, :, 1:SEQ + 1],
                                             ps_z[m][:].rearrange("p (b s) -> p b s", s=SEQ),
                                             ACT.Copy).then_inc(s["z_taken"], 1)
                    for m in range(KT):
                        ac.wait_ge(s["z_ready"], 4 * g + KT + m + 1)
                        nc.scalar.activation(half_g[:, m, :], ps_z[m][:], ACT.Copy, scale=0.5)
                        nc.scalar.activation(gate[:, m, :], ps_z[m][:], ACT.Tanh,
                                             scale=0.5).then_inc(s["z_taken"], 1)
                    ac.wait_ge(s["conv_ready"], g + 1)
                    nc.scalar.activation(tanh_v[:], half_v[:], ACT.Tanh).then_inc(s["tanh_ready"], 1)
                    ac.wait_ge(s["u_ready"], g + 1)
                    nc.scalar.activation(act[0][:], u[:], ACT.Copy).then_inc(s["u_high"], 1)
                    ac.wait_ge(s["bc_ready"], g + 1)
                    nc.scalar.activation(bc[:], ps_t[0][0:4 * STATE, :], ACT.Copy).then_inc(s["bc_high"], 1)
                    for m in range(KT):
                        ac.wait_ge(s["z1_ready"], KT * g + m + 1)
                        nc.scalar.activation(xnt[0][:, m, :], ps_z[m][:], ACT.Identity,
                                             bias=base[:, m:m + 1]).then_inc(s["z1_high"], 1)
                    for m in range(KT):
                        ac.wait_ge(s["z2_ready"], KT * g + m + 1)
                        chain.link(nc.scalar.activation(tanh_v[:, m, :], ps_z[m][:], ACT.Abs))
                    nc.scalar.activation(tanh_v[:], tanh_v[:], ACT.Exp, scale=-1.0).then_inc(s["exp_ready"], 1)
                    ac.wait_ge(s["one_plus_ready"], g + 1)
                    nc.scalar.activation(du[:], half_v[:], ACT.Ln).then_inc(s["ln_ready"], 1)
                    ac.wait_ge(s["delta_ready"], g + 1)
                    chain.leave(GROUPS)
                    for p in range(PAIRS):
                        i = g * PAIRS + p
                        ac.wait_ge(s["inverse_ready"], 2 * i + 2)
                        for k in range(2):
                            for c in range(KT):
                                n = 2 * p + k
                                last = nc.scalar.activation(den[:, p % 2, k, c, :], delta[:, c, :], ACT.Copy,
                                                            bias=EPS_DA, scale=rate_kept[:, c, n:n + 1])
                        last.then_inc(s["den_ready"], 1)
                        ac.wait_ge(s["state_ready"], i + 1)
                        for k in range(2):
                            for c in range(KT):
                                n = 2 * p + k
                                nc.scalar.activation(em[:, p % 2, k, c, :], delta[:, c, :], ACT.Tanh,
                                                     scale=half_rate[:, c, n:n + 1])
                                last = nc.scalar.activation(decay[:, p % 2, k, c, :], delta[:, c, :], ACT.Exp,
                                                            scale=rate[:, c, n:n + 1])
                        last.then_inc(s["em_ready"], 1)
                        for j in range(4):
                            ac.wait_ge(s["spread_ready"], 4 * i + j + 1)
                            if j == 0:
                                ac.wait_ge(s["weighted_b"], 2 * i + 2)
                            if j == 2:
                                ac.wait_ge(s["weighted_c"], i + 1)
                            nc.scalar.activation(bcs[:, j // 2, j % 2, :], ps_b[j][:],
                                                 ACT.Copy).then_inc(s["spread_taken"], 1)
                    ac.wait_ge(s["y_ready"], g + 1)
                    nc.scalar.activation(act[0][:], y[:], ACT.Copy).then_inc(s["y_high"], 1)

            @block.vector
            def _(dve):
                chain = Chain(dve, s["chain"])
                link = chain.link
                variance(core, dve, chain, s["variance_ready"])
                dve.wait_ge(s["w_loaded"], 16 * LOADS)
                dve.wait_ge(s["small_set"], 2)
                dve.wait_ge(s["pick_ready"], 2)
                nc.vector.tensor_copy(pick_r[:], pick[:])
                nc.vector.tensor_scalar(conv[:], conv[:], 0.5, None, ALU.mult)
                dve.wait_ge(s["rate_exp"], 1)
                nc.vector.tensor_scalar(half_rate[:], rate[:], -0.5, None, ALU.mult)
                nc.vector.tensor_scalar(rate_kept[:], rate[:], -1.0, LEAST_A, ALU.mult, ALU.max)
                nc.vector.tensor_scalar(rate[:], rate[:], -1.0, None, ALU.mult).then_inc(s["rate_set"], 1)
                dve.sem_inc(s["ratio_ready"], 1)
                dve.sem_inc(s["input_ready"], 1)
                dve.sem_inc(s["state_ready"], 2)
                dve.wait_ge(s["scale_ready"], 1)
                with dve.Fori(0, GROUPS) as g:
                    chain.enter(g, 3 + 7 + 2 * PAIRS + (2 * PAIRS - 1) + 1)
                    for t in range(GB):
                        last = nc.vector.tensor_scalar(xn[:, t, :], x[:, bass.ds(g * GB + t, 1), :].squeeze(1),
                                                       core.ln[:, 0, bass.ds(g * GB + t, 1)],
                                                       core.ln[:, 3, bass.ds(g * GB + t, 1)],
                                                       ALU.subtract, ALU.mult)
                    last.then_inc(s["xn_ready"], 1)
                    for k in range(KT):
                        dve.wait_ge(s["xnt_high"], KT * g + k + 1)
                        nc.vector.tensor_tensor(xnt[1][:, k, :], ps_t[k][:], xnt[0][:, k, :].bitcast(F32),
                                                ALU.subtract).then_inc(s["xnt_low"], 1)
                    dve.wait_ge(s["z_taken"], 4 * g + KT)
                    for j in range(3):
                        for c in range(KT):
                            out = half_v[:, c, :].rearrange("p (b s) -> p b s", s=SEQ)
                            src, tap = padded[:, c, :, j:j + SEQ], conv[:, c, j:j + 1]
                            if j == 0:
                                last = nc.vector.tensor_scalar(out, src, tap, None, ALU.mult)
                            else:
                                last = nc.vector.scalar_tensor_tensor(out=out, in0=src, scalar=tap, in1=out,
                                                                      op0=ALU.mult, op1=ALU.add)
                        if j < 2:
                            link(last)
                    last.then_inc(s["conv_ready"], 1)
                    dve.wait_ge(s["tanh_ready"], g + 1)
                    nc.vector.scalar_tensor_tensor(out=u[:], in0=tanh_v[:], scalar=1.0, in1=half_v[:],
                                                   op0=ALU.add, op1=ALU.mult).then_inc(s["u_ready"], 1)
                    dve.wait_ge(s["z_taken"], 4 * g + 2 * KT)
                    link(nc.vector.scalar_tensor_tensor(out=gate[:], in0=gate[:], scalar=1.0, in1=half_g[:],
                                                        op0=ALU.add, op1=ALU.mult))
                    dve.wait_ge(s["u_high"], g + 1)
                    nc.vector.tensor_tensor(act[1][:], u[:], act[0][:].bitcast(F32),
                                            ALU.subtract).then_inc(s["u_low"], 1)
                    dve.wait_ge(s["bc_high"], g + 1)
                    low = slice(2 * STATE, 4 * STATE)
                    nc.vector.tensor_tensor(bc[low, :], ps_t[0][low, :], bc[low, :].bitcast(F32),
                                            ALU.subtract).then_inc(s["bc_low"], 1)
                    for m in range(KT):
                        dve.wait_ge(s["z1_high"], KT * g + m + 1)
                        nc.vector.scalar_tensor_tensor(out=xnt[1][:, m, :], in0=ps_z[m][:], scalar=base[:, m:m + 1],
                                                       in1=xnt[0][:, m, :].bitcast(F32), op0=ALU.add,
                                                       op1=ALU.subtract).then_inc(s["z1_low"], 1)
                    dve.wait_ge(s["exp_ready"], g + 1)
                    dve.wait_ge(s["xn_added"], g + 1)
                    nc.vector.tensor_scalar(half_v[:], tanh_v[:], 1.0, None, ALU.add).then_inc(s["one_plus_ready"], 1)
                    dve.wait_ge(s["one_plus_ready"], g + 1)
                    link(nc.vector.tensor_scalar(y[:], half_v[:], 1.0, None, ALU.is_equal))
                    link(nc.vector.scalar_tensor_tensor(out=delta[:], in0=half_v[:], scalar=-1.0, in1=y[:],
                                                        op0=ALU.add, op1=ALU.add))
                    link(nc.vector.reciprocal(mult_pair[:], delta[:]))
                    dve.wait_ge(s["ln_ready"], g + 1)
                    link(nc.vector.tensor_tensor(du[:], du[:], y[:], ALU.add))
                    link(nc.vector.tensor_tensor(du[:], du[:], mult_pair[:], ALU.mult))
                    link(nc.vector.tensor_tensor(du[:], du[:], tanh_v[:], ALU.mult))
                    for m in range(KT):
                        last = nc.vector.scalar_tensor_tensor(out=delta[:, m, :], in0=ps_z[m][:], scalar=0.0,
                                                              in1=du[:, m, :], op0=ALU.max, op1=ALU.add)
                    link(last)
                    nc.vector.tensor_tensor(du[:], delta[:], u[:], ALU.mult).then_inc(s["delta_ready"], 1)

                    def invert(p):
                        dve.wait_ge(s["den_ready"], g * PAIRS + p + 1)
                        dve.wait_ge(s["inverse_ready"], 2 * (g * PAIRS + p) + 2)
                        if p:
                            dve.wait_ge(s["pair_inverted"], g * PAIRS + p)
                        link(nc.vector.tensor_tensor(mult_pair[:], den[:, p % 2, 0], den[:, p % 2, 1], ALU.mult))
                        nc.vector.reciprocal(inv_pair[:, p % 2], mult_pair[:]).then_inc(s["pair_inverted"], 1)

                    def add_outputs(p):
                        dve.wait_ge(s["weighted_c"], 1 + g * PAIRS + p + 1)
                        if p == 0:
                            link(nc.vector.tensor_tensor(y[:], h[:, 0], h[:, 1], ALU.add))
                        else:
                            link(nc.vector.tensor_tensor(y[:], y[:], h[:, 0], ALU.add))
                            link(nc.vector.tensor_tensor(y[:], y[:], h[:, 1], ALU.add))

                    invert(0)
                    for p in range(PAIRS):
                        i = g * PAIRS + p
                        e, a = em[:, p % 2], decay[:, p % 2]
                        if p + 1 < PAIRS:
                            invert(p + 1)
                        dve.wait_ge(s["em_ready"], i + 1)
                        link(nc.vector.scalar_tensor_tensor(out=e, in0=a, scalar=1.0, in1=e,
                                                            op0=ALU.add, op1=ALU.mult))
                        dve.wait_ge(s["inverse_ready"], 4 + 2 * i + 2)
                        nc.vector.tensor_tensor(e, e, inv[:], ALU.mult).then_inc(s["ratio_ready"], 1)
                        nc.vector.memset(a.rearrange("p k c (b t) -> p (k c b) t", t=SEQ)[:, :, 0:1], 0.0)
                        dve.wait_ge(s["weighted_b"], 2 + 2 * i + 2)
                        dve.wait_ge(s["ratio_ready"], 1 + i + 1)
                        nc.vector.tensor_tensor(e, e, wb[:], ALU.mult).then_inc(s["input_ready"], 1)
                        if p:
                            add_outputs(p - 1)
                        dve.wait_ge(s["input_ready"], 1 + i + 1)
                        for k in range(2):
                            for c in range(KT):
                                last = nc.vector.tensor_tensor_scan(h[:, k, c], a[:, k, c], e[:, k, c], 0.0,
                                                                    ALU.mult, ALU.add)
                        last.then_inc(s["state_ready"], 1)
                    add_outputs(PAIRS - 1)
                    nc.vector.tensor_tensor(y[:], y[:], gate[:], ALU.mult).then_inc(s["y_ready"], 1)
                    dve.wait_ge(s["y_high"], g + 1)
                    nc.vector.tensor_tensor(act[1][:], y[:], act[0][:].bitcast(F32),
                                            ALU.subtract).then_inc(s["y_low"], 1)
                    dve.wait_ge(s["xn_added"], g + 1)
                    for j in range(GB // 2):
                        dve.wait_ge(s["out_ready"], (GB // 2) * g + j + 1)
                        xg = x[:, bass.ds(g * GB + 2 * j, 2), :]
                        last = nc.vector.tensor_tensor(xg, xg, ps_t[j][:].rearrange("p (t d) -> p t d", d=DM),
                                                       ALU.add)
                    link(last)
                    for t in range(GB):
                        nc.vector.bn_stats(core.stats[:, bass.ds(g * GB + t, 1), :].squeeze(1),
                                           x[:, bass.ds(g * GB + t, 1), :].squeeze(1))
                    chain.leave(GROUPS)
        core.retire(s)


def cross_attention(core, w, name, masked):
    nc, x, ident = core.nc, core.x, core.ident
    HEADS, HD = 16, DM // 16
    PAIR = 2 * HD
    ROWS = P // PAIR
    VW = HD + 1
    NEG = -1e9
    SLOTS = GB * ROWS

    with ExitStack() as ctx:
        def sb(n, shape, dt=F32):
            return ctx.enter_context(nc.sbuf_tensor(f"{name}_{n}", shape, dt))

        def ps(n):
            return ctx.enter_context(nc.psum_tensor(f"{name}_{n}", [P, GT], F32))

        raw = [sb(n, [P, KT, DM]) for n in ("w_q", "w_k", "w_v", "w_o")]
        split = [(sb(f"hi{i}", t.shape, F32R), sb(f"lo{i}", t.shape, F32R)) for i, t in enumerate(raw)]
        s_q, s_k, s_v, s_o = split
        b_q, b_k = sb("b_q", [P, KT]), sb("b_k", [P, KT])
        b_v, b_o = sb("b_v", [P, DM]), sb("b_o", [P, DM])
        side = sb("side", [P, 2])
        b_side = sb("b_side", [P, KT, 2])
        context = sb("context", [P, GB, DM])
        if masked:
            padded = sb("padded", [P, TILES, SEQ], U8)
            causal = sb("causal", [P, SEQ])
            mask = sb("mask", [P, TILES, SEQ])
            keep = sb("keep", [P, TILES, SEQ])

        xn = sb("xn", [P, GB, DM])
        xnt = (sb("xnt_hi", [P, KT, GT], F32R), sb("xnt_lo", [P, KT, GT], F32R))
        cnt = (sb("cnt_hi", [P, KT, GT], F32R), sb("cnt_lo", [P, KT, GT], F32R))
        q = [sb(f"q{o}", [P, KT, GT]) for o in range(2)]
        k_t = sb("k", [P, KT, GT])
        v = sb("v", [P, GB, HEADS, VW])
        shifted = sb("shifted", [P, ROWS, 4, SEQ])
        top = sb("top", [P, ROWS, 4])
        masked_s = sb("masked_s", [P, ROWS, 4, SEQ]) if masked else None
        probs_t = sb("probs_t", [P, 2, 4 * SEQ])
        inv_sum = sb("inv_sum", [P, HEADS])
        mixed = sb("mixed", [P, DM])
        mixed_t = (sb("mixed_hi", [P, KT, SEQ], F32R), sb("mixed_lo", [P, KT, SEQ], F32R))

        ps_s = [ps(f"s{i}") for i in range(ROWS)]
        ps_t = [ps(f"t{i}") for i in range(2)]
        ps_o, ps_p = ps("o"), ps("p")
        v_banks = (ps_o, ps_p)

        names = ("w_loaded w_high w_low side_set variance_ready scale_ready cn_loaded cn_turned cn_high "
                 "cn_low k_ready k_taken v_ready v_taken xn_ready bias_added xn_turned xn_high xn_low q_ready q_even q_odd "
                 "scores_ready scores_taken scores_masked shift_ready probs_ready probs_turned "
                 "probs_copied heads_ready mixed_ready mixed_turned mixed_high mixed_low out_ready x_updated "
                 "ones_set mask_ready chain")
        s = core.stage_sems(name + "_", names)
        LOADS = 9 + 2 * masked
        taken = s["scores_taken"] if masked else s["shift_ready"]

        with nc.Block() as block:
            @block.sync
            def _(sp):
                for t, n in zip(raw, ("Wq", "Wk", "Wv", "Wo")):
                    sp.dma_start(t[:], w[f"{name}_{n}"]).then_inc(s["w_loaded"], 16)
                sp.dma_start(b_q[:], w[f"{name}_bq"]).then_inc(s["w_loaded"], 16)
                sp.dma_start(b_k[:], w[f"{name}_bk"]).then_inc(s["w_loaded"], 16)
                sp.dma_start(b_v[:], w[f"{name}_bv"].partition_broadcast(P)).then_inc(s["w_loaded"], 16)
                sp.dma_start(b_o[:], w[f"{name}_bo"].partition_broadcast(P)).then_inc(s["w_loaded"], 16)
                sp.dma_start(side[:], w["side"]).then_inc(s["w_loaded"], 16)
                if masked:
                    sp.dma_start(padded[:], w["padding"].partition_broadcast(P)).then_inc(s["w_loaded"], 16)
                    sp.dma_start(causal[:], w["causal"]).then_inc(s["w_loaded"], 16)
                with sp.Fori(0, GROUPS) as g:
                    sp.wait_ge(s["cn_turned"], KT * g + KT)
                    sp.dma_start(context[:], w["context"][:, bass.ds(g * GB, GB), :]).then_inc(s["cn_loaded"], 16)

            @block.gpsimd
            def _(pool):
                nc.gpsimd.memset(v[:, :, :, HD:VW], 1.0).then_inc(s["ones_set"], 1)
                inverse_deviation(core, pool, s["variance_ready"], s["scale_ready"])
                pool.wait_ge(s["w_loaded"], 16 * LOADS)
                for i, (t, (hi, lo)) in enumerate(zip(raw, split)):
                    pool.wait_ge(s["w_high"], i + 1)
                    nc.gpsimd.tensor_tensor(lo[:], t[:], hi[:].bitcast(F32), ALU.subtract).then_inc(s["w_low"], 1)
                with pool.Fori(0, GROUPS) as g:
                    pool.wait_ge(s["xn_ready"], g + 1)
                    xg = x[:, bass.ds(g * GB, GB), :]
                    nc.gpsimd.tensor_tensor(xg, xg, b_o[:].unsqueeze(1).to_broadcast([P, GB, DM]),
                                            ALU.add).then_inc(s["bias_added"], 1)
                    if masked:
                        for u in range(SLOTS):
                            i, r = g * SLOTS + u, u % ROWS
                            pool.wait_ge(s["scores_masked"], i + 1)
                            pool.wait_ge(s["probs_turned"], i + 1)
                            nc.gpsimd.tensor_tensor(shifted[:, r], masked_s[:, r],
                                                    top[:, r].unsqueeze(2).to_broadcast([P, 4, SEQ]),
                                                    ALU.subtract).then_inc(s["shift_ready"], 1)

            @block.tensor
            def _(pe):
                pe.sem_inc(s["cn_turned"], KT)
                pe.sem_inc(s["probs_turned"], ROWS)
                pe.sem_inc(s["heads_ready"], 2)
                pe.sem_inc(s["mixed_turned"], 1)
                pe.sem_inc(s["out_ready"], 1)
                pe.wait_ge(s["ones_set"], 1)
                with pe.Fori(0, GROUPS) as g:
                    pe.wait_ge(taken, ROWS + SLOTS * g)
                    pe.wait_ge(s["cn_loaded"], 16 * g + 16)
                    for k in range(KT):
                        for t in range(GB):
                            last = nc.tensor.transpose(ps_s[k][:, t * P:(t + 1) * P], context[:, t, k * P:(k + 1) * P],
                                                       ident[:])
                        last.then_inc(s["cn_turned"], 1)
                    pe.wait_ge(s["xn_ready"], g + 1)
                    for k in range(KT):
                        for t in range(GB):
                            last = nc.tensor.transpose(ps_s[2 + k][:, t * P:(t + 1) * P], xn[:, t, k * P:(k + 1) * P],
                                                       ident[:])
                        last.then_inc(s["xn_turned"], 1)
                    pe.wait_ge(s["w_low"], len(raw))
                    pe.wait_ge(s["cn_low"], KT * g + KT)
                    pe.wait_ge(s["probs_copied"], 2 + SLOTS * g)
                    for m in range(KT):
                        for k in range(KT):
                            last = product(nc, ps_t[m][:], [a[:, k, m * P:(m + 1) * P] for a in s_k],
                                           [a[:, k, :] for a in cnt], k == 0, k == KT - 1)
                        last.then_inc(s["k_ready"], 1)
                    pe.wait_ge(s["xn_low"], KT * g + KT)
                    for m in range(KT):
                        for k in range(KT):
                            last = product(nc, ps_s[m][:], [a[:, k, m * P:(m + 1) * P] for a in s_q],
                                           [a[:, k, :] for a in xnt], k == 0, k == KT - 1)
                        last.then_inc(s["q_ready"], 1)
                    pe.wait_ge(s["mixed_ready"], 1 + GB * g)
                    pe.wait_ge(s["x_updated"], 1 + GB * g)
                    for t in range(GB):
                        for k in range(KT):
                            last = product(nc, v_banks[t // 2][:, (t % 2) * DM:(t % 2 + 1) * DM],
                                           [a[:, k, t * P:(t + 1) * P] for a in cnt],
                                           [a[:, k, :] for a in s_v], k == 0, k == KT - 1)
                        if t % 2:
                            last.then_inc(s["v_ready"], 1)
                    pe.wait_ge(s["k_taken"], KT * g + KT)
                    pe.wait_ge(s["q_even"], KT * g + KT)
                    pe.wait_ge(s["q_odd"], KT * g + KT)
                    pe.wait_ge(s["v_taken"], 2 * g + 2)
                    for u in range(SLOTS + 6):
                        if u < SLOTS:
                            b, r = divmod(u, ROWS)
                            pe.wait_ge(taken, g * SLOTS + u + 1)
                            part, cols = slice(r * PAIR, (r + 1) * PAIR), slice(b * SEQ, (b + 1) * SEQ)
                            for m in range(KT):
                                for o in range(2):
                                    at = (2 * m + o) * SEQ
                                    last = nc.tensor.matmul(ps_s[r][:, at:at + SEQ], q[o][part, m, cols],
                                                            k_t[part, m, cols], start=True, stop=True)
                            last.then_inc(s["scores_ready"], 1)
                        if 0 <= u - 2 < SLOTS:
                            i, r = g * SLOTS + u - 2, (u - 2) % ROWS
                            pe.wait_ge(s["probs_ready"], i + 1)
                            pe.wait_ge(s["probs_copied"], i + 1)
                            for j in range(4):
                                last = nc.tensor.transpose(ps_t[u % 2][:, j * SEQ:(j + 1) * SEQ],
                                                           shifted[:, r, j, :], ident[:])
                            last.then_inc(s["probs_turned"], 1)
                        if 0 <= u - 3 < SLOTS:
                            b, r = divmod(u - 3, ROWS)
                            pe.wait_ge(s["probs_copied"], 2 + g * SLOTS + u - 3 + 1)
                            if r == 0:
                                pe.wait_ge(s["mixed_ready"], g * GB + b + 1)
                            for j in range(4):
                                head = 8 * (j // 2) + 2 * r + j % 2
                                last = nc.tensor.matmul(ps_o[:, head * VW:(head + 1) * VW],
                                                        probs_t[:, (u - 3) % 2, j * SEQ:(j + 1) * SEQ],
                                                        v[:, b, head, :], start=True, stop=True)
                            last.then_inc(s["heads_ready"], 1)
                        b, late = divmod(u - 8, ROWS)
                        if late == 0 and 0 <= b < GB:
                            pe.wait_ge(s["mixed_ready"], 1 + g * GB + b + 1)
                            pe.wait_ge(s["x_updated"], g * GB + b + 1)
                            for k in range(KT):
                                last = nc.tensor.transpose(ps_p[:, k * P:(k + 1) * P], mixed[:, k * P:(k + 1) * P],
                                                           ident[:])
                            last.then_inc(s["mixed_turned"], 1)
                        b, late = divmod(u - 9, ROWS)
                        if late == 0 and 0 <= b < GB:
                            pe.wait_ge(s["mixed_low"], g * GB + b + 1)
                            for k in range(KT):
                                last = product(nc, ps_p[:, DM:2 * DM], [a[:, k, :] for a in mixed_t],
                                               [a[:, k, :] for a in s_o], k == 0, k == KT - 1)
                            last.then_inc(s["out_ready"], 1)

            @block.scalar
            def _(ac):
                ac.wait_ge(s["w_loaded"], 16 * LOADS)
                for i, (t, (hi, lo)) in enumerate(zip(raw, split)):
                    nc.scalar.activation(hi[:], t[:], ACT.Copy).then_inc(s["w_high"], 1)
                ac.sem_inc(s["probs_copied"], 2)
                nc.scalar.preload_act_table(ACT.Exp)
                ac.wait_ge(s["side_set"], 1)
                with ac.Fori(0, GROUPS) as g:
                    for k in range(KT):
                        ac.wait_ge(s["cn_turned"], KT + KT * g + k + 1)
                        nc.scalar.activation(cnt[0][:, k, :], ps_s[k][:], ACT.Copy).then_inc(s["cn_high"], 1)
                    for k in range(KT):
                        ac.wait_ge(s["xn_turned"], KT * g + k + 1)
                        nc.scalar.activation(xnt[0][:, k, :], ps_s[2 + k][:], ACT.Copy).then_inc(s["xn_high"], 1)
                    if not masked:
                        for m in range(KT):
                            ac.wait_ge(s["k_ready"], KT * g + m + 1)
                            nc.scalar.activation(k_t[:, m, :], ps_t[m][:], ACT.Identity,
                                                 bias=b_k[:, m:m + 1]).then_inc(s["k_taken"], 1)
                    for m in range(KT):
                        ac.wait_ge(s["q_ready"], KT * g + m + 1)
                        nc.scalar.activation(q[0][:, m, :], ps_s[m][:], ACT.Identity, bias=b_side[:, m, 0:1],
                                             scale=side[:, 0:1]).then_inc(s["q_even"], 1)
                    for u in range(SLOTS + 6):
                        if u < SLOTS:
                            i, r = g * SLOTS + u, u % ROWS
                            ac.wait_ge(s["shift_ready"], ROWS + i + 1)
                            nc.scalar.activation(shifted[:, r], shifted[:, r], ACT.Exp).then_inc(s["probs_ready"], 1)
                        if 0 <= u - 2 < SLOTS:
                            i = g * SLOTS + u - 2
                            ac.wait_ge(s["probs_turned"], ROWS + i + 1)
                            ac.wait_ge(s["heads_ready"], i + 1)
                            nc.scalar.activation(probs_t[:, u % 2, :], ps_t[u % 2][:],
                                                 ACT.Copy).then_inc(s["probs_copied"], 1)
                        b, late = divmod(u - 8, ROWS)
                        if late == 0 and 0 <= b < GB:
                            ac.wait_ge(s["mixed_turned"], 1 + g * GB + b + 1)
                            ac.wait_ge(s["out_ready"], g * GB + b + 1)
                            nc.scalar.activation(mixed_t[0][:], ps_p[:, 0:DM].rearrange("p (k t) -> p k t", k=KT),
                                                 ACT.Copy).then_inc(s["mixed_high"], 1)

            @block.vector
            def _(dve):
                chain = Chain(dve, s["chain"])
                link = chain.link
                variance(core, dve, chain, s["variance_ready"])
                if masked:
                    dve.sem_inc(s["scores_taken"], ROWS)
                dve.sem_inc(s["shift_ready"], ROWS)
                dve.sem_inc(s["mixed_ready"], 1)
                dve.sem_inc(s["x_updated"], 1)
                dve.wait_ge(s["w_loaded"], 16 * LOADS)
                for o in range(2):
                    last = nc.vector.tensor_scalar(b_side[:, :, o], b_q[:], side[:, o:o + 1], None, ALU.mult)
                last.then_inc(s["side_set"], 1)
                if masked:
                    nc.vector.tensor_scalar(keep[:], padded[:], -1.0, 1.0, ALU.mult, ALU.add)
                    nc.vector.tensor_scalar(mask[:], padded[:], NEG, None, ALU.mult).then_inc(s["mask_ready"], 1)
                    dve.wait_ge(s["mask_ready"], 1)
                    nc.vector.tensor_tensor(mask[:], mask[:], causal[:].unsqueeze(1).to_broadcast([P, TILES, SEQ]),
                                            ALU.add).then_inc(s["mask_ready"], 1)
                    dve.wait_ge(s["mask_ready"], 2)
                dve.wait_ge(s["ones_set"], 1)
                dve.wait_ge(s["scale_ready"], 1)
                with dve.Fori(0, GROUPS) as g:
                    LINKS = GB + (0 if masked else SLOTS)
                    chain.enter(g, LINKS)
                    for t in range(GB):
                        last = nc.vector.tensor_scalar(xn[:, t, :], x[:, bass.ds(g * GB + t, 1), :].squeeze(1),
                                                       core.ln[:, 0, bass.ds(g * GB + t, 1)],
                                                       core.ln[:, 3, bass.ds(g * GB + t, 1)],
                                                       ALU.subtract, ALU.mult)
                    last.then_inc(s["xn_ready"], 1)
                    for k in range(KT):
                        dve.wait_ge(s["cn_high"], KT * g + k + 1)
                        nc.vector.tensor_tensor(cnt[1][:, k, :], ps_s[k][:], cnt[0][:, k, :].bitcast(F32),
                                                ALU.subtract).then_inc(s["cn_low"], 1)
                    for k in range(KT):
                        dve.wait_ge(s["xn_high"], KT * g + k + 1)
                        nc.vector.tensor_tensor(xnt[1][:, k, :], ps_s[2 + k][:], xnt[0][:, k, :].bitcast(F32),
                                                ALU.subtract).then_inc(s["xn_low"], 1)
                    if masked:
                        for m in range(KT):
                            dve.wait_ge(s["k_ready"], KT * g + m + 1)
                            kept = keep[:, bass.ds(g * GB, GB), :].rearrange("p b t -> p (b t)")
                            nc.vector.scalar_tensor_tensor(out=k_t[:, m, :], in0=ps_t[m][:], scalar=b_k[:, m:m + 1],
                                                           in1=kept, op0=ALU.add,
                                                           op1=ALU.mult).then_inc(s["k_taken"], 1)
                    for m in range(KT):
                        dve.wait_ge(s["q_even"], KT * g + m + 1)
                        nc.vector.tensor_scalar(q[1][:, m, :], ps_s[m][:], side[:, 1:2], b_side[:, m, 1:2],
                                                ALU.mult, ALU.add).then_inc(s["q_odd"], 1)
                    for j in range(2):
                        dve.wait_ge(s["v_ready"], 2 * g + j + 1)
                        for t in (2 * j, 2 * j + 1):
                            last = nc.vector.tensor_tensor(
                                v[:, t, :, 0:HD],
                                v_banks[j][:, (t % 2) * DM:(t % 2 + 1) * DM].rearrange("p (h d) -> p h d", d=HD),
                                b_v[:].rearrange("p (h d) -> p h d", d=HD), ALU.add)
                        last.then_inc(s["v_taken"], 1)
                    for u in range(SLOTS + 8):
                        b, late = divmod(u - 7, ROWS)
                        if late == 0 and 0 <= b < GB:
                            dve.wait_ge(s["heads_ready"], 2 + g * SLOTS + ROWS * (b + 1))
                            dve.wait_ge(s["mixed_turned"], g * GB + b + 1)
                            heads = ps_o[:, 0:HEADS * VW].rearrange("p (h d) -> p h d", d=VW)
                            link(nc.vector.reciprocal(inv_sum[:], heads[:, :, HD]))
                            nc.vector.tensor_tensor(mixed[:].rearrange("p (h d) -> p h d", d=HD), heads[:, :, 0:HD],
                                                    inv_sum[:].unsqueeze(2).to_broadcast([P, HEADS, HD]),
                                                    ALU.mult).then_inc(s["mixed_ready"], 1)
                        if u < SLOTS:
                            b, r = divmod(u, ROWS)
                            i = g * SLOTS + u
                            scores = ps_s[r][:].rearrange("p (j t) -> p j t", t=SEQ)
                            peak = top[:, r].unsqueeze(2).to_broadcast([P, 4, SEQ])
                            dve.wait_ge(s["scores_ready"], i + 1)
                            if masked:
                                dve.wait_ge(s["shift_ready"], i + 1)
                                mask_b = mask[:, bass.ds(g * GB + b, 1), :].to_broadcast([P, 4, SEQ])
                                nc.vector.tensor_tensor(masked_s[:, r], scores, mask_b,
                                                        ALU.add).then_inc(s["scores_taken"], 1)
                                dve.wait_ge(s["scores_taken"], ROWS + i + 1)
                                nc.vector.tensor_reduce(top[:, r], masked_s[:, r], AX.X,
                                                        ALU.max).then_inc(s["scores_masked"], 1)
                            else:
                                link(nc.vector.tensor_reduce(top[:, r], scores, AX.X, ALU.max))
                                dve.wait_ge(s["probs_turned"], i + 1)
                                nc.vector.tensor_tensor(shifted[:, r], scores, peak,
                                                        ALU.subtract).then_inc(s["shift_ready"], 1)
                        b, late = divmod(u - 9, ROWS)
                        if late == 0 and 0 <= b < GB:
                            dve.wait_ge(s["mixed_high"], g * GB + b + 1)
                            nc.vector.tensor_tensor(mixed_t[1][:], ps_p[:, 0:DM].rearrange("p (k t) -> p k t", k=KT),
                                                    mixed_t[0][:].bitcast(F32), ALU.subtract).then_inc(s["mixed_low"], 1)
                        b, late = divmod(u - 11, ROWS)
                        if late == 0 and 0 <= b < GB:
                            xb = x[:, bass.ds(g * GB + b, 1), :].squeeze(1)
                            dve.wait_ge(s["out_ready"], 1 + g * GB + b + 1)
                            if b == 0:
                                dve.wait_ge(s["bias_added"], g + 1)
                            nc.vector.tensor_tensor(xb, xb, ps_p[:, DM:2 * DM], ALU.add).then_inc(s["x_updated"], 1)
                            dve.wait_ge(s["x_updated"], 1 + g * GB + b + 1)
                            nc.vector.bn_stats(core.stats[:, bass.ds(g * GB + b, 1), :].squeeze(1), xb)
                    chain.leave(GROUPS)
        core.retire(s)


def experts(core, w, name, shared, routed, softmax_first, final):
    nc, x, ident = core.nc, core.x, core.ident
    E, PAIRS = shared + routed, (shared + routed) // 2
    FF = w[f"{name}_W1"].shape[3]
    FT = FF // P
    STEPS = 2 * GROUPS * FT
    UP, HID, RING = 3, 3, 4
    LAG = 3
    TOP = 2

    with ExitStack() as ctx:
        def sb(n, shape, dt=F32):
            return ctx.enter_context(nc.sbuf_tensor(f"{name}_{n}", shape, dt))

        def ps(n):
            return ctx.enter_context(nc.psum_tensor(f"{name}_{n}", [P, GT], F32))

        w_r, w_r_hi, w_r_lo = (sb(f"w_r{i}", [P, KT, routed], F32R if i else F32) for i in range(3))
        b_r, b_1, b_2 = sb("b_r", [P, routed]), sb("b_1", [P, E, FT]), sb("b_2", [E, DM])
        before = sb("before", [P, routed, routed])
        raw = sb("raw_1", [P, KT, FF]), sb("raw_2", [P, FT, DM])
        w_1 = [(sb(f"w1_hi{j}", [P, KT, FF], F32R), sb(f"w1_lo{j}", [P, KT, FF], F32R)) for j in range(2)]
        w_2 = [(sb(f"w2_hi{j}", [P, FT, DM], F32R), sb(f"w2_lo{j}", [P, FT, DM], F32R)) for j in range(2)]
        zero = sb("zero", [P, 1, 1])
        b_now = sb("b_now", [P, 2, FT])
        xnt = (sb("xnt_hi", [P, KT, TILES * SEQ], F32R), sb("xnt_lo", [P, KT, TILES * SEQ], F32R))
        xn = sb("xn", [P, 1 if final else 2, GB, DM])
        y = sb("y", [P, TILES, DM]) if final else x
        hid = sb("hid", [P, HID, GT])
        hid_hi, hid_lo = sb("hid_hi", [P, RING, GT], F32R), sb("hid_lo", [P, RING, GT], F32R)
        gates = sb("gates", [P, TILES, E])
        gates_t = sb("gates_t", [E, TILES * SEQ])
        score, excess = sb("score", [P, TILES, routed]), sb("excess", [P, TILES, routed])
        rank, best = sb("rank", [P, TILES, routed]), sb("best", [P, TILES])
        above, equal = (sb(n, [P, TILES, routed, routed]) for n in ("above", "equal"))
        if final:
            gamma, beta = sb("gamma", [P, DM]), sb("beta", [P, DM])

        ps_u = [ps(f"u{i}") for i in range(UP)]
        ps_a = [[ps(f"a{i}{j}") for j in range(2)] for i in range(2)]
        ps_r = ps("r")

        names = ("small_loaded w_loaded w_high w_split router_ready variance_ready scale_ready xn_ready xn_turned xn_high "
                 "xn_low logits_ready excess_ready exp_ready gates_ready gates_turned gates_copied bias_ready "
                 "bias_taken up_ready hid_ready hid_high hid_low down_done acc_taken variance2_ready scale2_ready "
                 "bias_copied y_set chain")
        s = core.stage_sems(name + "_", names)
        SMALL = 5 + 2 * final

        def group_of(step):
            return step // (GROUPS * FT), step // FT % GROUPS, step % FT

        with nc.Block() as block:
            @block.sync
            def _(sp):
                for t, n in ((w_r, "Wr"), (b_1, "b1"), (b_2, "b2"), (before, "before")):
                    sp.dma_start(t[:], w[f"{name}_{n}"]).then_inc(s["small_loaded"], 16)
                for t, n in ((b_r, "br"),) + (((gamma, "gamma"), (beta, "beta")) if final else ()):
                    sp.dma_start(t[:], w[f"{name}_{n}"].partition_broadcast(P)).then_inc(s["small_loaded"], 16)
                with sp.Fori(0, E) as e:
                    sp.wait_ge(s["w_split"], 2 * e + 2)
                    for t, n in zip(raw, ("W1", "W2")):
                        sp.dma_start(t[:], w[f"{name}_{n}"][bass.ds(e, 1)].squeeze(0)).then_inc(s["w_loaded"], 16)

            @block.gpsimd
            def _(pool):
                pool.sem_inc(s["w_split"], 2)
                pool.wait_ge(s["small_loaded"], 16 * SMALL)
                nc.gpsimd.memset(zero[:], 0.0)
                nc.gpsimd.tensor_copy(w_r_hi[:], w_r[:]).then_inc(s["router_ready"], 1)
                pool.wait_ge(s["router_ready"], 1)
                nc.gpsimd.tensor_tensor(w_r_lo[:], w_r[:], w_r_hi[:].bitcast(F32),
                                        ALU.subtract).then_inc(s["router_ready"], 1)
                if shared:
                    nc.gpsimd.memset(gates[:, :, 0:shared], 1.0 / shared).then_inc(s["router_ready"], 1)
                inverse_deviation(core, pool, s["variance_ready"], s["scale_ready"])
                with pool.Fori(0, PAIRS) as e2:
                    for j in range(2):
                        e = 2 * e2 + j
                        pool.wait_ge(s["w_loaded"], 32 * e + 32)
                        pool.wait_ge(s["down_done"], RING + GROUPS * FT * e)
                        for i, (t, (hi, lo)) in enumerate(zip(raw, (w_1[j], w_2[j]))):
                            nc.gpsimd.tensor_tensor(hi[:], t[:], zero[:].to_broadcast(t.shape),
                                                    ALU.add).then_inc(s["w_high"], 1)
                            pool.wait_ge(s["w_high"], 2 * e + i + 1)
                            nc.gpsimd.tensor_tensor(lo[:], t[:], hi[:].bitcast(F32),
                                                    ALU.subtract).then_inc(s["w_split"], 1)
                if final:
                    inverse_deviation(core, pool, s["variance2_ready"], s["scale2_ready"])

            @block.tensor
            def _(pe):
                pe.sem_inc(s["down_done"], RING + GROUPS * FT)
                pe.wait_ge(s["router_ready"], 2 + bool(shared))
                for g in range(GROUPS):
                    pe.wait_ge(s["xn_ready"], g + 1)
                    if g:
                        pe.wait_ge(s["xn_low"], KT * g)
                    for k in range(KT):
                        for t in range(GB):
                            last = nc.tensor.transpose(ps_u[k][:, t * P:(t + 1) * P],
                                                       xn[:, g % xn.shape[1], t, k * P:(k + 1) * P], ident[:])
                        last.then_inc(s["xn_turned"], 1)
                    pe.wait_ge(s["xn_low"], KT * g + KT)
                    for t in range(GB * g, GB * g + GB):
                        for k in range(KT):
                            last = product(nc, ps_r[:, t * routed:(t + 1) * routed],
                                           [a[:, k, t * P:(t + 1) * P] for a in xnt],
                                           [a[:, k, :] for a in (w_r_hi, w_r_lo)], k == 0, k == KT - 1)
                last.then_inc(s["logits_ready"], 1)
                pe.wait_ge(s["gates_ready"], 1)
                for g in range(GROUPS):
                    for t in range(GB):
                        last = nc.tensor.transpose(ps_a[g // 2][g % 2][0:E, t * P:(t + 1) * P],
                                                   gates[:, GB * g + t, :], ident[:])
                    last.then_inc(s["gates_turned"], 1)
                for i in range(TILES // 2):
                    pe.wait_ge(s["gates_copied"], i // 2 + 1 if i % 2 == 0 else GROUPS)
                    if i == 0:
                        pe.wait_ge(s["gates_copied"], GROUPS)
                    if i >= 4:
                        pe.wait_ge(s["bias_taken"], i - 3)
                    bank = ps_a[i // 2 % 2][i % 2]
                    for t in range(2):
                        last = nc.tensor.matmul(bank[:, t * DM:(t + 1) * DM],
                                                gates_t[:, (2 * i + t) * P:(2 * i + t + 1) * P], b_2[:],
                                                start=True, stop=True)
                    last.then_inc(s["bias_ready"], 1)
                pe.wait_ge(s["bias_taken"], TILES // 2)
                with pe.Fori(0, PAIRS) as e2:
                    for n in range(STEPS + LAG):
                        if n < STEPS:
                            j, g, f = group_of(n)
                            if n % (GROUPS * FT) == 0:
                                pe.wait_ge(s["w_split"], 2 + 4 * e2 + 2 * j + 2)
                            pe.wait_ge(s["hid_ready"], e2 * STEPS + n + 1)
                            for k in range(KT):
                                last = product(nc, ps_u[n % UP][:], [a[:, k, f * P:(f + 1) * P] for a in w_1[j]],
                                               [a[:, k, g * GT:(g + 1) * GT] for a in xnt], k == 0, k == KT - 1)
                            last.then_inc(s["up_ready"], 1)
                        d = n - LAG
                        if d >= 0:
                            j, g, f = group_of(d)
                            pe.wait_ge(s["hid_low"], HID + e2 * STEPS + d + 1)
                            if f == 0:
                                pe.wait_ge(s["acc_taken"], e2 * STEPS // FT + d // FT + 1)
                            for t in range(GB):
                                out = ps_a[d // FT % 2][t // 2][:, (t % 2) * DM:(t % 2 + 1) * DM]
                                last = product(nc, out, [a[:, d % RING, t * P:(t + 1) * P] for a in (hid_hi, hid_lo)],
                                               [a[:, f, :] for a in w_2[j]], f == 0 and t % 2 == 0, f == FT - 1,
                                               skip=True)
                            last.then_inc(s["down_done"], 1)

            @block.scalar
            def _(ac):
                for g in range(GROUPS):
                    for k in range(KT):
                        ac.wait_ge(s["xn_turned"], KT * g + k + 1)
                        nc.scalar.activation(xnt[0][:, k, g * GT:(g + 1) * GT], ps_u[k][:],
                                             ACT.Copy).then_inc(s["xn_high"], 1)
                ac.wait_ge(s["excess_ready"], 1)
                nc.scalar.activation(excess[:], excess[:], ACT.Exp).then_inc(s["exp_ready"], 1)
                for g in range(GROUPS):
                    ac.wait_ge(s["gates_turned"], g + 1)
                    nc.scalar.activation(gates_t[:, g * GT:(g + 1) * GT], ps_a[g // 2][g % 2][0:E, :],
                                         ACT.Copy).then_inc(s["gates_copied"], 1)
                ac.sem_inc(s["hid_ready"], UP)
                ac.sem_inc(s["hid_high"], HID)
                nc.scalar.preload_act_table(ACT.Relu)
                with ac.Fori(0, PAIRS) as e2:
                    nc.scalar.activation(b_now[:], b_1[:, bass.ds(2 * e2, 2), :], ACT.Copy).then_inc(s["bias_copied"], 1)
                    ac.wait_ge(s["bias_copied"], e2 + 1)
                    for n in range(STEPS + 1):
                        i = e2 * STEPS + n
                        if n < STEPS:
                            j, g, f = group_of(n)
                            ac.wait_ge(s["up_ready"], i + 1)
                            ac.wait_ge(s["hid_low"], i + 1)
                            nc.scalar.activation(hid[:, n % HID, :], ps_u[n % UP][:], ACT.Relu,
                                                 bias=b_now[:, j, f:f + 1]).then_inc(s["hid_ready"], 1)
                        if n:
                            m = n - 1
                            ac.wait_ge(s["hid_ready"], UP + i)
                            ac.wait_ge(s["down_done"], GROUPS * FT + i)
                            nc.scalar.activation(hid_hi[:, m % RING, :], hid[:, m % HID, :],
                                                 ACT.Copy).then_inc(s["hid_high"], 1)

            @block.vector
            def _(dve):
                chain = Chain(dve, s["chain"])
                link = chain.link
                variance(core, dve, chain, s["variance_ready"])
                dve.wait_ge(s["scale_ready"], 1)
                for g in range(GROUPS):
                    if final and g:
                        dve.wait_ge(s["xn_turned"], KT * g)
                        dve.wait_ge(s["y_set"], g)
                    elif g >= 2:
                        dve.wait_ge(s["xn_turned"], KT * (g - 1))
                    for t in range(GB):
                        last = normalise(core, xn[:, g % xn.shape[1], t, :], GB * g + t)
                    last.then_inc(s["xn_ready"], 1)
                    if final:
                        dve.wait_ge(s["xn_ready"], g + 1)
                        nc.vector.tensor_copy(y[:, GB * g:GB * g + GB, :], xn[:, 0]).then_inc(s["y_set"], 1)
                    for k in range(KT):
                        dve.wait_ge(s["xn_high"], KT * g + k + 1)
                        cols = slice(g * GT, (g + 1) * GT)
                        nc.vector.tensor_tensor(xnt[1][:, k, cols], ps_u[k][:], xnt[0][:, k, cols].bitcast(F32),
                                                ALU.subtract).then_inc(s["xn_low"], 1)
                dve.wait_ge(s["small_loaded"], 16 * SMALL)
                dve.wait_ge(s["logits_ready"], 1)
                wide = [P, TILES, routed]
                link(nc.vector.tensor_tensor(score[:], ps_r[:, 0:TILES * routed].rearrange("p (t e) -> p t e", e=routed),
                                             b_r[:].unsqueeze(1).to_broadcast(wide), ALU.add))
                link(nc.vector.tensor_reduce(best[:], score[:], AX.X, ALU.max))
                nc.vector.tensor_tensor(excess[:], score[:], best[:].unsqueeze(2).to_broadcast(wide),
                                        ALU.subtract).then_inc(s["excess_ready"], 1)
                dve.wait_ge(s["exp_ready"], 1)
                g_out = gates[:, :, shared:E]

                def over_sum(out, value):
                    link(nc.vector.tensor_reduce(best[:], value, AX.X, ALU.add))
                    link(nc.vector.reciprocal(best[:], best[:]))
                    link(nc.vector.tensor_tensor(out, value, best[:].unsqueeze(2).to_broadcast(wide), ALU.mult))

                if softmax_first:
                    over_sum(score[:], excess[:])
                square = [P, TILES, routed, routed]
                other = score[:].unsqueeze(2).to_broadcast(square)
                own = score[:].unsqueeze(3).to_broadcast(square)
                nc.vector.tensor_tensor(above[:], other, own, ALU.is_gt)
                link(nc.vector.tensor_tensor(equal[:], other, own, ALU.is_equal))
                link(nc.vector.tensor_tensor(equal[:], equal[:], before[:].unsqueeze(1).to_broadcast(square), ALU.mult))
                link(nc.vector.tensor_tensor(above[:], above[:], equal[:], ALU.add))
                link(nc.vector.tensor_reduce(rank[:], above[:], AX.X, ALU.add))
                link(nc.vector.tensor_scalar(rank[:], rank[:], float(TOP), None, ALU.is_lt))
                if softmax_first:
                    nc.vector.tensor_tensor(g_out, rank[:], score[:], ALU.mult).then_inc(s["gates_ready"], 1)
                else:
                    link(nc.vector.tensor_tensor(excess[:], rank[:], excess[:], ALU.mult))
                    over_sum(g_out, excess[:])
                    dve.sem_inc(s["gates_ready"], 1)
                for i in range(TILES // 2):
                    dve.wait_ge(s["bias_ready"], i + 1)
                    at = y[:, 2 * i:2 * i + 2, :]
                    nc.vector.tensor_tensor(at, at, ps_a[i // 2 % 2][i % 2][:].rearrange("p (t d) -> p t d", d=DM),
                                            ALU.add).then_inc(s["bias_taken"], 1)
                dve.sem_inc(s["hid_low"], HID)
                dve.sem_inc(s["acc_taken"], 2)
                dve.wait_ge(s["bias_taken"], TILES // 2)
                ACC_AT = FT - 1 + LAG + 1
                with dve.Fori(0, PAIRS) as e2:
                    for n in range(STEPS - FT + ACC_AT + 1):
                        if n < STEPS:
                            dve.wait_ge(s["hid_high"], HID + e2 * STEPS + n + 1)
                            nc.vector.tensor_tensor(hid_lo[:, n % RING, :], hid[:, n % HID, :],
                                                    hid_hi[:, n % RING, :].bitcast(F32),
                                                    ALU.subtract).then_inc(s["hid_low"], 1)
                        if n >= ACC_AT and (n - ACC_AT) % FT == 0:
                            r = (n - ACC_AT) // FT
                            q = e2 * (STEPS // FT) + r
                            j, g, _ = group_of(r * FT)
                            dve.wait_ge(s["down_done"], RING + GROUPS * FT + FT * q + FT)
                            dve.wait_ge(s["acc_taken"], 2 + q)
                            for t in range(GB):
                                yt = y[:, g * GB + t, :]
                                last = nc.vector.scalar_tensor_tensor(
                                    out=yt, in0=ps_a[r % 2][t // 2][:, (t % 2) * DM:(t % 2 + 1) * DM],
                                    scalar=gates[:, g * GB + t, bass.ds(2 * e2 + j, 1)], in1=yt,
                                    op0=ALU.mult, op1=ALU.add)
                            last.then_inc(s["acc_taken"], 1)
                dve.wait_ge(s["acc_taken"], 2 + PAIRS * STEPS // FT)
                for t in range(TILES):
                    last = nc.vector.bn_stats(core.stats[:, t, :], y[:, t, :])
                if final:
                    link(last)
                    variance(core, dve, chain, s["variance2_ready"])
                    dve.wait_ge(s["scale2_ready"], 1)
                    for t in range(TILES):
                        last = nc.vector.tensor_scalar(y[:, t, :], y[:, t, :], core.ln[:, 0, t:t + 1],
                                                       core.ln[:, 3, t:t + 1], ALU.subtract, ALU.mult)
                    link(last)
                    full = [P, TILES, DM]
                    link(nc.vector.tensor_tensor(y[:], y[:], gamma[:].unsqueeze(1).to_broadcast(full), ALU.mult))
                    link(nc.vector.tensor_tensor(y[:], y[:], beta[:].unsqueeze(1).to_broadcast(full), ALU.add))
                    nc.vector.tensor_tensor(x[:], x[:], y[:], ALU.add)
        core.retire(s)


def self_attention(core, w):
    nc, x, ident = core.nc, core.x, core.ident
    HEADS, HD = 8, 64
    INNER = HEADS * HD
    SIDES = P // HD
    JT = INNER // P
    VW = HD + 1
    SCALE = 16.0
    LEAST_NORM, LEAST_SUM = 1e-12, 1e-6

    with ExitStack() as ctx:
        def sb(n, shape, dt=F32):
            return ctx.enter_context(nc.sbuf_tensor(f"a_{n}", shape, dt))

        def ps(n):
            return ctx.enter_context(nc.psum_tensor(f"a_{n}", [P, GT], F32))

        raw = [sb("w_q", [P, KT, INNER]), sb("w_kv", [P, KT, 2 * INNER]), sb("w_o", [P, JT, DM])]
        split = [(sb(f"hi{i}", t.shape, F32R), sb(f"lo{i}", t.shape, F32R)) for i, t in enumerate(raw)]
        s_q, s_kv, s_o = split
        half = sb("half", [P, GB * 2 * HEADS])
        less_scale = sb("less_scale", [P, 1])
        xn = sb("xn", [P, GB, DM])
        xnt = (sb("xnt_hi", [P, KT, GT], F32R), sb("xnt_lo", [P, KT, GT], F32R))
        qk = sb("qk", [P, GB, 2, INNER])
        squares = sb("squares", [P, 2, 2, INNER])
        norm = sb("norm", [P, GB, 2 * HEADS])
        v = sb("v", [P, GB, HEADS, VW])
        q_t, k_t = sb("q_t", [P, JT, SEQ]), sb("k_t", [P, JT, SEQ])
        probs = sb("probs", [P, SIDES, JT * SEQ])
        inv_sum = sb("inv_sum", [P, SIDES, JT])
        mixed = sb("mixed", [P, INNER])
        mixed_t = (sb("mixed_hi", [P, JT, SEQ], F32R), sb("mixed_lo", [P, JT, SEQ], F32R))

        ps_a, ps_t, ps_s, ps_o = ([ps(f"{n}{i}") for i in range(2)] for n in "atso")

        names = ("w_loaded w_high w_low consts_set variance_ready scale_ready xn_ready xn_turned xn_high xn_low "
                 "q_ready k_ready v_ready q_copied k_copied v_copied squares_ready squares_summed norm_ready unit_ready "
                 "q_turned k_turned qt_ready kt_ready scores_ready probs_ready heads_ready mixed_ready mixed_turned "
                 "mixed_high mixed_low out_ready x_updated chain")
        s = core.stage_sems("a_", names)

        with nc.Block() as block:
            @block.sync
            def _(sp):
                for t, n in zip(raw, ("Wq", "Wkv", "Wo")):
                    sp.dma_start(t[:], w[f"a_{n}"]).then_inc(s["w_loaded"], 16)

            @block.gpsimd
            def _(pool):
                nc.gpsimd.memset(v[:, :, :, HD:VW], 1.0)
                nc.gpsimd.memset(less_scale[:], -SCALE)
                nc.gpsimd.memset(half[:], 0.5).then_inc(s["consts_set"], 1)
                inverse_deviation(core, pool, s["variance_ready"], s["scale_ready"])
                pool.wait_ge(s["w_loaded"], 16 * len(raw))
                for i, (t, (hi, lo)) in enumerate(zip(raw, split)):
                    pool.wait_ge(s["w_high"], i + 1)
                    nc.gpsimd.tensor_tensor(lo[:], t[:], hi[:].bitcast(F32), ALU.subtract).then_inc(s["w_low"], 1)
                pool.wait_ge(s["consts_set"], 1)
                with pool.Fori(0, GROUPS) as g:
                    for b in range(GB):
                        j = g * GB + b
                        pool.wait_ge(s["q_copied"], j + 1)
                        pool.wait_ge(s["k_copied"], j + 1)
                        pool.wait_ge(s["squares_summed"], j + 1)
                        nc.gpsimd.tensor_tensor(squares[:, b % 2], qk[:, b], qk[:, b],
                                                ALU.mult).then_inc(s["squares_ready"], 1)
                    pool.wait_ge(s["squares_summed"], 2 + g * GB + GB)
                    n = norm[:].rearrange("p b h -> p (b h)")
                    nc.gpsimd.tensor_tensor(n, n, half[:], ALU.pow).then_inc(s["norm_ready"], 1)

            @block.tensor
            def _(pe):
                pe.wait_ge(s["w_low"], len(raw))
                pe.wait_ge(s["consts_set"], 1)
                with pe.Fori(0, GROUPS) as g:
                    pe.wait_ge(s["xn_ready"], g + 1)
                    for k in range(KT):
                        for t in range(GB):
                            last = nc.tensor.transpose(ps_a[k][:, t * P:(t + 1) * P], xn[:, t, k * P:(k + 1) * P],
                                                       ident[:])
                        last.then_inc(s["xn_turned"], 1)
                    pe.wait_ge(s["xn_low"], KT * g + KT)
                    for b in range(GB):
                        lhs = [[a[:, k, b * SEQ:(b + 1) * SEQ] for a in xnt] for k in range(KT)]
                        if b:
                            pe.wait_ge(s["q_copied"], g * GB + b)
                        for k in range(KT):
                            last = product(nc, ps_a[0][:], lhs[k], [a[:, k, :] for a in s_q], k == 0, k == KT - 1)
                        last.then_inc(s["q_ready"], 1)
                        if b:
                            pe.wait_ge(s["k_copied"], g * GB + b)
                        for k in range(KT):
                            last = product(nc, ps_a[1][:], lhs[k], [a[:, k, 0:INNER] for a in s_kv],
                                           k == 0, k == KT - 1)
                        last.then_inc(s["k_ready"], 1)
                        if b >= 2:
                            pe.wait_ge(s["v_copied"], g * GB + b - 1)
                        for k in range(KT):
                            last = product(nc, ps_t[b % 2][:], lhs[k], [a[:, k, INNER:] for a in s_kv],
                                           k == 0, k == KT - 1)
                        last.then_inc(s["v_ready"], 1)
                    pe.wait_ge(s["k_copied"], g * GB + GB)
                    pe.wait_ge(s["v_copied"], g * GB + GB)
                    for u in range(GB + 1):
                        j = g * GB + u
                        if u < GB:
                            pe.wait_ge(s["unit_ready"], j + 1)
                            for c in range(JT):
                                last = nc.tensor.transpose(ps_t[0][:, c * SEQ:(c + 1) * SEQ],
                                                           qk[:, u, 0, c * P:(c + 1) * P], ident[:])
                            last.then_inc(s["q_turned"], 1)
                            for c in range(JT):
                                last = nc.tensor.transpose(ps_t[1][:, c * SEQ:(c + 1) * SEQ],
                                                           qk[:, u, 1, c * P:(c + 1) * P], ident[:])
                            last.then_inc(s["k_turned"], 1)
                        if u:
                            pe.wait_ge(s["mixed_ready"], j)
                            for c in range(JT):
                                last = nc.tensor.transpose(ps_a[0][:, c * SEQ:(c + 1) * SEQ],
                                                           mixed[:, c * P:(c + 1) * P], ident[:])
                            last.then_inc(s["mixed_turned"], 1)
                        if u < GB:
                            pe.wait_ge(s["qt_ready"], j + 1)
                            pe.wait_ge(s["kt_ready"], j + 1)
                            for o in range(SIDES):
                                part = slice(o * HD, (o + 1) * HD)
                                for c in range(JT):
                                    last = nc.tensor.matmul(ps_s[o][:, c * SEQ:(c + 1) * SEQ], k_t[part, c, :],
                                                            q_t[part, c, :], start=True, stop=True)
                                last.then_inc(s["scores_ready"], 1)
                        if u:
                            pe.wait_ge(s["mixed_low"], j)
                            for c in range(JT):
                                last = product(nc, ps_a[1][:, 0:DM], [a[:, c, :] for a in mixed_t],
                                               [a[:, c, :] for a in s_o], c == 0, c == JT - 1)
                            last.then_inc(s["out_ready"], 1)
                        if u < GB:
                            for o in range(SIDES):
                                pe.wait_ge(s["probs_ready"], SIDES * j + o + 1)
                                for c in range(JT):
                                    last = nc.tensor.matmul(ps_o[o][:, c * VW:(c + 1) * VW],
                                                            probs[:, o, c * SEQ:(c + 1) * SEQ],
                                                            v[:, u, SIDES * c + o, :], start=True, stop=True)
                            last.then_inc(s["heads_ready"], 1)

            @block.scalar
            def _(ac):
                ac.wait_ge(s["w_loaded"], 16 * len(raw))
                for i, (t, (hi, lo)) in enumerate(zip(raw, split)):
                    nc.scalar.activation(hi[:], t[:], ACT.Copy).then_inc(s["w_high"], 1)
                nc.scalar.preload_act_table(ACT.Exp)
                with ac.Fori(0, GROUPS) as g:
                    for k in range(KT):
                        ac.wait_ge(s["xn_turned"], KT * g + k + 1)
                        nc.scalar.activation(xnt[0][:, k, :], ps_a[k][:], ACT.Copy).then_inc(s["xn_high"], 1)
                    for b in range(GB):
                        ac.wait_ge(s["q_ready"], g * GB + b + 1)
                        nc.scalar.activation(qk[:, b, 0, :], ps_a[0][:], ACT.Copy).then_inc(s["q_copied"], 1)
                        ac.wait_ge(s["k_ready"], g * GB + b + 1)
                        nc.scalar.activation(qk[:, b, 1, :], ps_a[1][:], ACT.Copy).then_inc(s["k_copied"], 1)
                    for u in range(GB + 1):
                        j = g * GB + u
                        if u < GB:
                            ac.wait_ge(s["q_turned"], j + 1)
                            nc.scalar.activation(q_t[:].rearrange("p c t -> p (c t)"), ps_t[0][:],
                                                 ACT.Copy).then_inc(s["qt_ready"], 1)
                        if u:
                            ac.wait_ge(s["mixed_turned"], j)
                            nc.scalar.activation(mixed_t[0][:].rearrange("p c t -> p (c t)"), ps_a[0][:],
                                                 ACT.Copy).then_inc(s["mixed_high"], 1)
                        if u < GB:
                            for o in range(SIDES):
                                ac.wait_ge(s["scores_ready"], SIDES * j + o + 1)
                                if u and o == 0:
                                    ac.wait_ge(s["heads_ready"], j)
                                nc.scalar.activation(probs[:, o, :], ps_s[o][:], ACT.Exp, bias=less_scale[:, 0:1],
                                                     scale=SCALE).then_inc(s["probs_ready"], 1)

            @block.vector
            def _(dve):
                chain = Chain(dve, s["chain"])
                link = chain.link
                variance(core, dve, chain, s["variance_ready"])
                dve.sem_inc(s["squares_summed"], 2)
                dve.wait_ge(s["consts_set"], 1)
                dve.wait_ge(s["scale_ready"], 1)
                with dve.Fori(0, GROUPS) as g:
                    chain.enter(g, 2 + 2 * GB)
                    for t in range(GB):
                        last = nc.vector.tensor_scalar(xn[:, t, :], x[:, bass.ds(g * GB + t, 1), :].squeeze(1),
                                                       core.ln[:, 0, bass.ds(g * GB + t, 1)],
                                                       core.ln[:, 3, bass.ds(g * GB + t, 1)],
                                                       ALU.subtract, ALU.mult)
                    last.then_inc(s["xn_ready"], 1)
                    for k in range(KT):
                        dve.wait_ge(s["xn_high"], KT * g + k + 1)
                        nc.vector.tensor_tensor(xnt[1][:, k, :], ps_a[k][:], xnt[0][:, k, :].bitcast(F32),
                                                ALU.subtract).then_inc(s["xn_low"], 1)

                    def add_squares(b):
                        dve.wait_ge(s["squares_ready"], g * GB + b + 1)
                        nc.vector.tensor_reduce(norm[:, b, :],
                                                squares[:, b % 2].rearrange("p a (h d) -> p (a h) d", d=HD),
                                                AX.X, ALU.add).then_inc(s["squares_summed"], 1)

                    for b in range(GB):
                        dve.wait_ge(s["v_ready"], g * GB + b + 1)
                        nc.vector.tensor_copy(v[:, b, :, 0:HD],
                                              ps_t[b % 2][:].rearrange("p (h d) -> p h d", d=HD)).then_inc(s["v_copied"], 1)
                        if b:
                            add_squares(b - 1)
                    add_squares(GB - 1)
                    dve.wait_ge(s["norm_ready"], g + 1)
                    link(nc.vector.tensor_scalar(norm[:], norm[:], LEAST_NORM, None, ALU.max))
                    link(nc.vector.reciprocal(norm[:], norm[:]))
                    for b in range(GB):
                        qkb = qk[:, b].rearrange("p a (h d) -> p (a h) d", d=HD)
                        nc.vector.tensor_tensor(qkb, qkb, norm[:, b].unsqueeze(2).to_broadcast([P, 2 * HEADS, HD]),
                                                ALU.mult).then_inc(s["unit_ready"], 1)
                    for u in range(GB + 1):
                        j = g * GB + u
                        if u < GB:
                            dve.wait_ge(s["k_turned"], j + 1)
                            nc.vector.tensor_copy(k_t[:].rearrange("p c t -> p (c t)"),
                                                  ps_t[1][:]).then_inc(s["kt_ready"], 1)
                        if u:
                            dve.wait_ge(s["mixed_high"], j)
                            nc.vector.tensor_tensor(mixed_t[1][:].rearrange("p c t -> p (c t)"), ps_a[0][:],
                                                    mixed_t[0][:].rearrange("p c t -> p (c t)").bitcast(F32),
                                                    ALU.subtract).then_inc(s["mixed_low"], 1)
                            xb = x[:, bass.ds(j - 1, 1), :].squeeze(1)
                            dve.wait_ge(s["out_ready"], j)
                            nc.vector.tensor_tensor(xb, xb, ps_a[1][:, 0:DM], ALU.add).then_inc(s["x_updated"], 1)
                            dve.wait_ge(s["x_updated"], j)
                            nc.vector.bn_stats(core.stats[:, bass.ds(j - 1, 1), :].squeeze(1), xb)
                        if u < GB:
                            dve.wait_ge(s["heads_ready"], j + 1)
                            for o in range(SIDES):
                                sums = ps_o[o][:, 0:JT * VW].rearrange("p (c d) -> p c d", d=VW)[:, :, HD]
                                last = nc.vector.tensor_scalar(inv_sum[:, o, :], sums, LEAST_SUM, None, ALU.max)
                            link(last)
                            link(nc.vector.reciprocal(inv_sum[:], inv_sum[:]))
                            for o in range(SIDES):
                                last = nc.vector.tensor_tensor(
                                    mixed[:].rearrange("p (c o d) -> p c o d", o=SIDES, d=HD)[:, :, o, :],
                                    ps_o[o][:, 0:JT * VW].rearrange("p (c d) -> p c d", d=VW)[:, :, 0:HD],
                                    inv_sum[:, o, :].unsqueeze(2).to_broadcast([P, JT, HD]), ALU.mult)
                            last.then_inc(s["mixed_ready"], 1)
                    chain.leave(GROUPS)
        core.retire(s)


def as_is(a):
    return a


def rows(a):
    return a.reshape(-1, P, *a.shape[1:]).swapaxes(0, 1)


def turned(a):
    return rows(a.T)


def cross_layout(name, prefix, underscore):
    at = {f"{name}_W{c}": (f"{prefix}_W{underscore}{c}", turned) for c in "qkvo"}
    at |= {f"{name}_b{c}": (f"{prefix}_b{underscore}{c}", rows) for c in "qk"}
    return at | {f"{name}_b{c}": (f"{prefix}_b{underscore}{c}", as_is) for c in "vo"}


def stacked(a):
    return a.reshape(a.shape[0], -1, P, a.shape[2]).swapaxes(1, 2)


def joined(lay):
    return lambda a, b: lay(np.concatenate([a, b]))


LAYOUT = {
    "x": ("x", lambda a: a.swapaxes(0, 1)),
    "W_in": ("L0_attn_W_in", rows),
    "conv_w": ("L0_attn_conv_w", lambda a: rows(a[:, 0])),
    "W_B": ("L0_attn_W_B", rows),
    "W_C": ("L0_attn_W_C", rows),
    "W_delta": ("L0_attn_W_delta", rows),
    "delta_base": ("L0_attn_delta_base", rows),
    "W_tau": ("L0_attn_W_tau", rows),
    "A_log": ("L0_attn_A_log", rows),
    "W_out": ("L0_attn_W_out", rows),
    "context": ("ctx_1024", lambda a: a.swapaxes(0, 1)),
    "causal": ("mask_SxS2_fk0", as_is),
    "padding": ("mask_BxS2_bf0", as_is),
    **cross_layout("x0", "L0_xattn", ""),
    **cross_layout("x1", "L1_xattn", "_"),
    "a_Wq": ("L1_attn_Wq", rows),
    "a_Wkv": ("L1_attn_Wkv", rows),
    "a_Wo": ("L1_attn_Wo", rows),
    "e0_Wr": ("L0_ffn_gate_w", rows),
    "e0_br": ("L0_ffn_gate_b", as_is),
    "e0_W1": (("L0_ffn_sw1", "L0_ffn_rw1"), joined(stacked)),
    "e0_b1": (("L0_ffn_sb1", "L0_ffn_rb1"), joined(lambda a: a.reshape(len(a), -1, P).transpose(2, 0, 1))),
    "e0_W2": (("L0_ffn_sw2", "L0_ffn_rw2"), joined(stacked)),
    "e0_b2": (("L0_ffn_sb2", "L0_ffn_rb2"), joined(as_is)),
    "e1_Wr": ("L1_ffn_Wr", turned),
    "e1_br": ("L1_ffn_br", as_is),
    "e1_W1": ("L1_ffn_W1", lambda a: stacked(a.swapaxes(1, 2))),
    "e1_b1": ("L1_ffn_b1", lambda a: a.reshape(len(a), -1, P).transpose(2, 0, 1)),
    "e1_W2": ("L1_ffn_W2", lambda a: stacked(a.swapaxes(1, 2))),
    "e1_b2": ("L1_ffn_b2", as_is),
    "e1_gamma": ("L1_ffn_gamma", as_is),
    "e1_beta": ("L1_ffn_beta", as_is),
}


def constants():
    even = (np.arange(P) // 16 % 2 == 0)[:, None]
    at = {"side": np.concatenate([even, ~even], 1).astype(np.float32) / 4}
    for name, n in (("e0", 4), ("e1", 8)):
        at[f"{name}_before"] = np.broadcast_to(np.tril(np.ones((n, n), np.float32), -1), (P, n, n))
    return at


def decoder(nc, w, out):
    with ExitStack() as ctx:
        core = Core(nc, ctx)
        core.x = core.keep("x_stream", [P, TILES, DM])
        core.stats = core.keep("stats", [P, TILES, 6])
        core.ln = core.keep("ln", [P, 4, TILES])
        core.minus_half = core.keep("minus_half", [P, TILES])
        core.ident = core.keep("ident", [P, P])
        load(core, w)
        state_space(core, w)
        cross_attention(core, w, "x0", masked=False)
        experts(core, w, "e0", shared=2, routed=4, softmax_first=True, final=False)
        self_attention(core, w)
        cross_attention(core, w, "x1", masked=True)
        experts(core, w, "e1", shared=0, routed=8, softmax_first=False, final=True)
        store(core, out)


def store(core, out):
    nc, stored = core.nc, core.sem("stored")
    with nc.Block() as block:
        @block.sync
        def _(sp):
            sp.dma_start(out, core.x[:]).then_inc(stored, 16)
            sp.wait_ge(stored, 16)


def kernel(**inputs):
    import concourse.bacc as bacc
    from concourse.bass_utils import run_bass_kernel_spmd

    nc = bacc.Bacc("TRN2", target_bir_lowering=False, num_devices=1)
    arrays, w = {}, {}
    for name, (source, lay) in LAYOUT.items():
        sources = (source,) if isinstance(source, str) else source
        arrays[name] = lay(*(np.asarray(inputs[n]) for n in sources))
    arrays = {"in_" + n: np.ascontiguousarray(a) for n, a in (arrays | constants()).items()}
    for name, a in arrays.items():
        w[name[3:]] = nc.dram_tensor(name, a.shape, mybir.dt.from_np(a.dtype), kind="ExternalInput").ap()
    out = nc.dram_tensor("out", (SEQ, BATCH, DM), F32, kind="ExternalOutput").ap()
    decoder(nc, w, out)
    r = run_bass_kernel_spmd(nc, [arrays], core_ids=[0])
    return r.results[0]["out"].swapaxes(0, 1)
```

```python
from contextlib import ExitStack

import numpy as np

import concourse.bass as bass
from concourse import mybir

ALU = mybir.AluOpType
ACT = mybir.ActivationFunctionType
AX = mybir.AxisListType
F32 = mybir.dt.float32
F32R = mybir.dt.float32r
U8 = mybir.dt.uint8

P = 128
BATCH, SEQ, DM = 16, 128, 256
TILES = BATCH
KT = DM // P
GB = 4
GROUPS = TILES // GB
GT = GB * SEQ
LN_EPS = 1e-5


class Chain:

    def __init__(self, engine, sem):
        self.engine, self.sem = engine, sem
        self.done, self.base, self.inside = 0, 0, None

    def link(self, instruction):
        instruction.then_inc(self.sem, 1)
        self.done += 1
        self.engine.wait_ge(self.sem, self.base + self.done)

    def enter(self, turn, links):
        self.before, self.links = self.done, links
        self.base, self.done = turn * links + self.before, 0

    def leave(self, turns):
        assert self.done == self.links, (self.done, self.links)
        self.base, self.done = 0, self.before + turns * self.links


class Core:

    def __init__(self, nc, ctx):
        self.nc, self.ctx = nc, ctx

    def sem(self, name):
        return self.ctx.enter_context(self.nc.semaphore(name))

    def stage_sems(self, prefix, names):
        return {n: self.nc.alloc_semaphore(prefix + n) for n in names.split()}

    def retire(self, sems):
        nc, handles = self.nc, list(sems.values())
        numbers = sorted(h.num for h in handles)
        with nc.Block() as block:
            @block.sync
            def _(sp):
                at = 0
                while at < len(numbers):
                    end = at
                    while end + 1 < len(numbers) and numbers[end + 1] == numbers[end] + 1:
                        end += 1
                    sp.sem_clear(range(numbers[at], numbers[end] + 1))
                    at = end + 1
        for h in handles:
            nc.release_semaphore(h)

    def keep(self, name, shape, dt=F32):
        return self.ctx.enter_context(self.nc.sbuf_tensor(name, shape, dt))


def product(nc, out, lhs, rhs, first, last, skip=False):
    (lh, ll), (rh, rl) = lhs, rhs
    nc.tensor.matmul(out, lh, rl, start=first, stop=False, skip_group_check=skip)
    nc.tensor.matmul(out, ll, rh, start=False, stop=False, skip_group_check=skip)
    return nc.tensor.matmul(out, lh, rh, start=False, stop=last, skip_group_check=skip)


def variance(core, dve, chain, variance_ready):
    nc, st, ln = core.nc, core.stats, core.ln
    mean, var, diff = ln[:, 0, :], ln[:, 1, :], ln[:, 2, :]
    nc.vector.tensor_tensor(diff, st[:, :, 1], st[:, :, 4], ALU.subtract)
    nc.vector.tensor_tensor(mean, st[:, :, 1], st[:, :, 4], ALU.add)
    chain.link(nc.vector.tensor_tensor(var, st[:, :, 2], st[:, :, 5], ALU.add))
    nc.vector.tensor_scalar(mean, mean, 0.5, None, ALU.mult)
    nc.vector.tensor_scalar(var, var, 1.0 / DM, LN_EPS, ALU.mult, ALU.add)
    chain.link(nc.vector.tensor_tensor(diff, diff, diff, ALU.mult))
    nc.vector.scalar_tensor_tensor(out=var, in0=diff, scalar=0.25, in1=var,
                                   op0=ALU.mult, op1=ALU.add).then_inc(variance_ready, 1)


def inverse_deviation(core, pool, variance_ready, scale_ready):
    pool.wait_ge(variance_ready, 1)
    core.nc.gpsimd.tensor_tensor(core.ln[:, 3, :], core.ln[:, 1, :], core.minus_half[:],
                                 ALU.pow).then_inc(scale_ready, 1)


def normalise(core, out, tile):
    return core.nc.vector.tensor_scalar(out, core.x[:, tile, :], core.ln[:, 0, tile:tile + 1],
                                        core.ln[:, 3, tile:tile + 1], ALU.subtract, ALU.mult)


def load(core, w):
    nc = core.nc
    x_in, st = core.sem("x_in"), core.stats
    ident_set = core.sem("ident_set")
    with nc.Block() as block:
        @block.sync
        def _(sp):
            sp.dma_start(core.x[:], w["x"]).then_inc(x_in, 16)

        @block.gpsimd
        def _(pool):
            nc.gpsimd.memset(core.minus_half[:], -0.5)
            nc.gpsimd.memset(core.ident[:], 0.0).then_inc(ident_set, 1)
            pool.wait_ge(ident_set, 1)
            nc.gpsimd.affine_select(out=core.ident[:], in_=core.ident[:], compare_op=ALU.not_equal,
                                    fill=1.0, base=0, pattern=[[-1, P]], channel_multiplier=1)

        @block.vector
        def _(dve):
            dve.wait_ge(x_in, 16)
            for t in range(TILES):
                nc.vector.bn_stats(st[:, t, :], core.x[:, t, :])


def state_space(core, w):
    nc, x, ident = core.nc, core.x, core.ident
    STATE = w["A_log"].shape[2]
    PAIRS = STATE // 2
    PAD = SEQ + 2
    EPS_DA = 1e-6
    LEAST_A = -1e16

    with ExitStack() as ctx:
        def sb(name, shape, dt=F32):
            return ctx.enter_context(nc.sbuf_tensor("m_" + name, shape, dt))

        def ps(name, shape):
            return ctx.enter_context(nc.psum_tensor("m_" + name, shape, F32))

        w_in = sb("w_in", [P, KT, 2 * DM])
        w_bc = sb("w_bc", [P, KT, P])
        w_delta, w_tau, w_out = (sb(n, [P, KT, DM]) for n in ("w_delta", "w_tau", "w_out"))
        raw = [w_in, w_bc, w_delta, w_tau, w_out]
        split = [(sb(f"hi{i}", t.shape, F32R), sb(f"lo{i}", t.shape, F32R)) for i, t in enumerate(raw)]
        s_in, s_bc, s_delta, s_tau, s_out = split
        conv = sb("conv", [P, KT, 3])
        base = sb("base", [P, KT])
        a_log = sb("a_log", [P, KT, STATE])
        rate = sb("rate", [P, KT, STATE])
        half_rate = sb("half_rate", [P, KT, STATE])
        rate_kept = sb("rate_kept", [P, KT, STATE])
        pick = sb("pick", [2 * 2 * STATE, 2 * STATE])
        pick_r = sb("pick_r", [2 * 2 * STATE, 2 * STATE], F32R)

        xnt = (sb("xnt_hi", [P, KT, GT], F32R), sb("xnt_lo", [P, KT, GT], F32R))
        padded = sb("padded", [P, KT, GB, PAD])
        half_v = sb("half_v", [P, KT, GT])
        tanh_v = sb("tanh_v", [P, KT, GT])
        u = sb("u", [P, KT, GT])
        half_g = sb("half_g", [P, KT, GT])
        gate = sb("gate", [P, KT, GT])
        act = (sb("act_hi", [P, KT, GT], F32R), sb("act_lo", [P, KT, GT], F32R))
        bc = sb("bc", [4 * STATE, GT], F32R)
        delta = sb("delta", [P, KT, GT])
        du = sb("du", [P, KT, GT])
        y = sb("y", [P, KT, GT])
        xn = y[:].rearrange("p k (b d) -> p (k b) d", d=DM)
        den = sb("den", [P, 2, 2, KT, GT])
        inv_pair = sb("inv_pair", [P, 2, KT, GT])
        mult_pair = sb("mult_pair", [P, KT, GT])
        decay = sb("decay", [P, 2, 2, KT, GT])
        em = sb("em", [P, 2, 2, KT, GT])
        wb = sb("wb", [P, 2, KT, GT])
        h = sb("h", [P, 2, 2, KT, GT])
        bcs = sb("bcs", [P, 2, 2, 2, GT])

        ps_t = [ps(f"t{i}", [P, GT]) for i in range(2)]
        ps_z = [ps(f"z{i}", [P, GT]) for i in range(2)]
        ps_b = [ps(f"b{i}", [P, GT]) for i in range(4)]

        names = ("w_loaded w_high w_low small_set pick_ready rate_exp rate_set variance_ready scale_ready "
                 "xn_ready xnt_moved xnt_high xnt_low xn_added z_ready z_taken conv_ready tanh_ready u_ready "
                 "u_high u_low bc_ready bc_high bc_low z1_ready z1_high z1_low z2_ready exp_ready one_plus_ready "
                 "ln_ready delta_ready b_spread c_spread b_taken c_taken den_ready pair_inverted weighing_b em_ready "
                 "outputs_added weighted_b input_ready state_ready weighted_c y_ready y_high y_low out_ready "
                 "x_updated act_chain chain")
        s = core.stage_sems("m_", names)

        with nc.Block() as block:
            @block.sync
            def _(sp):
                sp.dma_start(w_in[:], w["W_in"]).then_inc(s["w_loaded"], 16)
                sp.dma_start(conv[:], w["conv_w"]).then_inc(s["w_loaded"], 16)
                for r in range(2):
                    for j, name in enumerate(("W_B", "W_C")):
                        at = (2 * r + j) * STATE
                        sp.dma_start(w_bc[:, :, at:at + STATE],
                                     w[name]).then_inc(s["w_loaded"], 16)
                sp.dma_start(w_delta[:], w["W_delta"]).then_inc(s["w_loaded"], 16)
                sp.dma_start(w_tau[:], w["W_tau"]).then_inc(s["w_loaded"], 16)
                sp.dma_start(w_out[:], w["W_out"]).then_inc(s["w_loaded"], 16)
                sp.dma_start(base[:], w["delta_base"]).then_inc(s["w_loaded"], 16)
                sp.dma_start(a_log[:], w["A_log"]).then_inc(s["w_loaded"], 16)
            LOADS = 11

            @block.gpsimd
            def _(pool):
                nc.gpsimd.memset(w_bc[:, :, 4 * STATE:], 0.0).then_inc(s["small_set"], 1)
                nc.gpsimd.memset(padded[:, :, :, 0:PAD:PAD - 1], 0.0).then_inc(s["small_set"], 1)
                nc.gpsimd.memset(pick[:], 0.0).then_inc(s["small_set"], 1)
                pool.wait_ge(s["small_set"], 3)
                for half in range(2):
                    at = pick[:]
                    nc.gpsimd.affine_select(out=at, in_=at, compare_op=ALU.not_equal, fill=1.0,
                                            base=-2 * STATE * half, pattern=[[-1, 2 * STATE]],
                                            channel_multiplier=1).then_inc(s["pick_ready"], 1)
                    pool.wait_ge(s["pick_ready"], half + 1)
                inverse_deviation(core, pool, s["variance_ready"], s["scale_ready"])
                pool.wait_ge(s["w_loaded"], 16 * LOADS)
                for i, (t, (hi, lo)) in enumerate(zip(raw, split)):
                    pool.wait_ge(s["w_high"], i + 1)
                    nc.gpsimd.tensor_tensor(lo[:], t[:], hi[:].bitcast(F32), ALU.subtract).then_inc(s["w_low"], 1)


                pool.sem_inc(s["weighted_b"], 2)
                pool.sem_inc(s["weighted_c"], 1)
                with pool.Fori(0, GROUPS) as g:
                    pool.wait_ge(s["xn_ready"], g + 1)
                    xg = x[:, bass.ds(g * GB, GB), :]
                    nc.gpsimd.tensor_tensor(xg, xg, xn, ALU.add).then_inc(s["xn_added"], 1)
                    pool.wait_ge(s["delta_ready"], g + 1)

                    def weigh_c(p):
                        pool.wait_ge(s["state_ready"], 2 + g * PAIRS + p + 1)
                        pool.wait_ge(s["c_taken"], 1 + g * PAIRS + p + 1)
                        for k in range(2):
                            c_all = bcs[:, p % 2, 1, k, :].unsqueeze(1).to_broadcast([P, KT, GT])
                            last = nc.gpsimd.tensor_tensor(h[:, p % 2, k], h[:, p % 2, k], c_all, ALU.mult)
                        last.then_inc(s["weighted_c"], 1)

                    for p in range(PAIRS):
                        i = g * PAIRS + p
                        pool.wait_ge(s["b_taken"], 1 + i + 1)
                        pool.wait_ge(s["pair_inverted"], i + 1)
                        pool.wait_ge(s["input_ready"], i + 1)
                        for k in range(2):
                            b_all = bcs[:, p % 2, 0, k, :].unsqueeze(1).to_broadcast([P, KT, GT])
                            nc.gpsimd.tensor_tensor(wb[:, k], inv_pair[:, p % 2], b_all,
                                                    ALU.mult).then_inc(s["weighing_b"], 1)
                        pool.wait_ge(s["weighing_b"], 2 * i + 2)
                        for k in range(2):
                            nc.gpsimd.tensor_tensor(wb[:, k], wb[:, k], den[:, p % 2, 1 - k],
                                                    ALU.mult).then_inc(s["weighted_b"], 1)
                        if p:
                            weigh_c(p - 1)
                    weigh_c(PAIRS - 1)

            @block.tensor
            def _(pe):
                pe.wait_ge(s["w_low"], len(raw))
                pe.wait_ge(s["rate_set"], 1)
                with pe.Fori(0, GROUPS) as g:
                    pe.wait_ge(s["xn_ready"], g + 1)
                    for k in range(KT):
                        for t in range(GB):
                            last = nc.tensor.transpose(ps_t[k][:, t * P:(t + 1) * P],
                                                       xn[:, t, k * P:(k + 1) * P], ident[:])
                        last.then_inc(s["xnt_moved"], 1)
                    pe.wait_ge(s["xnt_low"], KT * g + KT)
                    for m in range(2 * KT):
                        if m >= 2:
                            pe.wait_ge(s["z_taken"], 4 * g + m - 1)
                        for k in range(KT):
                            last = product(nc, ps_z[m % 2][:], [a[:, k, m * P:(m + 1) * P] for a in s_in],
                                           [a[:, k, :] for a in xnt], k == 0, k == KT - 1)
                        last.then_inc(s["z_ready"], 1)
                    pe.wait_ge(s["u_low"], g + 1)
                    for k in range(KT):
                        last = product(nc, ps_t[0][:], [a[:, k, :] for a in s_bc],
                                       [a[:, k, :] for a in act], k == 0, k == KT - 1)
                    last.then_inc(s["bc_ready"], 1)
                    for m in range(KT):
                        pe.wait_ge(s["z_taken"], 4 * g + 3 + m)
                        for k in range(KT):
                            last = product(nc, ps_z[m][:], [a[:, k, m * P:(m + 1) * P] for a in s_delta],
                                           [a[:, k, :] for a in act], k == 0, k == KT - 1)
                        last.then_inc(s["z1_ready"], 1)
                    pe.wait_ge(s["z1_low"], KT * g + KT)
                    for m in range(KT):
                        for k in range(KT):
                            last = product(nc, ps_z[m][:], [a[:, k, m * P:(m + 1) * P] for a in s_tau],
                                           [a[:, k, :] for a in xnt], k == 0, k == KT - 1)
                        last.then_inc(s["z2_ready"], 1)
                    pe.wait_ge(s["bc_low"], g + 1)

                    def add_outputs(p):
                        pe.wait_ge(s["weighted_c"], 1 + g * PAIRS + p + 1)
                        for k in range(2):
                            for c in range(KT):
                                last = nc.tensor.matmul(ps_t[c][:], ident[:], h[:, p % 2, k, c], start=(p == 0 and k == 0),
                                                        stop=(p == PAIRS - 1 and k == 1))
                        last.then_inc(s["outputs_added"], 1)

                    def spread(p, rows, taken, ready):
                        pe.wait_ge(taken, g * PAIRS + p + 1)
                        for k in range(2):
                            row = rows * STATE + 2 * p + k
                            last = nc.tensor.matmul(ps_b[2 * rows + k][:],
                                                    pick_r[:, row:row + 1].to_broadcast([4 * STATE, P]), bc[:],
                                                    start=True, stop=True)
                        last.then_inc(ready, 1)

                    spread(0, 0, s["b_taken"], s["b_spread"])
                    for p in range(PAIRS):
                        if p + 1 < PAIRS:
                            spread(p + 1, 0, s["b_taken"], s["b_spread"])
                        spread(p, 1, s["c_taken"], s["c_spread"])
                        if p >= 2:
                            add_outputs(p - 2)
                    add_outputs(PAIRS - 2)
                    add_outputs(PAIRS - 1)
                    pe.wait_ge(s["y_low"], g + 1)
                    for t in range(GB):
                        for k in range(KT):
                            last = product(nc, ps_t[t // 2][:, (t % 2) * DM:(t % 2 + 1) * DM],
                                           [a[:, k, t * P:(t + 1) * P] for a in act],
                                           [a[:, k, :] for a in s_out], k == 0, k == KT - 1)
                        if t % 2:
                            last.then_inc(s["out_ready"], 1)

            @block.scalar
            def _(ac):
                ac.wait_ge(s["w_loaded"], 16 * LOADS)
                ac.wait_ge(s["small_set"], 1)
                for i, (t, (hi, lo)) in enumerate(zip(raw, split)):
                    nc.scalar.activation(hi[:], t[:], ACT.Copy).then_inc(s["w_high"], 1)
                nc.scalar.activation(rate[:], a_log[:], ACT.Exp).then_inc(s["rate_exp"], 1)
                ac.sem_inc(s["b_taken"], 1)
                ac.sem_inc(s["c_taken"], 1)
                ac.wait_ge(s["rate_set"], 1)
                chain = Chain(ac, s["act_chain"])
                with ac.Fori(0, GROUPS) as g:
                    chain.enter(g, KT)
                    for k in range(KT):
                        ac.wait_ge(s["xnt_moved"], KT * g + k + 1)
                        nc.scalar.activation(xnt[0][:, k, :], ps_t[k][:], ACT.Copy).then_inc(s["xnt_high"], 1)
                    for m in range(KT):
                        ac.wait_ge(s["z_ready"], 4 * g + m + 1)
                        nc.scalar.activation(padded[:, m, :, 1:SEQ + 1],
                                             ps_z[m][:].rearrange("p (b s) -> p b s", s=SEQ),
                                             ACT.Copy).then_inc(s["z_taken"], 1)
                    for m in range(KT):
                        ac.wait_ge(s["z_ready"], 4 * g + KT + m + 1)
                        nc.scalar.activation(half_g[:, m, :], ps_z[m][:], ACT.Copy, scale=0.5)
                        nc.scalar.activation(gate[:, m, :], ps_z[m][:], ACT.Tanh,
                                             scale=0.5).then_inc(s["z_taken"], 1)
                    ac.wait_ge(s["conv_ready"], g + 1)
                    nc.scalar.activation(tanh_v[:], half_v[:], ACT.Tanh).then_inc(s["tanh_ready"], 1)
                    ac.wait_ge(s["u_ready"], g + 1)
                    nc.scalar.activation(act[0][:], u[:], ACT.Copy).then_inc(s["u_high"], 1)
                    ac.wait_ge(s["bc_ready"], g + 1)
                    nc.scalar.activation(bc[:], ps_t[0][0:4 * STATE, :], ACT.Copy).then_inc(s["bc_high"], 1)
                    for m in range(KT):
                        ac.wait_ge(s["z1_ready"], KT * g + m + 1)
                        nc.scalar.activation(xnt[0][:, m, :], ps_z[m][:], ACT.Identity,
                                             bias=base[:, m:m + 1]).then_inc(s["z1_high"], 1)
                    for m in range(KT):
                        ac.wait_ge(s["z2_ready"], KT * g + m + 1)
                        chain.link(nc.scalar.activation(tanh_v[:, m, :], ps_z[m][:], ACT.Abs))
                    nc.scalar.activation(tanh_v[:], tanh_v[:], ACT.Exp, scale=-1.0).then_inc(s["exp_ready"], 1)
                    ac.wait_ge(s["one_plus_ready"], g + 1)
                    nc.scalar.activation(du[:], half_v[:], ACT.Ln).then_inc(s["ln_ready"], 1)
                    ac.wait_ge(s["delta_ready"], g + 1)
                    chain.leave(GROUPS)

                    def copy_b(p):
                        i = g * PAIRS + p
                        if p >= 2:
                            ac.wait_ge(s["weighing_b"], 2 * i - 2)
                        ac.wait_ge(s["b_spread"], i + 1)
                        for k in range(2):
                            last = nc.scalar.activation(bcs[:, p % 2, 0, k, :], ps_b[k][:], ACT.Copy)
                        last.then_inc(s["b_taken"], 1)

                    def copy_c(p):
                        i = g * PAIRS + p
                        if p >= 2:
                            ac.wait_ge(s["weighted_c"], i)
                        ac.wait_ge(s["c_spread"], i + 1)
                        for k in range(2):
                            last = nc.scalar.activation(bcs[:, p % 2, 1, k, :], ps_b[2 + k][:], ACT.Copy)
                        last.then_inc(s["c_taken"], 1)

                    def denominators(p):
                        i = g * PAIRS + p
                        ac.wait_ge(s["weighted_b"], 2 * i)
                        for k in range(2):
                            for c in range(KT):
                                n = 2 * p + k
                                last = nc.scalar.activation(den[:, p % 2, k, c, :], delta[:, c, :], ACT.Copy,
                                                            bias=EPS_DA, scale=rate_kept[:, c, n:n + 1])
                        last.then_inc(s["den_ready"], 1)

                    def exponentials(p):
                        i = g * PAIRS + p
                        ac.wait_ge(s["state_ready"], i + 1)
                        for k in range(2):
                            for c in range(KT):
                                n = 2 * p + k
                                nc.scalar.activation(em[:, p % 2, k, c, :], delta[:, c, :], ACT.Tanh,
                                                     scale=half_rate[:, c, n:n + 1])
                                last = nc.scalar.activation(decay[:, p % 2, k, c, :], delta[:, c, :], ACT.Exp,
                                                            scale=rate[:, c, n:n + 1])
                        last.then_inc(s["em_ready"], 1)

                    denominators(0)
                    copy_b(0)
                    exponentials(0)
                    for p in range(PAIRS):
                        if p + 1 < PAIRS:
                            denominators(p + 1)
                            copy_b(p + 1)
                        copy_c(p)
                        if p + 1 < PAIRS:
                            exponentials(p + 1)
                    ac.wait_ge(s["y_ready"], g + 1)
                    nc.scalar.activation(act[0][:], y[:], ACT.Copy).then_inc(s["y_high"], 1)

            @block.vector
            def _(dve):
                chain = Chain(dve, s["chain"])
                link = chain.link
                variance(core, dve, chain, s["variance_ready"])
                dve.wait_ge(s["w_loaded"], 16 * LOADS)
                dve.wait_ge(s["small_set"], 2)
                dve.wait_ge(s["pick_ready"], 2)
                nc.vector.tensor_copy(pick_r[:], pick[:])
                nc.vector.tensor_scalar(conv[:], conv[:], 0.5, None, ALU.mult)
                dve.wait_ge(s["rate_exp"], 1)
                nc.vector.tensor_scalar(half_rate[:], rate[:], -0.5, None, ALU.mult)
                nc.vector.tensor_scalar(rate_kept[:], rate[:], -1.0, LEAST_A, ALU.mult, ALU.max)
                nc.vector.tensor_scalar(rate[:], rate[:], -1.0, None, ALU.mult).then_inc(s["rate_set"], 1)
                dve.sem_inc(s["outputs_added"], 2)
                dve.sem_inc(s["input_ready"], 1)
                dve.sem_inc(s["state_ready"], 2)
                dve.wait_ge(s["scale_ready"], 1)
                with dve.Fori(0, GROUPS) as g:
                    chain.enter(g, 3 + 7 + 3 * PAIRS + 1)
                    for t in range(GB):
                        last = nc.vector.tensor_scalar(xn[:, t, :], x[:, bass.ds(g * GB + t, 1), :].squeeze(1),
                                                       core.ln[:, 0, bass.ds(g * GB + t, 1)],
                                                       core.ln[:, 3, bass.ds(g * GB + t, 1)],
                                                       ALU.subtract, ALU.mult)
                    last.then_inc(s["xn_ready"], 1)
                    for k in range(KT):
                        dve.wait_ge(s["xnt_high"], KT * g + k + 1)
                        nc.vector.tensor_tensor(xnt[1][:, k, :], ps_t[k][:], xnt[0][:, k, :].bitcast(F32),
                                                ALU.subtract).then_inc(s["xnt_low"], 1)
                    dve.wait_ge(s["z_taken"], 4 * g + KT)
                    for j in range(3):
                        for c in range(KT):
                            out = half_v[:, c, :].rearrange("p (b s) -> p b s", s=SEQ)
                            src, tap = padded[:, c, :, j:j + SEQ], conv[:, c, j:j + 1]
                            if j == 0:
                                last = nc.vector.tensor_scalar(out, src, tap, None, ALU.mult)
                            else:
                                last = nc.vector.scalar_tensor_tensor(out=out, in0=src, scalar=tap, in1=out,
                                                                      op0=ALU.mult, op1=ALU.add)
                        if j < 2:
                            link(last)
                    last.then_inc(s["conv_ready"], 1)
                    dve.wait_ge(s["tanh_ready"], g + 1)
                    nc.vector.scalar_tensor_tensor(out=u[:], in0=tanh_v[:], scalar=1.0, in1=half_v[:],
                                                   op0=ALU.add, op1=ALU.mult).then_inc(s["u_ready"], 1)
                    dve.wait_ge(s["z_taken"], 4 * g + 2 * KT)
                    link(nc.vector.scalar_tensor_tensor(out=gate[:], in0=gate[:], scalar=1.0, in1=half_g[:],
                                                        op0=ALU.add, op1=ALU.mult))
                    dve.wait_ge(s["u_high"], g + 1)
                    nc.vector.tensor_tensor(act[1][:], u[:], act[0][:].bitcast(F32),
                                            ALU.subtract).then_inc(s["u_low"], 1)
                    dve.wait_ge(s["bc_high"], g + 1)
                    low = slice(2 * STATE, 4 * STATE)
                    nc.vector.tensor_tensor(bc[low, :], ps_t[0][low, :], bc[low, :].bitcast(F32),
                                            ALU.subtract).then_inc(s["bc_low"], 1)
                    for m in range(KT):
                        dve.wait_ge(s["z1_high"], KT * g + m + 1)
                        nc.vector.scalar_tensor_tensor(out=xnt[1][:, m, :], in0=ps_z[m][:], scalar=base[:, m:m + 1],
                                                       in1=xnt[0][:, m, :].bitcast(F32), op0=ALU.add,
                                                       op1=ALU.subtract).then_inc(s["z1_low"], 1)
                    dve.wait_ge(s["exp_ready"], g + 1)
                    dve.wait_ge(s["xn_added"], g + 1)
                    nc.vector.tensor_scalar(half_v[:], tanh_v[:], 1.0, None, ALU.add).then_inc(s["one_plus_ready"], 1)
                    dve.wait_ge(s["one_plus_ready"], g + 1)
                    link(nc.vector.tensor_scalar(y[:], half_v[:], 1.0, None, ALU.is_equal))
                    link(nc.vector.scalar_tensor_tensor(out=delta[:], in0=half_v[:], scalar=-1.0, in1=y[:],
                                                        op0=ALU.add, op1=ALU.add))
                    link(nc.vector.reciprocal(mult_pair[:], delta[:]))
                    dve.wait_ge(s["ln_ready"], g + 1)
                    link(nc.vector.tensor_tensor(du[:], du[:], y[:], ALU.add))
                    link(nc.vector.tensor_tensor(du[:], du[:], mult_pair[:], ALU.mult))
                    link(nc.vector.tensor_tensor(du[:], du[:], tanh_v[:], ALU.mult))
                    for m in range(KT):
                        last = nc.vector.scalar_tensor_tensor(out=delta[:, m, :], in0=ps_z[m][:], scalar=0.0,
                                                              in1=du[:, m, :], op0=ALU.max, op1=ALU.add)
                    link(last)
                    nc.vector.tensor_tensor(du[:], delta[:], u[:], ALU.mult).then_inc(s["delta_ready"], 1)

                    def invert(p):
                        dve.wait_ge(s["den_ready"], g * PAIRS + p + 1)
                        dve.wait_ge(s["weighted_b"], 2 * (g * PAIRS + p))
                        if p:
                            dve.wait_ge(s["pair_inverted"], g * PAIRS + p)
                        link(nc.vector.tensor_tensor(mult_pair[:], den[:, p % 2, 0], den[:, p % 2, 1], ALU.mult))
                        link(nc.vector.reciprocal(mult_pair[:], mult_pair[:]))
                        nc.vector.tensor_tensor(inv_pair[:, p % 2], mult_pair[:], du[:],
                                                ALU.mult).then_inc(s["pair_inverted"], 1)

                    invert(0)
                    for p in range(PAIRS):
                        i = g * PAIRS + p
                        e, a = em[:, p % 2], decay[:, p % 2]
                        if p + 1 < PAIRS:
                            invert(p + 1)
                        dve.wait_ge(s["em_ready"], i + 1)
                        link(nc.vector.scalar_tensor_tensor(out=e, in0=a, scalar=1.0, in1=e,
                                                            op0=ALU.add, op1=ALU.mult))
                        nc.vector.memset(a.rearrange("p k c (b t) -> p (k c b) t", t=SEQ)[:, :, 0:1], 0.0)
                        dve.wait_ge(s["weighted_b"], 2 + 2 * i + 2)
                        nc.vector.tensor_tensor(e, e, wb[:], ALU.mult).then_inc(s["input_ready"], 1)
                        dve.wait_ge(s["outputs_added"], i + 1)
                        dve.wait_ge(s["input_ready"], 1 + i + 1)
                        for k in range(2):
                            for c in range(KT):
                                last = nc.vector.tensor_tensor_scan(h[:, p % 2, k, c], a[:, k, c], e[:, k, c], 0.0,
                                                                    ALU.mult, ALU.add)
                        last.then_inc(s["state_ready"], 1)
                    dve.wait_ge(s["outputs_added"], 2 + g * PAIRS + PAIRS)
                    for c in range(KT):
                        last = nc.vector.tensor_tensor(y[:, c, :], ps_t[c][:], gate[:, c, :], ALU.mult)
                    last.then_inc(s["y_ready"], 1)
                    dve.wait_ge(s["y_high"], g + 1)
                    nc.vector.tensor_tensor(act[1][:], y[:], act[0][:].bitcast(F32),
                                            ALU.subtract).then_inc(s["y_low"], 1)
                    dve.wait_ge(s["xn_added"], g + 1)
                    for j in range(GB // 2):
                        dve.wait_ge(s["out_ready"], (GB // 2) * g + j + 1)
                        xg = x[:, bass.ds(g * GB + 2 * j, 2), :]
                        last = nc.vector.tensor_tensor(xg, xg, ps_t[j][:].rearrange("p (t d) -> p t d", d=DM),
                                                       ALU.add)
                    link(last)
                    for t in range(GB):
                        nc.vector.bn_stats(core.stats[:, bass.ds(g * GB + t, 1), :].squeeze(1),
                                           x[:, bass.ds(g * GB + t, 1), :].squeeze(1))
                    chain.leave(GROUPS)
        core.retire(s)


def cross_attention(core, w, name, masked):
    nc, x, ident = core.nc, core.x, core.ident
    HEADS, HD = 16, DM // 16
    SIDES = P // HD
    ROWS = SIDES // 2
    VW = HD + 1
    NEG = -1e9
    SLOTS = GB * ROWS

    with ExitStack() as ctx:
        def sb(n, shape, dt=F32):
            return ctx.enter_context(nc.sbuf_tensor(f"{name}_{n}", shape, dt))

        def ps(n):
            return ctx.enter_context(nc.psum_tensor(f"{name}_{n}", [P, GT], F32))

        raw = [sb(n, [P, KT, DM]) for n in ("w_q", "w_k", "w_v", "w_o")]
        split = [(sb(f"hi{i}", t.shape, F32R), sb(f"lo{i}", t.shape, F32R)) for i, t in enumerate(raw)]
        s_q, s_k, s_v, s_o = split
        b_q, b_k = sb("b_q", [P, KT]), sb("b_k", [P, KT])
        b_v, b_o = sb("b_v", [P, DM]), sb("b_o", [P, DM])
        side = sb("side", [P, SIDES])
        b_scaled = sb("b_scaled", [P, KT])
        context = sb("context", [P, GB, DM])
        if masked:
            padded = sb("padded", [P, TILES, SEQ], U8)
            causal = sb("causal", [P, SEQ])
            mask = sb("mask", [P, TILES, SEQ])
            keep = sb("keep", [P, TILES, SEQ])

        xn = sb("xn", [P, GB, DM])
        xnt = (sb("xnt_hi", [P, KT, GT], F32R), sb("xnt_lo", [P, KT, GT], F32R))
        cnt = (sb("cnt_hi", [P, KT, GT], F32R), sb("cnt_lo", [P, KT, GT], F32R))
        q_all = sb("q_all", [P, KT, GT])
        q = [sb(f"q{h}", [P, KT, GT]) for h in range(SIDES)]
        k_t = sb("k", [P, KT, GT])
        v = sb("v", [P, GB, HEADS, VW])
        shifted = sb("shifted", [P, ROWS, 4, SEQ])
        top = sb("top", [P, ROWS, 4])
        masked_s = sb("masked_s", [P, ROWS, 4, SEQ]) if masked else None
        probs_t = sb("probs_t", [P, 2, 4 * SEQ])
        inv_sum = sb("inv_sum", [P, HEADS])
        mixed = sb("mixed", [P, DM])
        mixed_t = (sb("mixed_hi", [P, KT, SEQ], F32R), sb("mixed_lo", [P, KT, SEQ], F32R))

        ps_s = [ps(f"s{i}") for i in range(ROWS)]
        ps_t = [ps(f"t{i}") for i in range(2)]
        ps_o, ps_p = ps("o"), ps("p")
        v_banks = (ps_o, ps_p)

        names = ("w_loaded w_high w_low side_set variance_ready scale_ready cn_loaded cn_turned cn_high "
                 "cn_low k_ready k_taken v_ready v_taken xn_ready bias_added xn_turned xn_high xn_low q_ready q_scaled q_even q_odd "
                 "scores_ready scores_taken scores_masked shift_ready probs_ready probs_turned "
                 "probs_copied heads_ready mixed_ready mixed_turned mixed_high mixed_low out_ready x_updated "
                 "ones_set mask_ready chain")
        s = core.stage_sems(name + "_", names)
        LOADS = 9 + 2 * masked
        taken = s["scores_taken"] if masked else s["shift_ready"]

        with nc.Block() as block:
            @block.sync
            def _(sp):
                for t, n in zip(raw, ("Wq", "Wk", "Wv", "Wo")):
                    sp.dma_start(t[:], w[f"{name}_{n}"]).then_inc(s["w_loaded"], 16)
                sp.dma_start(b_q[:], w[f"{name}_bq"]).then_inc(s["w_loaded"], 16)
                sp.dma_start(b_k[:], w[f"{name}_bk"]).then_inc(s["w_loaded"], 16)
                sp.dma_start(b_v[:], w[f"{name}_bv"].partition_broadcast(P)).then_inc(s["w_loaded"], 16)
                sp.dma_start(b_o[:], w[f"{name}_bo"].partition_broadcast(P)).then_inc(s["w_loaded"], 16)
                sp.dma_start(side[:], w["side"]).then_inc(s["w_loaded"], 16)
                if masked:
                    sp.dma_start(padded[:], w["padding"].partition_broadcast(P)).then_inc(s["w_loaded"], 16)
                    sp.dma_start(causal[:], w["causal"]).then_inc(s["w_loaded"], 16)
                with sp.Fori(0, GROUPS) as g:
                    sp.wait_ge(s["cn_turned"], KT * g + KT)
                    sp.dma_start(context[:], w["context"][:, bass.ds(g * GB, GB), :]).then_inc(s["cn_loaded"], 16)

            @block.gpsimd
            def _(pool):
                nc.gpsimd.memset(v[:, :, :, HD:VW], 1.0).then_inc(s["ones_set"], 1)
                inverse_deviation(core, pool, s["variance_ready"], s["scale_ready"])
                pool.wait_ge(s["w_loaded"], 16 * LOADS)
                for i, (t, (hi, lo)) in enumerate(zip(raw, split)):
                    pool.wait_ge(s["w_high"], i + 1)
                    nc.gpsimd.tensor_tensor(lo[:], t[:], hi[:].bitcast(F32), ALU.subtract).then_inc(s["w_low"], 1)
                with pool.Fori(0, GROUPS) as g:
                    pool.wait_ge(s["xn_ready"], g + 1)
                    xg = x[:, bass.ds(g * GB, GB), :]
                    nc.gpsimd.tensor_tensor(xg, xg, b_o[:].unsqueeze(1).to_broadcast([P, GB, DM]),
                                            ALU.add).then_inc(s["bias_added"], 1)
                    if masked:
                        for u in range(SLOTS):
                            i, r = g * SLOTS + u, u % ROWS
                            pool.wait_ge(s["scores_masked"], i + 1)
                            pool.wait_ge(s["probs_turned"], i + 1)
                            nc.gpsimd.tensor_tensor(shifted[:, r], masked_s[:, r],
                                                    top[:, r].unsqueeze(2).to_broadcast([P, 4, SEQ]),
                                                    ALU.subtract).then_inc(s["shift_ready"], 1)

            @block.tensor
            def _(pe):
                pe.sem_inc(s["cn_turned"], KT)
                pe.sem_inc(s["probs_turned"], ROWS)
                pe.sem_inc(s["heads_ready"], 2)
                pe.sem_inc(s["mixed_turned"], 1)
                pe.sem_inc(s["out_ready"], 1)
                pe.wait_ge(s["ones_set"], 1)
                with pe.Fori(0, GROUPS) as g:
                    pe.wait_ge(taken, ROWS + SLOTS * g)
                    pe.wait_ge(s["cn_loaded"], 16 * g + 16)
                    for k in range(KT):
                        for t in range(GB):
                            last = nc.tensor.transpose(ps_s[k][:, t * P:(t + 1) * P], context[:, t, k * P:(k + 1) * P],
                                                       ident[:])
                        last.then_inc(s["cn_turned"], 1)
                    pe.wait_ge(s["xn_ready"], g + 1)
                    for k in range(KT):
                        for t in range(GB):
                            last = nc.tensor.transpose(ps_s[2 + k][:, t * P:(t + 1) * P], xn[:, t, k * P:(k + 1) * P],
                                                       ident[:])
                        last.then_inc(s["xn_turned"], 1)
                    pe.wait_ge(s["w_low"], len(raw))
                    pe.wait_ge(s["cn_low"], KT * g + KT)
                    pe.wait_ge(s["probs_copied"], 2 + SLOTS * g)
                    for m in range(KT):
                        for k in range(KT):
                            last = product(nc, ps_t[m][:], [a[:, k, m * P:(m + 1) * P] for a in s_k],
                                           [a[:, k, :] for a in cnt], k == 0, k == KT - 1)
                        last.then_inc(s["k_ready"], 1)
                    pe.wait_ge(s["xn_low"], KT * g + KT)
                    for m in range(KT):
                        for k in range(KT):
                            last = product(nc, ps_s[m][:], [a[:, k, m * P:(m + 1) * P] for a in s_q],
                                           [a[:, k, :] for a in xnt], k == 0, k == KT - 1)
                        last.then_inc(s["q_ready"], 1)
                    pe.wait_ge(s["mixed_ready"], 1 + GB * g)
                    pe.wait_ge(s["x_updated"], 1 + GB * g)
                    for t in range(GB):
                        for k in range(KT):
                            last = product(nc, v_banks[t // 2][:, (t % 2) * DM:(t % 2 + 1) * DM],
                                           [a[:, k, t * P:(t + 1) * P] for a in cnt],
                                           [a[:, k, :] for a in s_v], k == 0, k == KT - 1)
                        if t % 2:
                            last.then_inc(s["v_ready"], 1)
                    pe.wait_ge(s["k_taken"], KT * g + KT)
                    pe.wait_ge(s["q_scaled"], KT * g + KT)
                    pe.wait_ge(s["v_taken"], 2 * g + 2)
                    for u in range(SLOTS + 6):
                        if u < SLOTS:
                            b, r = divmod(u, ROWS)
                            pe.wait_ge(taken, g * SLOTS + u + 1)
                            if b == 0:
                                pe.wait_ge(s["q_even"], ROWS * g + r + 1)
                                pe.wait_ge(s["q_odd"], ROWS * g + r + 1)
                            cols = slice(b * SEQ, (b + 1) * SEQ)
                            for m in range(KT):
                                for o in range(2):
                                    at = (2 * m + o) * SEQ
                                    last = nc.tensor.matmul(ps_s[r][:, at:at + SEQ], q[2 * r + o][:, m, cols],
                                                            k_t[:, m, cols], start=True, stop=True)
                            last.then_inc(s["scores_ready"], 1)
                        if 0 <= u - 2 < SLOTS:
                            i, r = g * SLOTS + u - 2, (u - 2) % ROWS
                            pe.wait_ge(s["probs_ready"], i + 1)
                            pe.wait_ge(s["probs_copied"], i + 1)
                            for j in range(4):
                                last = nc.tensor.transpose(ps_t[u % 2][:, j * SEQ:(j + 1) * SEQ],
                                                           shifted[:, r, j, :], ident[:])
                            last.then_inc(s["probs_turned"], 1)
                        if 0 <= u - 3 < SLOTS:
                            b, r = divmod(u - 3, ROWS)
                            pe.wait_ge(s["probs_copied"], 2 + g * SLOTS + u - 3 + 1)
                            if r == 0:
                                pe.wait_ge(s["mixed_ready"], g * GB + b + 1)
                            for j in range(4):
                                head = SIDES * (j // 2) + 2 * r + j % 2
                                last = nc.tensor.matmul(ps_o[:, head * VW:(head + 1) * VW],
                                                        probs_t[:, (u - 3) % 2, j * SEQ:(j + 1) * SEQ],
                                                        v[:, b, head, :], start=True, stop=True)
                            last.then_inc(s["heads_ready"], 1)
                        b, late = divmod(u - 8, ROWS)
                        if late == 0 and 0 <= b < GB:
                            pe.wait_ge(s["mixed_ready"], 1 + g * GB + b + 1)
                            pe.wait_ge(s["x_updated"], g * GB + b + 1)
                            for k in range(KT):
                                last = nc.tensor.transpose(ps_p[:, k * P:(k + 1) * P], mixed[:, k * P:(k + 1) * P],
                                                           ident[:])
                            last.then_inc(s["mixed_turned"], 1)
                        b, late = divmod(u - 9, ROWS)
                        if late == 0 and 0 <= b < GB:
                            pe.wait_ge(s["mixed_low"], g * GB + b + 1)
                            for k in range(KT):
                                last = product(nc, ps_p[:, DM:2 * DM], [a[:, k, :] for a in mixed_t],
                                               [a[:, k, :] for a in s_o], k == 0, k == KT - 1)
                            last.then_inc(s["out_ready"], 1)

            @block.scalar
            def _(ac):
                ac.wait_ge(s["w_loaded"], 16 * LOADS)
                for i, (t, (hi, lo)) in enumerate(zip(raw, split)):
                    nc.scalar.activation(hi[:], t[:], ACT.Copy).then_inc(s["w_high"], 1)
                ac.sem_inc(s["probs_copied"], 2)
                nc.scalar.preload_act_table(ACT.Exp)
                ac.wait_ge(s["side_set"], 1)
                with ac.Fori(0, GROUPS) as g:
                    for k in range(KT):
                        ac.wait_ge(s["cn_turned"], KT + KT * g + k + 1)
                        nc.scalar.activation(cnt[0][:, k, :], ps_s[k][:], ACT.Copy).then_inc(s["cn_high"], 1)
                    for k in range(KT):
                        ac.wait_ge(s["xn_turned"], KT * g + k + 1)
                        nc.scalar.activation(xnt[0][:, k, :], ps_s[2 + k][:], ACT.Copy).then_inc(s["xn_high"], 1)
                    if not masked:
                        for m in range(KT):
                            ac.wait_ge(s["k_ready"], KT * g + m + 1)
                            nc.scalar.activation(k_t[:, m, :], ps_t[m][:], ACT.Identity,
                                                 bias=b_k[:, m:m + 1]).then_inc(s["k_taken"], 1)
                    for m in range(KT):
                        ac.wait_ge(s["q_ready"], KT * g + m + 1)
                        nc.scalar.activation(q_all[:, m, :], ps_s[m][:], ACT.Identity, bias=b_scaled[:, m:m + 1],
                                             scale=HD ** -0.5).then_inc(s["q_scaled"], 1)
                    ac.wait_ge(s["q_scaled"], KT * g + KT)
                    for r in range(ROWS):
                        nc.scalar.activation(q[2 * r][:], q_all[:], ACT.Copy,
                                             scale=side[:, 2 * r:2 * r + 1]).then_inc(s["q_even"], 1)
                    for u in range(SLOTS + 6):
                        if 0 <= u - 2 < SLOTS:
                            i = g * SLOTS + u - 2
                            ac.wait_ge(s["probs_turned"], ROWS + i + 1)
                            ac.wait_ge(s["heads_ready"], i + 1)
                            nc.scalar.activation(probs_t[:, u % 2, :], ps_t[u % 2][:],
                                                 ACT.Copy).then_inc(s["probs_copied"], 1)
                        if u < SLOTS:
                            i, r = g * SLOTS + u, u % ROWS
                            ac.wait_ge(s["shift_ready"], ROWS + i + 1)
                            nc.scalar.activation(shifted[:, r], shifted[:, r], ACT.Exp).then_inc(s["probs_ready"], 1)
                        b, late = divmod(u - 8, ROWS)
                        if late == 0 and 0 <= b < GB:
                            ac.wait_ge(s["mixed_turned"], 1 + g * GB + b + 1)
                            ac.wait_ge(s["out_ready"], g * GB + b + 1)
                            nc.scalar.activation(mixed_t[0][:], ps_p[:, 0:DM].rearrange("p (k t) -> p k t", k=KT),
                                                 ACT.Copy).then_inc(s["mixed_high"], 1)

            @block.vector
            def _(dve):
                chain = Chain(dve, s["chain"])
                link = chain.link
                variance(core, dve, chain, s["variance_ready"])
                if masked:
                    dve.sem_inc(s["scores_taken"], ROWS)
                dve.sem_inc(s["shift_ready"], ROWS)
                dve.sem_inc(s["mixed_ready"], 1)
                dve.sem_inc(s["x_updated"], 1)
                dve.wait_ge(s["w_loaded"], 16 * LOADS)
                nc.vector.tensor_scalar(b_scaled[:], b_q[:], HD ** -0.5, None, ALU.mult).then_inc(s["side_set"], 1)
                if masked:
                    nc.vector.tensor_scalar(keep[:], padded[:], -1.0, 1.0, ALU.mult, ALU.add)
                    nc.vector.tensor_scalar(mask[:], padded[:], NEG, None, ALU.mult).then_inc(s["mask_ready"], 1)
                    dve.wait_ge(s["mask_ready"], 1)
                    nc.vector.tensor_tensor(mask[:], mask[:], causal[:].unsqueeze(1).to_broadcast([P, TILES, SEQ]),
                                            ALU.add).then_inc(s["mask_ready"], 1)
                    dve.wait_ge(s["mask_ready"], 2)
                dve.wait_ge(s["ones_set"], 1)
                dve.wait_ge(s["scale_ready"], 1)
                with dve.Fori(0, GROUPS) as g:
                    LINKS = GB + (0 if masked else SLOTS)
                    chain.enter(g, LINKS)
                    for t in range(GB):
                        last = nc.vector.tensor_scalar(xn[:, t, :], x[:, bass.ds(g * GB + t, 1), :].squeeze(1),
                                                       core.ln[:, 0, bass.ds(g * GB + t, 1)],
                                                       core.ln[:, 3, bass.ds(g * GB + t, 1)],
                                                       ALU.subtract, ALU.mult)
                    last.then_inc(s["xn_ready"], 1)
                    for k in range(KT):
                        dve.wait_ge(s["cn_high"], KT * g + k + 1)
                        nc.vector.tensor_tensor(cnt[1][:, k, :], ps_s[k][:], cnt[0][:, k, :].bitcast(F32),
                                                ALU.subtract).then_inc(s["cn_low"], 1)
                    for k in range(KT):
                        dve.wait_ge(s["xn_high"], KT * g + k + 1)
                        nc.vector.tensor_tensor(xnt[1][:, k, :], ps_s[2 + k][:], xnt[0][:, k, :].bitcast(F32),
                                                ALU.subtract).then_inc(s["xn_low"], 1)
                    if masked:
                        for m in range(KT):
                            dve.wait_ge(s["k_ready"], KT * g + m + 1)
                            kept = keep[:, bass.ds(g * GB, GB), :].rearrange("p b t -> p (b t)")
                            nc.vector.scalar_tensor_tensor(out=k_t[:, m, :], in0=ps_t[m][:], scalar=b_k[:, m:m + 1],
                                                           in1=kept, op0=ALU.add,
                                                           op1=ALU.mult).then_inc(s["k_taken"], 1)
                    dve.wait_ge(s["q_scaled"], KT * g + KT)
                    for r in range(ROWS):
                        nc.vector.tensor_scalar(q[2 * r + 1][:], q_all[:], side[:, 2 * r + 1:2 * r + 2], None,
                                                ALU.mult).then_inc(s["q_odd"], 1)
                    for j in range(2):
                        dve.wait_ge(s["v_ready"], 2 * g + j + 1)
                        for t in (2 * j, 2 * j + 1):
                            last = nc.vector.tensor_tensor(
                                v[:, t, :, 0:HD],
                                v_banks[j][:, (t % 2) * DM:(t % 2 + 1) * DM].rearrange("p (h d) -> p h d", d=HD),
                                b_v[:].rearrange("p (h d) -> p h d", d=HD), ALU.add)
                        last.then_inc(s["v_taken"], 1)
                    for u in range(SLOTS + 8):
                        b, late = divmod(u - 7, ROWS)
                        if late == 0 and 0 <= b < GB:
                            dve.wait_ge(s["heads_ready"], 2 + g * SLOTS + ROWS * (b + 1))
                            dve.wait_ge(s["mixed_turned"], g * GB + b + 1)
                            heads = ps_o[:, 0:HEADS * VW].rearrange("p (h d) -> p h d", d=VW)
                            link(nc.vector.reciprocal(inv_sum[:], heads[:, :, HD]))
                            nc.vector.tensor_tensor(mixed[:].rearrange("p (h d) -> p h d", d=HD), heads[:, :, 0:HD],
                                                    inv_sum[:].unsqueeze(2).to_broadcast([P, HEADS, HD]),
                                                    ALU.mult).then_inc(s["mixed_ready"], 1)
                        if u < SLOTS:
                            b, r = divmod(u, ROWS)
                            i = g * SLOTS + u
                            scores = ps_s[r][:].rearrange("p (j t) -> p j t", t=SEQ)
                            peak = top[:, r].unsqueeze(2).to_broadcast([P, 4, SEQ])
                            dve.wait_ge(s["scores_ready"], i + 1)
                            if masked:
                                dve.wait_ge(s["shift_ready"], i + 1)
                                mask_b = mask[:, bass.ds(g * GB + b, 1), :].to_broadcast([P, 4, SEQ])
                                nc.vector.tensor_tensor(masked_s[:, r], scores, mask_b,
                                                        ALU.add).then_inc(s["scores_taken"], 1)
                                dve.wait_ge(s["scores_taken"], ROWS + i + 1)
                                nc.vector.tensor_reduce(top[:, r], masked_s[:, r], AX.X,
                                                        ALU.max).then_inc(s["scores_masked"], 1)
                            else:
                                link(nc.vector.tensor_reduce(top[:, r], scores, AX.X, ALU.max))
                                dve.wait_ge(s["probs_turned"], i + 1)
                                nc.vector.tensor_tensor(shifted[:, r], scores, peak,
                                                        ALU.subtract).then_inc(s["shift_ready"], 1)
                        b, late = divmod(u - 9, ROWS)
                        if late == 0 and 0 <= b < GB:
                            dve.wait_ge(s["mixed_high"], g * GB + b + 1)
                            nc.vector.tensor_tensor(mixed_t[1][:], ps_p[:, 0:DM].rearrange("p (k t) -> p k t", k=KT),
                                                    mixed_t[0][:].bitcast(F32), ALU.subtract).then_inc(s["mixed_low"], 1)
                        b, late = divmod(u - 11, ROWS)
                        if late == 0 and 0 <= b < GB:
                            xb = x[:, bass.ds(g * GB + b, 1), :].squeeze(1)
                            dve.wait_ge(s["out_ready"], 1 + g * GB + b + 1)
                            if b == 0:
                                dve.wait_ge(s["bias_added"], g + 1)
                            nc.vector.tensor_tensor(xb, xb, ps_p[:, DM:2 * DM], ALU.add).then_inc(s["x_updated"], 1)
                            dve.wait_ge(s["x_updated"], 1 + g * GB + b + 1)
                            nc.vector.bn_stats(core.stats[:, bass.ds(g * GB + b, 1), :].squeeze(1), xb)
                    chain.leave(GROUPS)
        core.retire(s)


def experts(core, w, name, shared, routed, softmax_first, final):
    nc, x, ident = core.nc, core.x, core.ident
    E, PAIRS = shared + routed, (shared + routed) // 2
    FF = w[f"{name}_W1"].shape[3]
    FT = FF // P
    STEPS = 2 * GROUPS * FT
    UP, HID, RING = 3, 3, 4
    LAG = 3
    TOP = 2

    with ExitStack() as ctx:
        def sb(n, shape, dt=F32):
            return ctx.enter_context(nc.sbuf_tensor(f"{name}_{n}", shape, dt))

        def ps(n):
            return ctx.enter_context(nc.psum_tensor(f"{name}_{n}", [P, GT], F32))

        w_r, w_r_hi, w_r_lo = (sb(f"w_r{i}", [P, KT, routed], F32R if i else F32) for i in range(3))
        b_r, b_1, b_2 = sb("b_r", [P, routed]), sb("b_1", [P, E, FT]), sb("b_2", [E, DM])
        before = sb("before", [P, routed, routed])
        raw = sb("raw_1", [P, KT, FF]), sb("raw_2", [P, FT, DM])
        w_1 = [(sb(f"w1_hi{j}", [P, KT, FF], F32R), sb(f"w1_lo{j}", [P, KT, FF], F32R)) for j in range(2)]
        w_2 = [(sb(f"w2_hi{j}", [P, FT, DM], F32R), sb(f"w2_lo{j}", [P, FT, DM], F32R)) for j in range(2)]
        zero = sb("zero", [P, 1, 1])
        b_now = sb("b_now", [P, 2, FT])
        xnt = (sb("xnt_hi", [P, KT, TILES * SEQ], F32R), sb("xnt_lo", [P, KT, TILES * SEQ], F32R))
        xn = sb("xn", [P, 1 if final else 2, GB, DM])
        y = sb("y", [P, TILES, DM]) if final else x
        hid = sb("hid", [P, HID, GT])
        hid_hi, hid_lo = sb("hid_hi", [P, RING, GT], F32R), sb("hid_lo", [P, RING, GT], F32R)
        gates = sb("gates", [P, TILES, E])
        gates_t = sb("gates_t", [E, TILES * SEQ])
        score, excess = sb("score", [P, TILES, routed]), sb("excess", [P, TILES, routed])
        rank, best = sb("rank", [P, TILES, routed]), sb("best", [P, TILES])
        above, equal = (sb(n, [P, TILES, routed, routed]) for n in ("above", "equal"))
        if final:
            gamma, beta = sb("gamma", [P, DM]), sb("beta", [P, DM])

        ps_u = [ps(f"u{i}") for i in range(UP)]
        ps_a = [[ps(f"a{i}{j}") for j in range(2)] for i in range(2)]
        ps_r = ps("r")

        names = ("small_loaded w_loaded w_high w_split router_ready variance_ready scale_ready xn_ready xn_turned xn_high "
                 "xn_low logits_ready excess_ready exp_ready gates_ready gates_turned gates_copied bias_ready "
                 "bias_taken up_ready hid_ready hid_high hid_low down_done acc_taken variance2_ready scale2_ready "
                 "bias_copied y_set chain")
        s = core.stage_sems(name + "_", names)
        SMALL = 5 + 2 * final

        def group_of(step):
            return step // (GROUPS * FT), step // FT % GROUPS, step % FT

        with nc.Block() as block:
            @block.sync
            def _(sp):
                for t, n in ((w_r, "Wr"), (b_1, "b1"), (b_2, "b2"), (before, "before")):
                    sp.dma_start(t[:], w[f"{name}_{n}"]).then_inc(s["small_loaded"], 16)
                for t, n in ((b_r, "br"),) + (((gamma, "gamma"), (beta, "beta")) if final else ()):
                    sp.dma_start(t[:], w[f"{name}_{n}"].partition_broadcast(P)).then_inc(s["small_loaded"], 16)
                with sp.Fori(0, E) as e:
                    sp.wait_ge(s["w_split"], 2 * e + 2)
                    for t, n in zip(raw, ("W1", "W2")):
                        sp.dma_start(t[:], w[f"{name}_{n}"][bass.ds(e, 1)].squeeze(0)).then_inc(s["w_loaded"], 16)

            @block.gpsimd
            def _(pool):
                pool.sem_inc(s["w_split"], 2)
                pool.wait_ge(s["small_loaded"], 16 * SMALL)
                nc.gpsimd.memset(zero[:], 0.0)
                nc.gpsimd.tensor_copy(w_r_hi[:], w_r[:]).then_inc(s["router_ready"], 1)
                pool.wait_ge(s["router_ready"], 1)
                nc.gpsimd.tensor_tensor(w_r_lo[:], w_r[:], w_r_hi[:].bitcast(F32),
                                        ALU.subtract).then_inc(s["router_ready"], 1)
                if shared:
                    nc.gpsimd.memset(gates[:, :, 0:shared], 1.0 / shared).then_inc(s["router_ready"], 1)
                inverse_deviation(core, pool, s["variance_ready"], s["scale_ready"])
                with pool.Fori(0, PAIRS) as e2:
                    for j in range(2):
                        e = 2 * e2 + j
                        pool.wait_ge(s["w_loaded"], 32 * e + 32)
                        pool.wait_ge(s["down_done"], RING + GROUPS * FT * e)
                        for i, (t, (hi, lo)) in enumerate(zip(raw, (w_1[j], w_2[j]))):
                            nc.gpsimd.tensor_tensor(hi[:], t[:], zero[:].to_broadcast(t.shape),
                                                    ALU.add).then_inc(s["w_high"], 1)
                            pool.wait_ge(s["w_high"], 2 * e + i + 1)
                            nc.gpsimd.tensor_tensor(lo[:], t[:], hi[:].bitcast(F32),
                                                    ALU.subtract).then_inc(s["w_split"], 1)
                if final:
                    inverse_deviation(core, pool, s["variance2_ready"], s["scale2_ready"])

            @block.tensor
            def _(pe):
                pe.sem_inc(s["down_done"], RING + GROUPS * FT)
                pe.wait_ge(s["router_ready"], 2 + bool(shared))
                for g in range(GROUPS):
                    pe.wait_ge(s["xn_ready"], g + 1)
                    if g:
                        pe.wait_ge(s["xn_low"], KT * g)
                    for k in range(KT):
                        for t in range(GB):
                            last = nc.tensor.transpose(ps_u[k][:, t * P:(t + 1) * P],
                                                       xn[:, g % xn.shape[1], t, k * P:(k + 1) * P], ident[:])
                        last.then_inc(s["xn_turned"], 1)
                    pe.wait_ge(s["xn_low"], KT * g + KT)
                    for t in range(GB * g, GB * g + GB):
                        for k in range(KT):
                            last = product(nc, ps_r[:, t * routed:(t + 1) * routed],
                                           [a[:, k, t * P:(t + 1) * P] for a in xnt],
                                           [a[:, k, :] for a in (w_r_hi, w_r_lo)], k == 0, k == KT - 1)
                last.then_inc(s["logits_ready"], 1)
                pe.wait_ge(s["gates_ready"], 1)
                for g in range(GROUPS):
                    for t in range(GB):
                        last = nc.tensor.transpose(ps_a[g // 2][g % 2][0:E, t * P:(t + 1) * P],
                                                   gates[:, GB * g + t, :], ident[:])
                    last.then_inc(s["gates_turned"], 1)
                for i in range(TILES // 2):
                    pe.wait_ge(s["gates_copied"], i // 2 + 1 if i % 2 == 0 else GROUPS)
                    if i == 0:
                        pe.wait_ge(s["gates_copied"], GROUPS)
                    if i >= 4:
                        pe.wait_ge(s["bias_taken"], i - 3)
                    bank = ps_a[i // 2 % 2][i % 2]
                    for t in range(2):
                        last = nc.tensor.matmul(bank[:, t * DM:(t + 1) * DM],
                                                gates_t[:, (2 * i + t) * P:(2 * i + t + 1) * P], b_2[:],
                                                start=True, stop=True)
                    last.then_inc(s["bias_ready"], 1)
                pe.wait_ge(s["bias_taken"], TILES // 2)
                with pe.Fori(0, PAIRS) as e2:
                    for n in range(STEPS + LAG):
                        if n < STEPS:
                            j, g, f = group_of(n)
                            if n % (GROUPS * FT) == 0:
                                pe.wait_ge(s["w_split"], 2 + 4 * e2 + 2 * j + 2)
                            pe.wait_ge(s["hid_ready"], e2 * STEPS + n + 1)
                            for k in range(KT):
                                last = product(nc, ps_u[n % UP][:], [a[:, k, f * P:(f + 1) * P] for a in w_1[j]],
                                               [a[:, k, g * GT:(g + 1) * GT] for a in xnt], k == 0, k == KT - 1)
                            last.then_inc(s["up_ready"], 1)
                        d = n - LAG
                        if d >= 0:
                            j, g, f = group_of(d)
                            pe.wait_ge(s["hid_low"], HID + e2 * STEPS + d + 1)
                            if f == 0:
                                pe.wait_ge(s["acc_taken"], e2 * STEPS // FT + d // FT + 1)
                            for t in range(GB):
                                out = ps_a[d // FT % 2][t // 2][:, (t % 2) * DM:(t % 2 + 1) * DM]
                                last = product(nc, out, [a[:, d % RING, t * P:(t + 1) * P] for a in (hid_hi, hid_lo)],
                                               [a[:, f, :] for a in w_2[j]], f == 0 and t % 2 == 0, f == FT - 1,
                                               skip=True)
                            last.then_inc(s["down_done"], 1)

            @block.scalar
            def _(ac):
                for g in range(GROUPS):
                    for k in range(KT):
                        ac.wait_ge(s["xn_turned"], KT * g + k + 1)
                        nc.scalar.activation(xnt[0][:, k, g * GT:(g + 1) * GT], ps_u[k][:],
                                             ACT.Copy).then_inc(s["xn_high"], 1)
                ac.wait_ge(s["excess_ready"], 1)
                nc.scalar.activation(excess[:], excess[:], ACT.Exp).then_inc(s["exp_ready"], 1)
                for g in range(GROUPS):
                    ac.wait_ge(s["gates_turned"], g + 1)
                    nc.scalar.activation(gates_t[:, g * GT:(g + 1) * GT], ps_a[g // 2][g % 2][0:E, :],
                                         ACT.Copy).then_inc(s["gates_copied"], 1)
                ac.sem_inc(s["hid_ready"], UP)
                ac.sem_inc(s["hid_high"], HID)
                nc.scalar.preload_act_table(ACT.Relu)
                with ac.Fori(0, PAIRS) as e2:
                    nc.scalar.activation(b_now[:], b_1[:, bass.ds(2 * e2, 2), :], ACT.Copy).then_inc(s["bias_copied"], 1)
                    ac.wait_ge(s["bias_copied"], e2 + 1)
                    for n in range(STEPS + 1):
                        i = e2 * STEPS + n
                        if n < STEPS:
                            j, g, f = group_of(n)
                            ac.wait_ge(s["up_ready"], i + 1)
                            ac.wait_ge(s["hid_low"], i + 1)
                            nc.scalar.activation(hid[:, n % HID, :], ps_u[n % UP][:], ACT.Relu,
                                                 bias=b_now[:, j, f:f + 1]).then_inc(s["hid_ready"], 1)
                        if n:
                            m = n - 1
                            ac.wait_ge(s["hid_ready"], UP + i)
                            ac.wait_ge(s["down_done"], GROUPS * FT + i)
                            nc.scalar.activation(hid_hi[:, m % RING, :], hid[:, m % HID, :],
                                                 ACT.Copy).then_inc(s["hid_high"], 1)

            @block.vector
            def _(dve):
                chain = Chain(dve, s["chain"])
                link = chain.link
                variance(core, dve, chain, s["variance_ready"])
                dve.wait_ge(s["scale_ready"], 1)
                for g in range(GROUPS):
                    if final and g:
                        dve.wait_ge(s["xn_turned"], KT * g)
                        dve.wait_ge(s["y_set"], g)
                    elif g >= 2:
                        dve.wait_ge(s["xn_turned"], KT * (g - 1))
                    for t in range(GB):
                        last = normalise(core, xn[:, g % xn.shape[1], t, :], GB * g + t)
                    last.then_inc(s["xn_ready"], 1)
                    if final:
                        dve.wait_ge(s["xn_ready"], g + 1)
                        nc.vector.tensor_copy(y[:, GB * g:GB * g + GB, :], xn[:, 0]).then_inc(s["y_set"], 1)
                    for k in range(KT):
                        dve.wait_ge(s["xn_high"], KT * g + k + 1)
                        cols = slice(g * GT, (g + 1) * GT)
                        nc.vector.tensor_tensor(xnt[1][:, k, cols], ps_u[k][:], xnt[0][:, k, cols].bitcast(F32),
                                                ALU.subtract).then_inc(s["xn_low"], 1)
                dve.wait_ge(s["small_loaded"], 16 * SMALL)
                dve.wait_ge(s["logits_ready"], 1)
                wide = [P, TILES, routed]
                link(nc.vector.tensor_tensor(score[:], ps_r[:, 0:TILES * routed].rearrange("p (t e) -> p t e", e=routed),
                                             b_r[:].unsqueeze(1).to_broadcast(wide), ALU.add))
                link(nc.vector.tensor_reduce(best[:], score[:], AX.X, ALU.max))
                nc.vector.tensor_tensor(excess[:], score[:], best[:].unsqueeze(2).to_broadcast(wide),
                                        ALU.subtract).then_inc(s["excess_ready"], 1)
                dve.wait_ge(s["exp_ready"], 1)
                g_out = gates[:, :, shared:E]

                def over_sum(out, value):
                    link(nc.vector.tensor_reduce(best[:], value, AX.X, ALU.add))
                    link(nc.vector.reciprocal(best[:], best[:]))
                    link(nc.vector.tensor_tensor(out, value, best[:].unsqueeze(2).to_broadcast(wide), ALU.mult))

                if softmax_first:
                    over_sum(score[:], excess[:])
                square = [P, TILES, routed, routed]
                other = score[:].unsqueeze(2).to_broadcast(square)
                own = score[:].unsqueeze(3).to_broadcast(square)
                nc.vector.tensor_tensor(above[:], other, own, ALU.is_gt)
                link(nc.vector.tensor_tensor(equal[:], other, own, ALU.is_equal))
                link(nc.vector.tensor_tensor(equal[:], equal[:], before[:].unsqueeze(1).to_broadcast(square), ALU.mult))
                link(nc.vector.tensor_tensor(above[:], above[:], equal[:], ALU.add))
                link(nc.vector.tensor_reduce(rank[:], above[:], AX.X, ALU.add))
                link(nc.vector.tensor_scalar(rank[:], rank[:], float(TOP), None, ALU.is_lt))
                if softmax_first:
                    nc.vector.tensor_tensor(g_out, rank[:], score[:], ALU.mult).then_inc(s["gates_ready"], 1)
                else:
                    link(nc.vector.tensor_tensor(excess[:], rank[:], excess[:], ALU.mult))
                    over_sum(g_out, excess[:])
                    dve.sem_inc(s["gates_ready"], 1)
                for i in range(TILES // 2):
                    dve.wait_ge(s["bias_ready"], i + 1)
                    at = y[:, 2 * i:2 * i + 2, :]
                    nc.vector.tensor_tensor(at, at, ps_a[i // 2 % 2][i % 2][:].rearrange("p (t d) -> p t d", d=DM),
                                            ALU.add).then_inc(s["bias_taken"], 1)
                dve.sem_inc(s["hid_low"], HID)
                dve.sem_inc(s["acc_taken"], 2)
                dve.wait_ge(s["bias_taken"], TILES // 2)
                ACC_AT = FT - 1 + LAG + 1
                with dve.Fori(0, PAIRS) as e2:
                    for n in range(STEPS - FT + ACC_AT + 1):
                        if n < STEPS:
                            dve.wait_ge(s["hid_high"], HID + e2 * STEPS + n + 1)
                            nc.vector.tensor_tensor(hid_lo[:, n % RING, :], hid[:, n % HID, :],
                                                    hid_hi[:, n % RING, :].bitcast(F32),
                                                    ALU.subtract).then_inc(s["hid_low"], 1)
                        if n >= ACC_AT and (n - ACC_AT) % FT == 0:
                            r = (n - ACC_AT) // FT
                            q = e2 * (STEPS // FT) + r
                            j, g, _ = group_of(r * FT)
                            dve.wait_ge(s["down_done"], RING + GROUPS * FT + FT * q + FT)
                            dve.wait_ge(s["acc_taken"], 2 + q)
                            for t in range(GB):
                                yt = y[:, g * GB + t, :]
                                last = nc.vector.scalar_tensor_tensor(
                                    out=yt, in0=ps_a[r % 2][t // 2][:, (t % 2) * DM:(t % 2 + 1) * DM],
                                    scalar=gates[:, g * GB + t, bass.ds(2 * e2 + j, 1)], in1=yt,
                                    op0=ALU.mult, op1=ALU.add)
                            last.then_inc(s["acc_taken"], 1)
                dve.wait_ge(s["acc_taken"], 2 + PAIRS * STEPS // FT)
                for t in range(TILES):
                    last = nc.vector.bn_stats(core.stats[:, t, :], y[:, t, :])
                if final:
                    link(last)
                    variance(core, dve, chain, s["variance2_ready"])
                    dve.wait_ge(s["scale2_ready"], 1)
                    for t in range(TILES):
                        last = nc.vector.tensor_scalar(y[:, t, :], y[:, t, :], core.ln[:, 0, t:t + 1],
                                                       core.ln[:, 3, t:t + 1], ALU.subtract, ALU.mult)
                    link(last)
                    full = [P, TILES, DM]
                    link(nc.vector.tensor_tensor(y[:], y[:], gamma[:].unsqueeze(1).to_broadcast(full), ALU.mult))
                    link(nc.vector.tensor_tensor(y[:], y[:], beta[:].unsqueeze(1).to_broadcast(full), ALU.add))
                    nc.vector.tensor_tensor(x[:], x[:], y[:], ALU.add)
        core.retire(s)


def self_attention(core, w):
    nc, x, ident = core.nc, core.x, core.ident
    HEADS, HD = 8, 64
    INNER = HEADS * HD
    SIDES = P // HD
    JT = INNER // P
    VW = HD + 1
    SCALE = 16.0
    LEAST_NORM, LEAST_SUM = 1e-12, 1e-6
    RING = 4

    with ExitStack() as ctx:
        def sb(n, shape, dt=F32):
            return ctx.enter_context(nc.sbuf_tensor(f"a_{n}", shape, dt))

        def ps(n):
            return ctx.enter_context(nc.psum_tensor(f"a_ps_{n}", [P, GT], F32))

        raw = [sb("w_q", [P, KT, INNER]), sb("w_kv", [P, KT, 2 * INNER]), sb("w_o", [P, JT, DM])]
        split = [(sb(f"hi{i}", t.shape, F32R), sb(f"lo{i}", t.shape, F32R)) for i, t in enumerate(raw)]
        s_q, s_kv, s_o = split
        minus_half = sb("minus_half", [P, 2 * HEADS])
        less_scale = sb("less_scale", [P, 1])
        xn = sb("xn", [P, RING, DM])
        xnt = (sb("xnt_hi", [P, KT, SEQ], F32R), sb("xnt_lo", [P, KT, SEQ], F32R))
        qk = sb("qk", [P, RING, 2, INNER])
        squares = sb("squares", [P, 2, INNER])
        norm = sb("norm", [P, RING, 2 * HEADS])
        v = sb("v", [P, RING, HEADS, VW])
        q_t, k_t = sb("q_t", [P, JT, SEQ]), sb("k_t", [P, JT, SEQ])
        probs = sb("probs", [P, SIDES, JT * SEQ])
        inv_sum = sb("inv_sum", [P, SIDES, JT])
        mixed = sb("mixed", [P, INNER])
        mixed_t = (sb("mixed_hi", [P, JT, SEQ], F32R), sb("mixed_lo", [P, JT, SEQ], F32R))

        ps_q, ps_k = ps("q"), ps("k")
        ps_v = ps("v")
        ps_x = ps("x")
        ps_s, ps_o = ([ps(f"{n}{i}") for i in range(2)] for n in "so")

        names = ("w_loaded w_high w_low consts_set variance_ready scale_ready xn_ready xn_turned xn_high xn_low "
                 "q_ready k_ready v_ready q_copied k_copied v_copied squares_ready squares_summed norm_ready unit_ready "
                 "q_turned k_turned qt_ready kt_ready scores_ready probs_ready heads_ready mixed_ready mixed_turned "
                 "mixed_high mixed_low out_ready x_updated chain")
        s = core.stage_sems("a_", names)

        FIRST, PEELED, LAST = -2, 1, TILES + 1
        LOOPS = (TILES - 4) // RING

        def turns(engine, step, chain=None, links=0):
            def plain(t):
                step(t, t % RING, lambda n: 0 <= t + n < TILES)

            for t in range(FIRST, PEELED):
                plain(t)
            with engine.Fori(0, LOOPS) as g:
                if chain:
                    chain.enter(g, RING * links)
                for i in range(RING):
                    step(g * RING + PEELED + i, (PEELED + i) % RING, lambda n: True)
                if chain:
                    chain.leave(LOOPS)
            for t in range(PEELED + LOOPS * RING, LAST):
                plain(t)

        with nc.Block() as block:
            @block.sync
            def _(sp):
                for t, n in zip(raw, ("Wq", "Wkv", "Wo")):
                    sp.dma_start(t[:], w[f"a_{n}"]).then_inc(s["w_loaded"], 16)

            @block.gpsimd
            def _(pool):
                nc.gpsimd.memset(v[:, :, :, HD:VW], 1.0)
                nc.gpsimd.memset(less_scale[:], -SCALE)
                nc.gpsimd.memset(minus_half[:], -0.5).then_inc(s["consts_set"], 1)
                inverse_deviation(core, pool, s["variance_ready"], s["scale_ready"])
                pool.wait_ge(s["w_loaded"], 16 * len(raw))
                for i, (t, (hi, lo)) in enumerate(zip(raw, split)):
                    pool.wait_ge(s["w_high"], i + 1)
                    nc.gpsimd.tensor_tensor(lo[:], t[:], hi[:].bitcast(F32), ALU.subtract).then_inc(s["w_low"], 1)
                pool.wait_ge(s["consts_set"], 1)

                def step(t, at, on):
                    if on(1):
                        pool.wait_ge(s["squares_summed"], t + 2)
                        n = norm[:, (at + 1) % RING, :]
                        nc.gpsimd.tensor_tensor(n, n, minus_half[:], ALU.pow).then_inc(s["norm_ready"], 1)
                    if on(2):
                        pool.wait_ge(s["q_copied"], t + 3)
                        pool.wait_ge(s["k_copied"], t + 3)
                        qk_at = qk[:, (at + 2) % RING]
                        nc.gpsimd.tensor_tensor(squares[:], qk_at, qk_at, ALU.mult).then_inc(s["squares_ready"], 1)

                turns(pool, step)

            @block.tensor
            def _(pe):
                pe.wait_ge(s["w_low"], len(raw))
                pe.wait_ge(s["consts_set"], 1)

                def step(t, at, on):
                    if on(0):
                        pe.wait_ge(s["unit_ready"], t + 1)
                        if on(1):
                            pe.wait_ge(s["q_copied"], t + 2)
                            pe.wait_ge(s["k_copied"], t + 2)
                        for c in range(JT):
                            last = nc.tensor.transpose(ps_q[:, c * SEQ:(c + 1) * SEQ],
                                                       qk[:, at, 0, c * P:(c + 1) * P], ident[:])
                        last.then_inc(s["q_turned"], 1)
                        for c in range(JT):
                            last = nc.tensor.transpose(ps_k[:, c * SEQ:(c + 1) * SEQ],
                                                       qk[:, at, 1, c * P:(c + 1) * P], ident[:])
                        last.then_inc(s["k_turned"], 1)
                    if on(-1):
                        pe.wait_ge(s["mixed_ready"], t)
                        if on(1):
                            pe.wait_ge(s["v_copied"], t + 2)
                        for c in range(JT):
                            last = nc.tensor.transpose(ps_v[:, c * SEQ:(c + 1) * SEQ],
                                                       mixed[:, c * P:(c + 1) * P], ident[:])
                        last.then_inc(s["mixed_turned"], 1)
                    if on(2):
                        pe.wait_ge(s["xn_ready"], t + 3)
                        if on(-1):
                            pe.wait_ge(s["x_updated"], t)
                        for k in range(KT):
                            last = nc.tensor.transpose(ps_x[:, k * P:(k + 1) * P],
                                                       xn[:, (at + 2) % RING, k * P:(k + 1) * P], ident[:])
                        last.then_inc(s["xn_turned"], 1)
                    if on(0):
                        pe.wait_ge(s["qt_ready"], t + 1)
                        pe.wait_ge(s["kt_ready"], t + 1)
                        for o in range(SIDES):
                            part = slice(o * HD, (o + 1) * HD)
                            for c in range(JT):
                                last = nc.tensor.matmul(ps_s[o][:, c * SEQ:(c + 1) * SEQ], k_t[part, c, :],
                                                        q_t[part, c, :], start=True, stop=True)
                            last.then_inc(s["scores_ready"], 1)
                    if on(2):
                        pe.wait_ge(s["xn_low"], t + 3)
                    if on(-1):
                        pe.wait_ge(s["mixed_low"], t)
                        for c in range(JT):
                            last = product(nc, ps_x[:, DM:2 * DM], [a[:, c, :] for a in mixed_t],
                                           [a[:, c, :] for a in s_o], c == 0, c == JT - 1)
                        last.then_inc(s["out_ready"], 1)
                    if on(2):
                        for bank, weights, ready in ((ps_q, [a[:] for a in s_q], "q_ready"),
                                                     (ps_k, [a[:, :, 0:INNER] for a in s_kv], "k_ready"),
                                                     (ps_v, [a[:, :, INNER:] for a in s_kv], "v_ready")):
                            for k in range(KT):
                                last = product(nc, bank[:], [a[:, k, :] for a in xnt], [a[:, k, :] for a in weights],
                                               k == 0, k == KT - 1)
                            last.then_inc(s[ready], 1)
                    if on(0):
                        for o in range(SIDES):
                            pe.wait_ge(s["probs_ready"], SIDES * t + o + 1)
                            for c in range(JT):
                                last = nc.tensor.matmul(ps_o[o][:, c * VW:(c + 1) * VW],
                                                        probs[:, o, c * SEQ:(c + 1) * SEQ],
                                                        v[:, at, SIDES * c + o, :], start=True, stop=True)
                        last.then_inc(s["heads_ready"], 1)

                turns(pe, step)

            @block.scalar
            def _(ac):
                ac.wait_ge(s["w_loaded"], 16 * len(raw))
                for i, (t, (hi, lo)) in enumerate(zip(raw, split)):
                    nc.scalar.activation(hi[:], t[:], ACT.Copy).then_inc(s["w_high"], 1)
                nc.scalar.preload_act_table(ACT.Exp)

                def step(t, at, on):
                    if on(0):
                        ac.wait_ge(s["q_turned"], t + 1)
                        nc.scalar.activation(q_t[:].rearrange("p c t -> p (c t)"), ps_q[:],
                                             ACT.Copy).then_inc(s["qt_ready"], 1)
                    if on(-1):
                        ac.wait_ge(s["mixed_turned"], t)
                        nc.scalar.activation(mixed_t[0][:].rearrange("p c t -> p (c t)"), ps_v[:],
                                             ACT.Copy).then_inc(s["mixed_high"], 1)
                    if on(2):
                        ac.wait_ge(s["xn_turned"], t + 3)
                        nc.scalar.activation(xnt[0][:].rearrange("p k t -> p (k t)"), ps_x[:, 0:DM],
                                             ACT.Copy).then_inc(s["xn_high"], 1)
                    if on(0):
                        if on(-1):
                            ac.wait_ge(s["heads_ready"], t)
                        for o in range(SIDES):
                            ac.wait_ge(s["scores_ready"], SIDES * t + o + 1)
                            nc.scalar.activation(probs[:, o, :], ps_s[o][:], ACT.Exp, bias=less_scale[:, 0:1],
                                                 scale=SCALE).then_inc(s["probs_ready"], 1)
                    if on(2):
                        ac.wait_ge(s["q_ready"], t + 3)
                        nc.scalar.activation(qk[:, (at + 2) % RING, 0, :], ps_q[:], ACT.Copy).then_inc(s["q_copied"], 1)
                        ac.wait_ge(s["k_ready"], t + 3)
                        nc.scalar.activation(qk[:, (at + 2) % RING, 1, :], ps_k[:], ACT.Copy).then_inc(s["k_copied"], 1)

                turns(ac, step)

            @block.vector
            def _(dve):
                chain = Chain(dve, s["chain"])
                link = chain.link
                variance(core, dve, chain, s["variance_ready"])
                dve.wait_ge(s["consts_set"], 1)
                dve.wait_ge(s["scale_ready"], 1)

                def entry(a, j):
                    return a[:, bass.ds(j, 1), :].squeeze(1)

                def layer_norm(j, at):
                    nc.vector.tensor_scalar(xn[:, at % RING, :], entry(x, j), core.ln[:, 0, bass.ds(j, 1)],
                                            core.ln[:, 3, bass.ds(j, 1)], ALU.subtract,
                                            ALU.mult).then_inc(s["xn_ready"], 1)

                layer_norm(0, 0)
                dve.sem_inc(s["x_updated"], 1)

                def step(t, at, on):
                    if on(0):
                        dve.wait_ge(s["k_turned"], t + 1)
                        nc.vector.tensor_copy(k_t[:].rearrange("p c t -> p (c t)"), ps_k[:]).then_inc(s["kt_ready"], 1)
                    if on(-1):
                        dve.wait_ge(s["mixed_high"], t)
                        nc.vector.tensor_tensor(mixed_t[1][:].rearrange("p c t -> p (c t)"), ps_v[:],
                                                mixed_t[0][:].rearrange("p c t -> p (c t)").bitcast(F32),
                                                ALU.subtract).then_inc(s["mixed_low"], 1)
                    if on(2):
                        dve.wait_ge(s["xn_high"], t + 3)
                        nc.vector.tensor_tensor(xnt[1][:].rearrange("p k t -> p (k t)"), ps_x[:, 0:DM],
                                                xnt[0][:].rearrange("p k t -> p (k t)").bitcast(F32),
                                                ALU.subtract).then_inc(s["xn_low"], 1)
                    if on(1):
                        n = norm[:, (at + 1) % RING, :]
                        dve.wait_ge(s["squares_ready"], t + 2)
                        link(nc.vector.tensor_reduce(n, squares[:].rearrange("p a (h d) -> p (a h) d", d=HD),
                                                     AX.X, ALU.add))
                        nc.vector.tensor_scalar(n, n, LEAST_NORM ** 2, None, ALU.max).then_inc(s["squares_summed"], 1)
                    if on(3):
                        layer_norm(t + 3, at + 3)
                    if on(-1):
                        xb = entry(x, t - 1)
                        dve.wait_ge(s["out_ready"], t)
                        nc.vector.tensor_tensor(xb, xb, ps_x[:, DM:2 * DM], ALU.add).then_inc(s["x_updated"], 1)
                        dve.wait_ge(s["x_updated"], t + 1)
                        nc.vector.bn_stats(entry(core.stats, t - 1), xb)
                    if on(1):
                        dve.wait_ge(s["norm_ready"], t + 2)
                        qk_at = qk[:, (at + 1) % RING].rearrange("p a (h d) -> p (a h) d", d=HD)
                        nc.vector.tensor_tensor(qk_at, qk_at, norm[:, (at + 1) % RING].unsqueeze(2)
                                                .to_broadcast([P, 2 * HEADS, HD]), ALU.mult).then_inc(s["unit_ready"], 1)
                    if on(2):
                        dve.wait_ge(s["v_ready"], t + 3)
                        nc.vector.tensor_copy(v[:, (at + 2) % RING, :, 0:HD],
                                              ps_v[:].rearrange("p (h d) -> p h d", d=HD)).then_inc(s["v_copied"], 1)
                    if on(0):
                        dve.wait_ge(s["heads_ready"], t + 1)
                        for o in range(SIDES):
                            sums = ps_o[o][:, 0:JT * VW].rearrange("p (c d) -> p c d", d=VW)[:, :, HD]
                            last = nc.vector.tensor_scalar(inv_sum[:, o, :], sums, LEAST_SUM, None, ALU.max)
                        link(last)
                        link(nc.vector.reciprocal(inv_sum[:], inv_sum[:]))
                        for o in range(SIDES):
                            last = nc.vector.tensor_tensor(
                                mixed[:].rearrange("p (c o d) -> p c o d", o=SIDES, d=HD)[:, :, o, :],
                                ps_o[o][:, 0:JT * VW].rearrange("p (c d) -> p c d", d=VW)[:, :, 0:HD],
                                inv_sum[:, o, :].unsqueeze(2).to_broadcast([P, JT, HD]), ALU.mult)
                        last.then_inc(s["mixed_ready"], 1)

                turns(dve, step, chain, 3)
        core.retire(s)


def as_is(a):
    return a


def rows(a):
    return a.reshape(-1, P, *a.shape[1:]).swapaxes(0, 1)


def turned(a):
    return rows(a.T)


def cross_layout(name, prefix, underscore):
    at = {f"{name}_W{c}": (f"{prefix}_W{underscore}{c}", turned) for c in "qkvo"}
    at |= {f"{name}_b{c}": (f"{prefix}_b{underscore}{c}", rows) for c in "qk"}
    return at | {f"{name}_b{c}": (f"{prefix}_b{underscore}{c}", as_is) for c in "vo"}


def stacked(a):
    return a.reshape(a.shape[0], -1, P, a.shape[2]).swapaxes(1, 2)


def joined(lay):
    return lambda a, b: lay(np.concatenate([a, b]))


LAYOUT = {
    "x": ("x", lambda a: a.swapaxes(0, 1)),
    "W_in": ("L0_attn_W_in", rows),
    "conv_w": ("L0_attn_conv_w", lambda a: rows(a[:, 0])),
    "W_B": ("L0_attn_W_B", rows),
    "W_C": ("L0_attn_W_C", rows),
    "W_delta": ("L0_attn_W_delta", rows),
    "delta_base": ("L0_attn_delta_base", rows),
    "W_tau": ("L0_attn_W_tau", rows),
    "A_log": ("L0_attn_A_log", rows),
    "W_out": ("L0_attn_W_out", rows),
    "context": ("ctx_1024", lambda a: a.swapaxes(0, 1)),
    "causal": ("mask_SxS2_fk0", as_is),
    "padding": ("mask_BxS2_bf0", as_is),
    **cross_layout("x0", "L0_xattn", ""),
    **cross_layout("x1", "L1_xattn", "_"),
    "a_Wq": ("L1_attn_Wq", rows),
    "a_Wkv": ("L1_attn_Wkv", rows),
    "a_Wo": ("L1_attn_Wo", rows),
    "e0_Wr": ("L0_ffn_gate_w", rows),
    "e0_br": ("L0_ffn_gate_b", as_is),
    "e0_W1": (("L0_ffn_sw1", "L0_ffn_rw1"), joined(stacked)),
    "e0_b1": (("L0_ffn_sb1", "L0_ffn_rb1"), joined(lambda a: a.reshape(len(a), -1, P).transpose(2, 0, 1))),
    "e0_W2": (("L0_ffn_sw2", "L0_ffn_rw2"), joined(stacked)),
    "e0_b2": (("L0_ffn_sb2", "L0_ffn_rb2"), joined(as_is)),
    "e1_Wr": ("L1_ffn_Wr", turned),
    "e1_br": ("L1_ffn_br", as_is),
    "e1_W1": ("L1_ffn_W1", lambda a: stacked(a.swapaxes(1, 2))),
    "e1_b1": ("L1_ffn_b1", lambda a: a.reshape(len(a), -1, P).transpose(2, 0, 1)),
    "e1_W2": ("L1_ffn_W2", lambda a: stacked(a.swapaxes(1, 2))),
    "e1_b2": ("L1_ffn_b2", as_is),
    "e1_gamma": ("L1_ffn_gamma", as_is),
    "e1_beta": ("L1_ffn_beta", as_is),
}


def constants():
    at = {"side": np.kron(np.eye(P // 16), np.ones((16, 1))).astype(np.float32)}
    for name, n in (("e0", 4), ("e1", 8)):
        at[f"{name}_before"] = np.broadcast_to(np.tril(np.ones((n, n), np.float32), -1), (P, n, n))
    return at


def decoder(nc, w, out):
    with ExitStack() as ctx:
        core = Core(nc, ctx)
        core.x = core.keep("x_stream", [P, TILES, DM])
        core.stats = core.keep("stats", [P, TILES, 6])
        core.ln = core.keep("ln", [P, 4, TILES])
        core.minus_half = core.keep("minus_half", [P, TILES])
        core.ident = core.keep("ident", [P, P])
        load(core, w)
        state_space(core, w)
        cross_attention(core, w, "x0", masked=False)
        experts(core, w, "e0", shared=2, routed=4, softmax_first=True, final=False)
        self_attention(core, w)
        cross_attention(core, w, "x1", masked=True)
        experts(core, w, "e1", shared=0, routed=8, softmax_first=False, final=True)
        store(core, out)


def store(core, out):
    nc, stored = core.nc, core.sem("stored")
    with nc.Block() as block:
        @block.sync
        def _(sp):
            sp.dma_start(out, core.x[:]).then_inc(stored, 16)
            sp.wait_ge(stored, 16)


def kernel(**inputs):
    import concourse.bacc as bacc
    from concourse.bass_utils import run_bass_kernel_spmd

    nc = bacc.Bacc("TRN2", target_bir_lowering=False, num_devices=1)
    arrays, w = {}, {}
    for name, (source, lay) in LAYOUT.items():
        sources = (source,) if isinstance(source, str) else source
        arrays[name] = lay(*(np.asarray(inputs[n]) for n in sources))
    arrays = {"in_" + n: np.ascontiguousarray(a) for n, a in (arrays | constants()).items()}
    for name, a in arrays.items():
        w[name[3:]] = nc.dram_tensor(name, a.shape, mybir.dt.from_np(a.dtype), kind="ExternalInput").ap()
    out = nc.dram_tensor("out", (SEQ, BATCH, DM), F32, kind="ExternalOutput").ap()
    decoder(nc, w, out)
    r = run_bass_kernel_spmd(nc, [arrays], core_ids=[0])
    return r.results[0]["out"].swapaxes(0, 1)
```

```python
from contextlib import ExitStack

import numpy as np

import concourse.bass as bass
from concourse import mybir

ALU = mybir.AluOpType
ACT = mybir.ActivationFunctionType
AX = mybir.AxisListType
F32 = mybir.dt.float32
F32R = mybir.dt.float32r
BF16 = mybir.dt.bfloat16
U8 = mybir.dt.uint8
U32 = mybir.dt.uint32

P = 128
BATCH, SEQ, DM = 16, 128, 256
TILES = BATCH
KT = DM // P
GB = 4
GROUPS = TILES // GB
GT = GB * SEQ
LN_EPS = 1e-5


class Chain:

    def __init__(self, engine, sem):
        self.engine, self.sem = engine, sem
        self.done, self.base, self.inside = 0, 0, None

    def link(self, instruction):
        instruction.then_inc(self.sem, 1)
        self.done += 1
        self.engine.wait_ge(self.sem, self.base + self.done)

    def enter(self, turn, links):
        self.before, self.links = self.done, links
        self.base, self.done = turn * links + self.before, 0

    def leave(self, turns):
        assert self.done == self.links, (self.done, self.links)
        self.base, self.done = 0, self.before + turns * self.links


class Core:

    def __init__(self, nc, ctx):
        self.nc, self.ctx = nc, ctx

    def sem(self, name):
        return self.ctx.enter_context(self.nc.semaphore(name))

    def stage_sems(self, prefix, names):
        return {n: self.nc.alloc_semaphore(prefix + n) for n in names.split()}

    def retire(self, sems):
        nc, handles = self.nc, list(sems.values())
        numbers = sorted(h.num for h in handles)
        with nc.Block() as block:
            @block.sync
            def _(sp):
                at = 0
                while at < len(numbers):
                    end = at
                    while end + 1 < len(numbers) and numbers[end + 1] == numbers[end] + 1:
                        end += 1
                    sp.sem_clear(range(numbers[at], numbers[end] + 1))
                    at = end + 1
        for h in handles:
            nc.release_semaphore(h)

    def keep(self, name, shape, dt=F32):
        return self.ctx.enter_context(self.nc.sbuf_tensor(name, shape, dt))


def product(nc, out, lhs, rhs, first, last, skip=False):
    (lh, ll), (rh, rl) = lhs, rhs
    nc.tensor.matmul(out, lh, rl, start=first, stop=False, skip_group_check=skip)
    nc.tensor.matmul(out, ll, rh, start=False, stop=False, skip_group_check=skip)
    return nc.tensor.matmul(out, lh, rh, start=False, stop=last, skip_group_check=skip)


def variance(core, dve, chain, variance_ready, tiles=slice(0, TILES)):
    nc, st = core.nc, core.stats[:, tiles, :]
    mean, var, diff = (core.ln[:, i, tiles] for i in range(3))
    nc.vector.tensor_tensor(diff, st[:, :, 1], st[:, :, 4], ALU.subtract)
    nc.vector.tensor_tensor(mean, st[:, :, 1], st[:, :, 4], ALU.add)
    chain.link(nc.vector.tensor_tensor(var, st[:, :, 2], st[:, :, 5], ALU.add))
    nc.vector.tensor_scalar(mean, mean, 0.5, None, ALU.mult)
    nc.vector.tensor_scalar(var, var, 1.0 / DM, LN_EPS, ALU.mult, ALU.add)
    chain.link(nc.vector.tensor_tensor(diff, diff, diff, ALU.mult))
    nc.vector.scalar_tensor_tensor(out=var, in0=diff, scalar=0.25, in1=var,
                                   op0=ALU.mult, op1=ALU.add).then_inc(variance_ready, 1)


def inverse_deviation(core, pool, variance_ready, scale_ready, parts=((0, GB), (GB, TILES)), count=1):
    pool.wait_ge(variance_ready, count)
    for start, end in parts:
        core.nc.gpsimd.tensor_tensor(core.ln[:, 3, start:end], core.ln[:, 1, start:end],
                                     core.minus_half[:, start:end], ALU.pow).then_inc(scale_ready, 1)


def split_low(core, dve, raw, split, w_high, w_low):
    for i, (whole, (high, low)) in enumerate(zip(raw, split)):
        dve.wait_ge(w_high, i + 1)
        core.nc.vector.tensor_tensor(low[:], whole, high[:].bitcast(F32), ALU.subtract).then_inc(w_low, 1)


def normalise(core, out, tile):
    return core.nc.vector.tensor_scalar(out, core.x[:, tile, :], core.ln[:, 0, tile:tile + 1],
                                        core.ln[:, 3, tile:tile + 1], ALU.subtract, ALU.mult)


def clear_blocks(core, sp):
    rows = core.sorted_in.rearrange("(b p) d -> p b d", p=P)
    sp.dma_start(rows, core.zeros[:].unsqueeze(1).to_broadcast([P, rows.shape[1], DM])).then_inc(core.blocks_cleared, 16)


def load(core, w):
    nc = core.nc
    x_in, st = core.sem("x_in"), core.stats
    ident_set = core.sem("ident_set")
    with nc.Block() as block:
        @block.sync
        def _(sp):
            sp.dma_start(core.x[:], w["x"]).then_inc(x_in, 16)

        @block.gpsimd
        def _(pool):
            nc.gpsimd.memset(core.minus_half[:], -0.5)
            nc.gpsimd.memset(core.zeros[:], 0.0)
            nc.gpsimd.memset(core.ident[:], 0.0).then_inc(ident_set, 1)
            pool.wait_ge(ident_set, 1)
            nc.gpsimd.affine_select(out=core.ident[:], in_=core.ident[:], compare_op=ALU.not_equal,
                                    fill=1.0, base=0, pattern=[[-1, P]], channel_multiplier=1)

        @block.vector
        def _(dve):
            dve.wait_ge(x_in, 16)
            for t in range(TILES):
                nc.vector.bn_stats(st[:, t, :], core.x[:, t, :])


def state_space(core, w):
    nc, x, ident = core.nc, core.x, core.ident
    STATE = w["A_log"].shape[2]
    PAIRS = STATE // 2
    PAD = SEQ + 2
    EPS_DA = 1e-6
    LEAST_A = -1e16

    with ExitStack() as ctx:
        def sb(name, shape, dt=F32):
            return ctx.enter_context(nc.sbuf_tensor("m_" + name, shape, dt))

        def ps(name, shape):
            return ctx.enter_context(nc.psum_tensor("m_" + name, shape, F32))

        em = sb("em", [P, 2, 2, KT, GT])
        decay = sb("decay", [P, 2, 2, KT, GT])
        w_in = em[:, 0, 0]
        w_delta, w_tau = decay[:, 0, 0, :, 0:DM], decay[:, 0, 0, :, DM:2 * DM]
        w_out, w_bc = decay[:, 0, 1, :, 0:DM], decay[:, 0, 1, :, DM:DM + P]
        raw = [w_in, w_bc, w_delta, w_tau, w_out]
        split = [(sb(f"hi{i}", t.shape, F32R), sb(f"lo{i}", t.shape, F32R)) for i, t in enumerate(raw)]
        s_in, s_bc, s_delta, s_tau, s_out = split
        conv = sb("conv", [P, KT, 3])
        base = sb("base", [P, KT])
        a_log = sb("a_log", [P, KT, STATE])
        rate = sb("rate", [P, KT, STATE])
        half_rate = sb("half_rate", [P, KT, STATE])
        rate_kept = sb("rate_kept", [P, KT, STATE])
        pick = sb("pick", [2 * 2 * STATE, 2 * STATE])
        pick_r = sb("pick_r", [2 * 2 * STATE, 2 * STATE], F32R)

        xnt = (sb("xnt_hi", [P, KT, GT], F32R), sb("xnt_lo", [P, KT, GT], F32R))
        padded = sb("padded", [P, KT, GB, PAD])
        inner = padded[:, :, :, 1:SEQ + 1]
        half_v = sb("half_v", [P, KT, GT])
        tanh_v = sb("tanh_v", [P, KT, GT])
        u = sb("u", [P, KT, GT])
        half_g, tanh_g = sb("half_g", [P, KT, GT]), sb("tanh_g", [P, KT, GT])
        gate = sb("gate", [P, KT, GT])
        act = (sb("act_hi", [P, KT, GT], F32R), sb("act_lo", [P, KT, GT], F32R))
        bc_sum = sb("bc_sum", [4 * STATE, GT])
        bc = sb("bc", [4 * STATE, GT], F32R)
        delta = sb("delta", [P, KT, GT])
        du = sb("du", [P, KT, GT])
        y = sb("y", [P, KT, GT])
        xn = y[:].rearrange("p k (b d) -> p (k b) d", d=DM)
        den = sb("den", [P, 2, 2, KT, GT])
        inv_pair = sb("inv_pair", [P, 2, KT, GT])
        mult_pair = sb("mult_pair", [P, 2, KT, GT])
        wb = sb("wb", [P, 2, KT, GT])
        h = sb("h", [P, 2, 2, KT, GT])
        bcs = sb("bcs", [P, 2, 2, 2, GT])

        ps_y = [ps(f"y{i}", [P, GT]) for i in range(2)]
        ps_z = [ps(f"z{i}", [P, GT]) for i in range(2)]
        ps_b = [ps(f"b{i}", [P, GT]) for i in range(4)]

        names = ("w_loaded w_high w_low small_set pick_ready rate_exp rate_set variance_ready scale_ready "
                 "xn_ready xnt_moved xnt_high xnt_low xn_added z_ready z_taken conv_ready tanh_ready u_ready "
                 "u_high u_low bc_ready bc_taken bc_high bc_low z1_ready z1_high z1_low z2_ready exp_ready "
                 "one_plus_ready ln_ready delta_ready b_spread c_spread b_taken c_taken den_ready pair_ready pair_inverted "
                 "weighing_b em_ready outputs_added weighted_b input_ready state_ready weighted_c gate_ready y_ready "
                 "y_high y_low out_ready x_updated act_chain chain")
        s = core.stage_sems("m_", names)
        FRONT = 3

        def run(engine, front, slot, close, chain=None, links=0):
            front(0)
            for p in range(FRONT):
                slot(0, p, False, True)
            with engine.Fori(0, GROUPS - 1) as g:
                if chain:
                    chain.enter(g, links)
                for p in range(FRONT, PAIRS):
                    slot(g, p, True, True)
                for p in range(FRONT):
                    slot(g + 1, p, True, True)
                if chain:
                    chain.leave(GROUPS - 1)
            for p in range(FRONT, PAIRS):
                slot(GROUPS - 1, p, True, False)
            close()

        with nc.Block() as block:
            @block.sync
            def _(sp):
                sp.dma_start(w_in, w["W_in"]).then_inc(s["w_loaded"], 16)
                sp.dma_start(conv[:], w["conv_w"]).then_inc(s["w_loaded"], 16)
                for r in range(2):
                    for j, name in enumerate(("W_B", "W_C")):
                        at = (2 * r + j) * STATE
                        sp.dma_start(w_bc[:, :, at:at + STATE],
                                     w[name]).then_inc(s["w_loaded"], 16)
                sp.dma_start(w_delta, w["W_delta"]).then_inc(s["w_loaded"], 16)
                sp.dma_start(w_tau, w["W_tau"]).then_inc(s["w_loaded"], 16)
                sp.dma_start(w_out, w["W_out"]).then_inc(s["w_loaded"], 16)
                sp.dma_start(base[:], w["delta_base"]).then_inc(s["w_loaded"], 16)
                sp.dma_start(a_log[:], w["A_log"]).then_inc(s["w_loaded"], 16)
            LOADS = 11

            @block.gpsimd
            def _(pool):
                nc.gpsimd.memset(w_bc[:, :, 4 * STATE:], 0.0).then_inc(s["small_set"], 1)
                nc.gpsimd.memset(padded[:, :, :, 0:PAD:PAD - 1], 0.0).then_inc(s["small_set"], 1)
                nc.gpsimd.memset(pick[:], 0.0).then_inc(s["small_set"], 1)
                pool.wait_ge(s["small_set"], 3)
                for half in range(2):
                    at = pick[:]
                    nc.gpsimd.affine_select(out=at, in_=at, compare_op=ALU.not_equal, fill=1.0,
                                            base=-2 * STATE * half, pattern=[[-1, 2 * STATE]],
                                            channel_multiplier=1).then_inc(s["pick_ready"], 1)
                    pool.wait_ge(s["pick_ready"], half + 1)
                inverse_deviation(core, pool, s["variance_ready"], s["scale_ready"])
                pool.sem_inc(s["weighing_b"], 4)
                pool.sem_inc(s["weighted_b"], 4)
                pool.sem_inc(s["weighted_c"], 2)

                def front(g):
                    pool.wait_ge(s["xn_ready"], g + 1)
                    xg = x[:, bass.ds(g * GB, GB), :]
                    nc.gpsimd.tensor_tensor(xg, xg, xn, ALU.add).then_inc(s["xn_added"], 1)

                def weigh_c(i, parity):
                    pool.wait_ge(s["state_ready"], 2 + i + 1)
                    pool.wait_ge(s["c_taken"], 1 + i + 1)
                    for k in range(2):
                        c_all = bcs[:, parity, 1, k, :].unsqueeze(1).to_broadcast([P, KT, GT])
                        last = nc.gpsimd.tensor_tensor(h[:, parity, k], h[:, parity, k], c_all, ALU.mult)
                    last.then_inc(s["weighted_c"], 1)

                def multiply(i, parity):
                    pool.wait_ge(s["den_ready"], i + 1)
                    nc.gpsimd.tensor_tensor(mult_pair[:, parity], den[:, parity, 0], den[:, parity, 1],
                                            ALU.mult).then_inc(s["pair_ready"], 1)

                def slot(g, p, before, after):
                    i = g * PAIRS + p
                    if p == 0 and not before:
                        multiply(0, 0)
                    if p + 1 < PAIRS:
                        multiply(i + 1, (p + 1) % 2)
                    pool.wait_ge(s["b_taken"], 1 + i + 1)
                    pool.wait_ge(s["pair_inverted"], i + 1)
                    pool.wait_ge(s["input_ready"], i + 1)
                    for k in range(2):
                        b_all = bcs[:, p % 2, 0, k, :].unsqueeze(1).to_broadcast([P, KT, GT])
                        nc.gpsimd.tensor_tensor(wb[:, k], inv_pair[:, p % 2], b_all,
                                                ALU.mult).then_inc(s["weighing_b"], 1)
                    pool.wait_ge(s["weighing_b"], 4 + 2 * i + 2)
                    for k in range(2):
                        nc.gpsimd.tensor_tensor(wb[:, k], wb[:, k], den[:, p % 2, 1 - k],
                                                ALU.mult).then_inc(s["weighted_b"], 1)
                    if p + 1 == PAIRS and after:
                        multiply(i + 1, 0)
                    if p or before:
                        weigh_c(i - 1, (p + 1) % 2)
                    if p == 3 and after:
                        front(g + 1)

                run(pool, front, slot, lambda: weigh_c(GROUPS * PAIRS - 1, 1))

            @block.tensor
            def _(pe):
                def turn(g, first):
                    pe.wait_ge(s["xn_ready"], g + 1)
                    if not first:
                        pe.wait_ge(s["x_updated"], g)
                    for k in range(KT):
                        for t in range(GB):
                            last = nc.tensor.transpose(ps_z[k][:, t * P:(t + 1) * P],
                                                       xn[:, t, k * P:(k + 1) * P], ident[:])
                        last.then_inc(s["xnt_moved"], 1)

                def project(g, half):
                    for m in range(KT):
                        if half:
                            pe.wait_ge(s["z_taken"], 4 * g + m + 1)
                        elif m == 0:
                            pe.wait_ge(s["xnt_low"], KT * g + KT)
                        for k in range(KT):
                            cols = slice((KT * half + m) * P, (KT * half + m + 1) * P)
                            last = product(nc, ps_z[m][:], [a[:, k, cols] for a in s_in],
                                           [a[:, k, :] for a in xnt], k == 0, k == KT - 1)
                        last.then_inc(s["z_ready"], 1)

                def project_u(g):
                    pe.wait_ge(s["u_low"], g + 1)
                    pe.wait_ge(s["z_taken"], 4 * g + 2 * KT)
                    for k in range(KT):
                        last = product(nc, ps_z[0][:], [a[:, k, :] for a in s_bc],
                                       [a[:, k, :] for a in act], k == 0, k == KT - 1)
                    last.then_inc(s["bc_ready"], 1)
                    for m in range(KT):
                        if m:
                            pe.wait_ge(s["bc_taken"], g + 1)
                        for k in range(KT):
                            last = product(nc, ps_z[1 - m][:], [a[:, k, m * P:(m + 1) * P] for a in s_delta],
                                           [a[:, k, :] for a in act], k == 0, k == KT - 1)
                        last.then_inc(s["z1_ready"], 1)
                    pe.wait_ge(s["z1_low"], KT * g + KT)
                    for m in range(KT):
                        for k in range(KT):
                            last = product(nc, ps_z[1 - m][:], [a[:, k, m * P:(m + 1) * P] for a in s_tau],
                                           [a[:, k, :] for a in xnt], k == 0, k == KT - 1)
                        last.then_inc(s["z2_ready"], 1)

                def spread(g, p, rows, taken, ready):
                    if rows == 0 and p == 0:
                        pe.wait_ge(s["bc_low"], g + 1)
                    pe.wait_ge(taken, g * PAIRS + p + 1)
                    for k in range(2):
                        row = rows * STATE + 2 * p + k
                        last = nc.tensor.matmul(ps_b[2 * rows + k][:],
                                                pick_r[:, row:row + 1].to_broadcast([4 * STATE, P]), bc[:],
                                                start=True, stop=True)
                    last.then_inc(ready, 1)

                def add_outputs(i, p):
                    pe.wait_ge(s["weighted_c"], 2 + i + 1)
                    for k in range(2):
                        for c in range(KT):
                            last = nc.tensor.matmul(ps_y[c][:], ident[:], h[:, p % 2, k, c], start=(p == 0 and k == 0),
                                                    stop=(p == PAIRS - 1 and k == 1))
                    last.then_inc(s["outputs_added"], 1)

                def project_out(g):
                    pe.wait_ge(s["y_low"], g + 1)
                    for t in range(GB):
                        for k in range(KT):
                            last = product(nc, ps_z[t // 2][:, (t % 2) * DM:(t % 2 + 1) * DM],
                                           [a[:, k, t * P:(t + 1) * P] for a in act],
                                           [a[:, k, :] for a in s_out], k == 0, k == KT - 1)
                        if t % 2:
                            last.then_inc(s["out_ready"], 1)

                def front(g):
                    turn(g, True)
                    pe.wait_ge(s["w_low"], len(raw))
                    pe.wait_ge(s["rate_set"], 1)
                    project(g, 0)
                    project(g, 1)
                    project_u(g)
                    spread(g, 0, 0, s["b_taken"], s["b_spread"])

                def slot(g, p, before, after):
                    if p + 1 < PAIRS:
                        spread(g, p + 1, 0, s["b_taken"], s["b_spread"])
                    spread(g, p, 1, s["c_taken"], s["c_spread"])
                    if p == 2 and before:
                        pe.wait_ge(s["y_ready"], g)
                    if p >= 2 or before:
                        add_outputs(g * PAIRS + p - 2, (p - 2) % PAIRS)
                    if p == 2 and before:
                        project_out(g - 1)
                    if after:
                        if p == 3:
                            turn(g + 1, False)
                            project(g + 1, 0)
                        if p == 4:
                            project(g + 1, 1)
                        if p == 5:
                            project_u(g + 1)
                        if p == PAIRS - 1:
                            spread(g + 1, 0, 0, s["b_taken"], s["b_spread"])

                def close():
                    for p in (PAIRS - 2, PAIRS - 1):
                        add_outputs((GROUPS - 1) * PAIRS + p, p)
                    project_out(GROUPS - 1)

                run(pe, front, slot, close)

            @block.scalar
            def _(ac):
                ac.wait_ge(s["w_loaded"], 16 * LOADS)
                ac.wait_ge(s["small_set"], 1)
                for i, (t, (hi, lo)) in enumerate(zip(raw, split)):
                    nc.scalar.activation(hi[:], t, ACT.Copy).then_inc(s["w_high"], 1)
                nc.scalar.activation(rate[:], a_log[:], ACT.Exp).then_inc(s["rate_exp"], 1)
                ac.sem_inc(s["b_taken"], 1)
                ac.sem_inc(s["c_taken"], 1)
                ac.wait_ge(s["rate_set"], 1)
                ac.wait_ge(s["w_low"], len(raw))
                chain = Chain(ac, s["act_chain"])

                def turned_high(g):
                    for k in range(KT):
                        ac.wait_ge(s["xnt_moved"], KT * g + k + 1)
                        nc.scalar.activation(xnt[0][:, k, :], ps_z[k][:], ACT.Copy).then_inc(s["xnt_high"], 1)

                def pad(g):
                    for m in range(KT):
                        ac.wait_ge(s["z_ready"], 4 * g + m + 1)
                        nc.scalar.activation(padded[:, m, :, 1:SEQ + 1],
                                             ps_z[m][:].rearrange("p (b s) -> p b s", s=SEQ),
                                             ACT.Copy).then_inc(s["z_taken"], 1)

                def tanh_value(g):
                    ac.wait_ge(s["conv_ready"], g + 1)
                    nc.scalar.activation(tanh_v[:], half_v[:], ACT.Tanh).then_inc(s["tanh_ready"], 1)

                def tanh_gate(g, first):
                    if not first:
                        ac.wait_ge(s["gate_ready"], g)
                    for m in range(KT):
                        ac.wait_ge(s["z_ready"], 4 * g + KT + m + 1)
                        nc.scalar.activation(half_g[:, m, :], ps_z[m][:], ACT.Copy, scale=0.5)
                        nc.scalar.activation(tanh_g[:, m, :], ps_z[m][:], ACT.Tanh,
                                             scale=0.5).then_inc(s["z_taken"], 1)

                def value_high(g):
                    ac.wait_ge(s["u_ready"], g + 1)
                    nc.scalar.activation(act[0][:], u[:], ACT.Copy).then_inc(s["u_high"], 1)

                def take_bc(g):
                    ac.wait_ge(s["bc_ready"], g + 1)
                    nc.scalar.activation(bc_sum[:], ps_z[0][0:4 * STATE, :], ACT.Copy).then_inc(s["bc_taken"], 1)
                    for m in range(KT):
                        ac.wait_ge(s["z1_ready"], KT * g + m + 1)
                        nc.scalar.activation(xnt[0][:, m, :], ps_z[1 - m][:], ACT.Identity,
                                             bias=base[:, m:m + 1]).then_inc(s["z1_high"], 1)

                def decay_exp(g):
                    for m in range(KT):
                        ac.wait_ge(s["z2_ready"], KT * g + m + 1)
                        chain.link(nc.scalar.activation(tanh_v[:, m, :], ps_z[1 - m][:], ACT.Abs))
                    nc.scalar.activation(tanh_v[:], tanh_v[:], ACT.Exp, scale=-1.0).then_inc(s["exp_ready"], 1)

                def log(g):
                    ac.wait_ge(s["one_plus_ready"], g + 1)
                    nc.scalar.activation(inner, half_v[:].rearrange("p k (b s) -> p k b s", s=SEQ), ACT.Ln).then_inc(s["ln_ready"], 1)

                def bc_high(g):
                    ac.wait_ge(s["bc_taken"], g + 1)
                    nc.scalar.activation(bc[:], bc_sum[:], ACT.Copy).then_inc(s["bc_high"], 1)

                def copy_b(i, parity):
                    ac.wait_ge(s["weighing_b"], 2 * i + 2)
                    ac.wait_ge(s["b_spread"], i + 1)
                    for k in range(2):
                        last = nc.scalar.activation(bcs[:, parity, 0, k, :], ps_b[k][:], ACT.Copy)
                    last.then_inc(s["b_taken"], 1)

                def copy_c(i, parity):
                    ac.wait_ge(s["weighted_c"], i + 1)
                    ac.wait_ge(s["c_spread"], i + 1)
                    for k in range(2):
                        last = nc.scalar.activation(bcs[:, parity, 1, k, :], ps_b[2 + k][:], ACT.Copy)
                    last.then_inc(s["c_taken"], 1)

                def denominators(g, p):
                    i = g * PAIRS + p
                    if p == 0:
                        ac.wait_ge(s["delta_ready"], g + 1)
                    ac.wait_ge(s["weighted_b"], 2 * i + 2)
                    for k in range(2):
                        for c in range(KT):
                            n = 2 * p + k
                            last = nc.scalar.activation(den[:, p % 2, k, c, :], delta[:, c, :], ACT.Copy,
                                                        bias=EPS_DA, scale=rate_kept[:, c, n:n + 1])
                    last.then_inc(s["den_ready"], 1)

                def exponentials(g, p):
                    ac.wait_ge(s["state_ready"], g * PAIRS + p + 1)
                    for k in range(2):
                        for c in range(KT):
                            n = 2 * p + k
                            nc.scalar.activation(em[:, p % 2, k, c, :], delta[:, c, :], ACT.Tanh,
                                                 scale=half_rate[:, c, n:n + 1])
                            last = nc.scalar.activation(decay[:, p % 2, k, c, :], delta[:, c, :], ACT.Exp,
                                                        scale=rate[:, c, n:n + 1])
                    last.then_inc(s["em_ready"], 1)

                def result_high(g):
                    ac.wait_ge(s["y_ready"], g + 1)
                    nc.scalar.activation(act[0][:], y[:], ACT.Copy).then_inc(s["y_high"], 1)

                def start(g):
                    bc_high(g)
                    denominators(g, 0)
                    exponentials(g, 0)
                    copy_b(g * PAIRS, 0)

                def front(g):
                    turned_high(g)
                    pad(g)
                    tanh_gate(g, True)
                    tanh_value(g)
                    value_high(g)
                    take_bc(g)
                    decay_exp(g)
                    log(g)
                    start(g)

                def slot(g, p, before, after):
                    i = g * PAIRS + p
                    if p + 1 < PAIRS:
                        denominators(g, p + 1)
                        copy_b(i + 1, (p + 1) % 2)
                    copy_c(i, p % 2)
                    if p == 2 and before:
                        result_high(g - 1)
                    if p == 4 and after:
                        pad(g + 1)
                    if p == 5 and after:
                        value_high(g + 1)
                    if p == 6 and after:
                        decay_exp(g + 1)
                    if p + 1 < PAIRS:
                        exponentials(g, p + 1)
                    elif after:
                        start(g + 1)
                    if p == 3 and after:
                        turned_high(g + 1)
                    if p == 4 and after:
                        tanh_value(g + 1)
                        tanh_gate(g + 1, False)
                    if p == 5 and after:
                        take_bc(g + 1)
                    if p == 6 and after:
                        log(g + 1)

                run(ac, front, slot, lambda: result_high(GROUPS - 1), chain, KT)

            @block.vector
            def _(dve):
                def layer_norm(g):
                    for t in range(GB):
                        last = nc.vector.tensor_scalar(xn[:, t, :], x[:, bass.ds(g * GB + t, 1), :].squeeze(1),
                                                       core.ln[:, 0, bass.ds(g * GB + t, 1)],
                                                       core.ln[:, 3, bass.ds(g * GB + t, 1)],
                                                       ALU.subtract, ALU.mult)
                    last.then_inc(s["xn_ready"], 1)

                chain = Chain(dve, s["chain"])
                link = chain.link
                variance(core, dve, chain, s["variance_ready"])
                dve.wait_ge(s["scale_ready"], 1)
                layer_norm(0)
                dve.wait_ge(s["scale_ready"], 2)
                dve.wait_ge(s["w_loaded"], 16 * LOADS)
                split_low(core, dve, raw, split, s["w_high"], s["w_low"])
                dve.wait_ge(s["small_set"], 2)
                dve.wait_ge(s["pick_ready"], 2)
                nc.vector.tensor_copy(pick_r[:], pick[:])
                nc.vector.tensor_scalar(conv[:], conv[:], 0.5, None, ALU.mult)
                dve.wait_ge(s["rate_exp"], 1)
                nc.vector.tensor_scalar(half_rate[:], rate[:], -0.5, None, ALU.mult)
                nc.vector.tensor_scalar(rate_kept[:], rate[:], -1.0, LEAST_A, ALU.mult, ALU.max)
                link(nc.vector.tensor_scalar(rate[:], rate[:], -1.0, None, ALU.mult))
                dve.sem_inc(s["rate_set"], 1)
                dve.sem_inc(s["outputs_added"], 2)
                dve.sem_inc(s["input_ready"], 1)
                dve.sem_inc(s["state_ready"], 2)
                dve.sem_inc(s["x_updated"], 1)

                def turned_low(g):
                    for k in range(KT):
                        dve.wait_ge(s["xnt_high"], KT * g + k + 1)
                        nc.vector.tensor_tensor(xnt[1][:, k, :], ps_z[k][:], xnt[0][:, k, :].bitcast(F32),
                                                ALU.subtract).then_inc(s["xnt_low"], 1)

                def convolve(g):
                    dve.wait_ge(s["z_taken"], 4 * g + KT)
                    for j in range(3):
                        for c in range(KT):
                            out = half_v[:, c, :].rearrange("p (b s) -> p b s", s=SEQ)
                            src, tap = padded[:, c, :, j:j + SEQ], conv[:, c, j:j + 1]
                            if j == 0:
                                last = nc.vector.tensor_scalar(out, src, tap, None, ALU.mult)
                            else:
                                last = nc.vector.scalar_tensor_tensor(out=out, in0=src, scalar=tap, in1=out,
                                                                      op0=ALU.mult, op1=ALU.add)
                        if j < 2:
                            link(last)
                    last.then_inc(s["conv_ready"], 1)

                def value(g):
                    dve.wait_ge(s["tanh_ready"], g + 1)
                    nc.vector.scalar_tensor_tensor(out=u[:], in0=tanh_v[:], scalar=1.0, in1=half_v[:],
                                                   op0=ALU.add, op1=ALU.mult).then_inc(s["u_ready"], 1)

                def value_low(g):
                    dve.wait_ge(s["u_high"], g + 1)
                    nc.vector.tensor_tensor(act[1][:], u[:], act[0][:].bitcast(F32),
                                            ALU.subtract).then_inc(s["u_low"], 1)

                def z1_low(g):
                    for m in range(KT):
                        dve.wait_ge(s["z1_high"], KT * g + m + 1)
                        nc.vector.scalar_tensor_tensor(out=xnt[1][:, m, :], in0=ps_z[1 - m][:],
                                                       scalar=base[:, m:m + 1], in1=xnt[0][:, m, :].bitcast(F32),
                                                       op0=ALU.add, op1=ALU.subtract).then_inc(s["z1_low"], 1)

                def one_plus(g):
                    dve.wait_ge(s["exp_ready"], g + 1)
                    nc.vector.tensor_scalar(half_v[:], tanh_v[:], 1.0, None, ALU.add).then_inc(s["one_plus_ready"], 1)

                def log1p(g):
                    dve.wait_ge(s["one_plus_ready"], g + 1)
                    link(nc.vector.scalar_tensor_tensor(out=tanh_v[:], in0=half_v[:], scalar=-1.0, in1=tanh_v[:],
                                                        op0=ALU.add, op1=ALU.subtract))
                    dve.wait_ge(s["ln_ready"], g + 1)
                    for c in range(KT):
                        last = nc.vector.tensor_tensor(tanh_v[:, c, :].rearrange("p (b s) -> p b s", s=SEQ), inner[:, c],
                                                       tanh_v[:, c, :].rearrange("p (b s) -> p b s", s=SEQ),
                                                       ALU.subtract)
                    link(last)

                def start(g):
                    for m in range(KT):
                        last = nc.vector.scalar_tensor_tensor(out=delta[:, m, :], in0=ps_z[1 - m][:], scalar=0.0,
                                                              in1=tanh_v[:, m, :], op0=ALU.max, op1=ALU.add)
                    link(last)
                    nc.vector.tensor_tensor(du[:], delta[:], u[:], ALU.mult).then_inc(s["delta_ready"], 1)

                def bc_low(g):
                    dve.wait_ge(s["bc_high"], g + 1)
                    low = slice(2 * STATE, 4 * STATE)
                    nc.vector.tensor_tensor(bc[low, :], bc_sum[low, :], bc[low, :].bitcast(F32),
                                            ALU.subtract).then_inc(s["bc_low"], 1)

                def invert(i, parity, first=False):
                    dve.wait_ge(s["weighted_b"], 2 * i + 2)
                    if not first:
                        dve.wait_ge(s["pair_inverted"], i)
                    dve.wait_ge(s["pair_ready"], i + 1)
                    link(nc.vector.reciprocal(mult_pair[:, parity], mult_pair[:, parity]))
                    nc.vector.tensor_tensor(inv_pair[:, parity], mult_pair[:, parity], du[:],
                                            ALU.mult).then_inc(s["pair_inverted"], 1)

                def make_gate(g):
                    dve.wait_ge(s["z_taken"], 4 * g + 2 * KT)
                    nc.vector.scalar_tensor_tensor(out=gate[:], in0=tanh_g[:], scalar=1.0, in1=half_g[:],
                                                   op0=ALU.add, op1=ALU.mult).then_inc(s["gate_ready"], 1)

                def result(g, newer):
                    dve.wait_ge(s["outputs_added"], 2 + g * PAIRS + PAIRS)
                    dve.wait_ge(s["xn_added"], g + 1 + newer)
                    dve.wait_ge(s["gate_ready"], g + 1)
                    for c in range(KT):
                        last = nc.vector.tensor_tensor(y[:, c, :], ps_y[c][:], gate[:, c, :], ALU.mult)
                    last.then_inc(s["y_ready"], 1)

                def result_low(g):
                    dve.wait_ge(s["y_high"], g + 1)
                    nc.vector.tensor_tensor(act[1][:], y[:], act[0][:].bitcast(F32),
                                            ALU.subtract).then_inc(s["y_low"], 1)

                def update(g):
                    for j in range(GB // 2):
                        dve.wait_ge(s["out_ready"], (GB // 2) * g + j + 1)
                        xg = x[:, bass.ds(g * GB + 2 * j, 2), :]
                        last = nc.vector.tensor_tensor(xg, xg, ps_z[j][:].rearrange("p (t d) -> p t d", d=DM),
                                                       ALU.add)
                    last.then_inc(s["x_updated"], 1)
                    dve.wait_ge(s["x_updated"], 1 + g + 1)
                    for t in range(GB):
                        nc.vector.bn_stats(core.stats[:, bass.ds(g * GB + t, 1), :].squeeze(1),
                                           x[:, bass.ds(g * GB + t, 1), :].squeeze(1))

                def scan(i, parity):
                    e, a = em[:, parity], decay[:, parity]
                    dve.wait_ge(s["em_ready"], i + 1)
                    link(nc.vector.scalar_tensor_tensor(out=e, in0=a, scalar=1.0, in1=e, op0=ALU.add, op1=ALU.mult))
                    nc.vector.memset(a.rearrange("p k c (b t) -> p (k c b) t", t=SEQ)[:, :, 0:1], 0.0)
                    dve.wait_ge(s["weighted_b"], 4 + 2 * i + 2)
                    nc.vector.tensor_tensor(e, e, wb[:], ALU.mult).then_inc(s["input_ready"], 1)
                    dve.wait_ge(s["outputs_added"], i + 1)
                    dve.wait_ge(s["input_ready"], 1 + i + 1)
                    for k in range(2):
                        for c in range(KT):
                            last = nc.vector.tensor_tensor_scan(h[:, parity, k, c], a[:, k, c], e[:, k, c], 0.0,
                                                                ALU.mult, ALU.add)
                    last.then_inc(s["state_ready"], 1)

                def front(g):
                    turned_low(g)
                    convolve(g)
                    value(g)
                    value_low(g)
                    z1_low(g)
                    one_plus(g)
                    log1p(g)
                    start(g)
                    bc_low(g)
                    invert(g * PAIRS, 0, True)

                def slot(g, p, before, after):
                    i = g * PAIRS + p
                    if after:
                        if p == 3:
                            layer_norm(g + 1)
                        if p == 4:
                            convolve(g + 1)
                        if p == 5:
                            value_low(g + 1)
                        if p == 6:
                            one_plus(g + 1)
                        if p == PAIRS - 1:
                            dve.wait_ge(s["em_ready"], i + 1)
                            start(g + 1)
                    if p == 2 and before:
                        result_low(g - 1)
                    if p + 1 < PAIRS:
                        invert(i + 1, (p + 1) % 2)
                    if after:
                        if p == 3:
                            turned_low(g + 1)
                        if p == 4:
                            value(g + 1)
                        if p == 5:
                            z1_low(g + 1)
                        if p == 6:
                            log1p(g + 1)
                    if p == 1 and before:
                        result(g - 1, 1)
                    if p == 2:
                        if before:
                            update(g - 1)
                        make_gate(g)
                    scan(i, p % 2)
                    if p == PAIRS - 1 and after:
                        bc_low(g + 1)
                        invert(i + 1, 0)

                def close():
                    result(GROUPS - 1, 0)
                    result_low(GROUPS - 1)
                    update(GROUPS - 1)

                run(dve, front, slot, close, chain, PAIRS + PAIRS + 5)
        core.retire(s)


def cross_attention(core, w, name, masked):
    nc, x, ident = core.nc, core.x, core.ident
    HEADS, HD = 16, DM // 16
    SIDES = P // HD
    ROWS = SIDES // 2
    VW = HD + 1
    NEG = -1e9
    SLOTS = BATCH * ROWS
    UB = 2
    UT, US, UNITS = UB * SEQ, UB * ROWS, BATCH // UB
    TURN, USE, SCALE, HEADS_TURN, PROJECT, ADD = 2, 3, 7, 8, 9, 11
    BODY = 2 * US
    HEAD = ADD
    LOOPS = (SLOTS - HEAD) // BODY

    with ExitStack() as ctx:
        def sb(n, shape, dt=F32):
            return ctx.enter_context(nc.sbuf_tensor(f"{name}_{n}", shape, dt))

        def ps(n):
            return ctx.enter_context(nc.psum_tensor(f"{name}_{n}", [P, GT], F32))

        raw = [sb(n, [P, KT, DM]) for n in ("w_q", "w_k", "w_v", "w_o")]
        split = [(sb(f"hi{i}", t.shape, F32R), sb(f"lo{i}", t.shape, F32R)) for i, t in enumerate(raw)]
        s_q, s_k, s_v, s_o = split
        b_q, b_k = sb("b_q", [P, KT]), sb("b_k", [P, KT])
        b_v, b_o = sb("b_v", [P, DM]), sb("b_o", [P, DM])
        side = sb("side", [P, SIDES])
        b_scaled = sb("b_scaled", [P, KT])
        context = sb("context", [P, UB, DM])
        if masked:
            padded = sb("padded", [P, TILES, SEQ], U8)
            causal = sb("causal", [P, SEQ])
            mask = sb("mask", [P, TILES, SEQ])
            keep = sb("keep", [P, TILES, SEQ])

        xn = sb("xn", [P, UB, DM])
        xnt = (sb("xnt_hi", [P, KT, UT], F32R), sb("xnt_lo", [P, KT, UT], F32R))
        cnt = (sb("cnt_hi", [P, KT, UT], F32R), sb("cnt_lo", [P, KT, UT], F32R))
        q_all = sb("q_all", [P, KT, UT])
        q = [[sb(f"q{i}_{h}", [P, KT, UT]) for h in range(SIDES)] for i in range(2)]
        k_t = [sb(f"k{i}", [P, KT, UT]) for i in range(2)]
        v = sb("v", [P, 2, UB, HEADS, VW])
        shifted = sb("shifted", [P, ROWS, 4, SEQ])
        top = sb("top", [P, ROWS, 4])
        masked_s = sb("masked_s", [P, 2, 4, SEQ]) if masked else None
        probs_t = sb("probs_t", [P, 2, 4 * SEQ])
        inv_sum = sb("inv_sum", [P, HEADS])
        mixed = sb("mixed", [P, DM])
        mixed_t = (sb("mixed_hi", [P, KT, SEQ], F32R), sb("mixed_lo", [P, KT, SEQ], F32R))

        ps_s, ps_t, ps_f = ([ps(f"{n}{i}") for i in range(2)] for n in ("s", "t", "f"))
        ps_o, ps_p = ps("o"), ps("p")

        names = ("w_loaded w_high w_low side_set variance_ready scale_ready cn_loaded cn_turned cn_high "
                 "cn_low k_ready k_taken v_ready v_taken xn_ready bias_added xn_turned xn_high xn_low q_ready q_scaled "
                 "q_even q_odd scores_ready scores_taken scores_masked shift_ready probs_ready probs_turned "
                 "probs_copied heads_ready mixed_ready mixed_turned mixed_high mixed_low out_ready x_updated "
                 "ones_set mask_ready chain")
        s = core.stage_sems(name + "_", names)
        LOADS = 9 + 2 * masked
        taken = s["scores_taken"] if masked else s["shift_ready"]

        def run(engine, front, step, chain=None, links=0):
            front(0)
            for c in range(HEAD):
                step(0, c)
            with engine.Fori(0, LOOPS) as k:
                if chain:
                    chain.enter(k, links)
                for c in range(HEAD, HEAD + BODY):
                    step(k, c)
                if chain:
                    chain.leave(LOOPS)
            for c in range(HEAD + LOOPS * BODY, SLOTS + ADD):
                step(0, c)

        def at(k, c, lag):
            c = c - lag
            return k * BODY + c, k * 2 + c // US, k * 2 * UB + c // ROWS, 0 <= c < SLOTS

        def ends(c, lag):
            return (c - lag) % ROWS == 0 and 0 <= c - lag < SLOTS

        def ahead(c, place):
            return c % US == place and c // US + 1 < UNITS

        with nc.Block() as block:
            @block.sync
            def _(sp):
                for t, n in zip(raw, ("Wq", "Wk", "Wv", "Wo")):
                    sp.dma_start(t[:], w[f"{name}_{n}"]).then_inc(s["w_loaded"], 16)
                sp.dma_start(b_q[:], w[f"{name}_bq"]).then_inc(s["w_loaded"], 16)
                sp.dma_start(b_k[:], w[f"{name}_bk"]).then_inc(s["w_loaded"], 16)
                sp.dma_start(b_v[:], w[f"{name}_bv"].partition_broadcast(P)).then_inc(s["w_loaded"], 16)
                sp.dma_start(b_o[:], w[f"{name}_bo"].partition_broadcast(P)).then_inc(s["w_loaded"], 16)
                sp.dma_start(side[:], w["side"]).then_inc(s["w_loaded"], 16)
                if masked:
                    sp.dma_start(padded[:], w["padding"].partition_broadcast(P)).then_inc(s["w_loaded"], 16)
                    sp.dma_start(causal[:], w["causal"]).then_inc(s["w_loaded"], 16)
                with sp.Fori(0, UNITS) as t:
                    sp.wait_ge(s["cn_turned"], t + 1)
                    sp.dma_start(context[:], w["context"][:, bass.ds(t * UB, UB), :]).then_inc(s["cn_loaded"], 16)

            @block.gpsimd
            def _(pool):
                nc.gpsimd.memset(v[:, :, :, :, HD:VW], 1.0).then_inc(s["ones_set"], 1)
                inverse_deviation(core, pool, s["variance_ready"], s["scale_ready"])
                pool.wait_ge(s["w_loaded"], 16 * LOADS)

                def front(t):
                    pool.wait_ge(s["xn_ready"], t + 1)
                    xu = x[:, bass.ds(t * UB, UB), :]
                    nc.gpsimd.tensor_tensor(xu, xu, b_o[:].unsqueeze(1).to_broadcast([P, UB, DM]),
                                            ALU.add).then_inc(s["bias_added"], 1)

                def step(k, c):
                    n, t, _, there = at(k, c, 0)
                    if masked and there:
                        pool.wait_ge(s["scores_masked"], n + 1)
                        pool.wait_ge(s["probs_turned"], n + 1)
                        nc.gpsimd.tensor_tensor(shifted[:, c % ROWS], masked_s[:, c % 2],
                                                top[:, c % ROWS].unsqueeze(2).to_broadcast([P, 4, SEQ]),
                                                ALU.subtract).then_inc(s["shift_ready"], 1)
                    if ahead(c, 3):
                        front(t + 1)

                run(pool, front, step)

            @block.tensor
            def _(pe):
                pe.sem_inc(s["cn_turned"], 1)
                pe.sem_inc(s["probs_turned"], ROWS)
                pe.sem_inc(s["heads_ready"], 2)
                pe.sem_inc(s["mixed_turned"], 1)
                pe.sem_inc(s["out_ready"], 1)
                pe.wait_ge(s["ones_set"], 1)

                def turn(t, first=False):
                    pe.wait_ge(s["cn_loaded"], 16 * t + 16)
                    pe.wait_ge(s["xn_ready"], t + 1)
                    if not first:
                        pe.wait_ge(s["v_taken"], t)
                        pe.wait_ge(s["q_scaled"], t)
                    for bank, source, turned in ((ps_f[0], context, "cn_turned"), (ps_f[1], xn, "xn_turned")):
                        for k in range(KT):
                            for b in range(UB):
                                last = nc.tensor.transpose(bank[:, k * UT + b * P:k * UT + (b + 1) * P],
                                                           source[:, b, k * P:(k + 1) * P], ident[:])
                        last.then_inc(s[turned], 1)

                def project(t):
                    for bank, weights, source, low, ready in ((ps_f[0], s_k, cnt, "cn_low", "k_ready"),
                                                              (ps_f[1], s_q, xnt, "xn_low", "q_ready")):
                        pe.wait_ge(s[low], t + 1)
                        for m in range(KT):
                            for k in range(KT):
                                last = product(nc, bank[:, m * UT:(m + 1) * UT],
                                               [a[:, k, m * P:(m + 1) * P] for a in weights],
                                               [a[:, k, :] for a in source], k == 0, k == KT - 1)
                        last.then_inc(s[ready], 1)

                def project_v(t):
                    pe.wait_ge(s["k_taken"], t + 1)
                    for b in range(UB):
                        for k in range(KT):
                            last = product(nc, ps_f[0][:, b * DM:(b + 1) * DM],
                                           [a[:, k, b * P:(b + 1) * P] for a in cnt],
                                           [a[:, k, :] for a in s_v], k == 0, k == KT - 1)
                    last.then_inc(s["v_ready"], 1)

                def front(t):
                    turn(t, True)
                    pe.wait_ge(s["w_low"], len(raw))
                    project(t)
                    project_v(t)

                def step(k, c):
                    n, t, _, there = at(k, c, 0)
                    if there:
                        r, cols = c % ROWS, slice(c // ROWS % UB * SEQ, (c // ROWS % UB + 1) * SEQ)
                        i = c // US % 2
                        pe.wait_ge(taken, n + 1)
                        if c % US == 0:
                            pe.wait_ge(s["k_taken"], t + 1)
                        if c % US < ROWS:
                            pe.wait_ge(s["q_even"], ROWS * t + r + 1)
                            pe.wait_ge(s["q_odd"], ROWS * t + r + 1)
                        for m in range(KT):
                            for o in range(2):
                                j = 2 * m + o
                                last = nc.tensor.matmul(ps_s[c % 2][:, j * SEQ:(j + 1) * SEQ],
                                                        q[i][2 * r + o][:, m, cols], k_t[i][:, m, cols],
                                                        start=True, stop=True)
                        last.then_inc(s["scores_ready"], 1)
                    n, _, _, there = at(k, c, TURN)
                    if there:
                        pe.wait_ge(s["probs_ready"], n + 1)
                        pe.wait_ge(s["probs_copied"], n + 1)
                        for j in range(4):
                            last = nc.tensor.transpose(ps_t[c % 2][:, j * SEQ:(j + 1) * SEQ],
                                                       shifted[:, (c - TURN) % ROWS, j, :], ident[:])
                        last.then_inc(s["probs_turned"], 1)
                    n, t, b, there = at(k, c, USE)
                    if there:
                        r, i = (c - USE) % ROWS, (c - USE) // US % 2
                        pe.wait_ge(s["probs_copied"], 2 + n + 1)
                        if (c - USE) % US == 0:
                            pe.wait_ge(s["v_taken"], t + 1)
                        if r == 0:
                            pe.wait_ge(s["mixed_ready"], b + 1)
                        for j in range(4):
                            head = SIDES * (j // 2) + 2 * r + j % 2
                            last = nc.tensor.matmul(ps_o[:, head * VW:(head + 1) * VW],
                                                    probs_t[:, (c - USE) % 2, j * SEQ:(j + 1) * SEQ],
                                                    v[:, i, (c - USE) // ROWS % UB, head, :], start=True, stop=True)
                        last.then_inc(s["heads_ready"], 1)
                    if ends(c, HEADS_TURN):
                        b = at(k, c, HEADS_TURN)[2]
                        pe.wait_ge(s["mixed_ready"], 1 + b + 1)
                        pe.wait_ge(s["x_updated"], b + 1)
                        for m in range(KT):
                            last = nc.tensor.transpose(ps_p[:, m * P:(m + 1) * P], mixed[:, m * P:(m + 1) * P],
                                                       ident[:])
                        last.then_inc(s["mixed_turned"], 1)
                    if ends(c, PROJECT):
                        pe.wait_ge(s["mixed_low"], at(k, c, PROJECT)[2] + 1)
                        for m in range(KT):
                            last = product(nc, ps_p[:, DM:2 * DM], [a[:, m, :] for a in mixed_t],
                                           [a[:, m, :] for a in s_o], m == 0, m == KT - 1)
                        last.then_inc(s["out_ready"], 1)
                    unit = at(k, c, 0)[1] + 1
                    if ahead(c, 3):
                        turn(unit)
                    if ahead(c, 5):
                        project(unit)
                    if ahead(c, 6):
                        project_v(unit)

                run(pe, front, step)

            @block.scalar
            def _(ac):
                ac.wait_ge(s["w_loaded"], 16 * LOADS)
                for i, (t, (hi, lo)) in enumerate(zip(raw, split)):
                    nc.scalar.activation(hi[:], t[:], ACT.Copy).then_inc(s["w_high"], 1)
                ac.sem_inc(s["probs_copied"], 2)
                nc.scalar.preload_act_table(ACT.Exp)
                ac.wait_ge(s["side_set"], 1)

                def turned_high(t):
                    for bank, parts, turned, high in ((ps_f[0], cnt, "cn_turned", "cn_high"),
                                                      (ps_f[1], xnt, "xn_turned", "xn_high")):
                        ac.wait_ge(s[turned], t + 1 + (parts is cnt))
                        nc.scalar.activation(parts[0][:].rearrange("p k t -> p (k t)"), bank[:],
                                             ACT.Copy).then_inc(s[high], 1)

                def take(t, i):
                    if not masked:
                        ac.wait_ge(s["k_ready"], t + 1)
                        for m in range(KT):
                            last = nc.scalar.activation(k_t[i][:, m, :], ps_f[0][:, m * UT:(m + 1) * UT], ACT.Identity,
                                                        bias=b_k[:, m:m + 1])
                        last.then_inc(s["k_taken"], 1)
                    ac.wait_ge(s["q_ready"], t + 1)
                    for m in range(KT):
                        last = nc.scalar.activation(q_all[:, m, :], ps_f[1][:, m * UT:(m + 1) * UT], ACT.Identity,
                                                    bias=b_scaled[:, m:m + 1], scale=HD ** -0.5)
                    last.then_inc(s["q_scaled"], 1)

                def even_heads(t, i, pairs):
                    ac.wait_ge(s["q_scaled"], t + 1)
                    for r in pairs:
                        nc.scalar.activation(q[i][2 * r][:], q_all[:], ACT.Copy,
                                             scale=side[:, 2 * r:2 * r + 1]).then_inc(s["q_even"], 1)

                def front(t):
                    turned_high(t)
                    take(t, 0)
                    even_heads(t, 0, range(ROWS))

                def step(k, c):
                    n, _, _, there = at(k, c, TURN)
                    if there:
                        ac.wait_ge(s["probs_turned"], ROWS + n + 1)
                        ac.wait_ge(s["heads_ready"], n + 1)
                        nc.scalar.activation(probs_t[:, c % 2, :], ps_t[c % 2][:],
                                             ACT.Copy).then_inc(s["probs_copied"], 1)
                    n, t, _, there = at(k, c, 0)
                    if there:
                        ac.wait_ge(s["shift_ready"], 2 + n + 1)
                        nc.scalar.activation(shifted[:, c % ROWS], shifted[:, c % ROWS],
                                             ACT.Exp).then_inc(s["probs_ready"], 1)
                    if ends(c, HEADS_TURN):
                        b = at(k, c, HEADS_TURN)[2]
                        ac.wait_ge(s["mixed_turned"], 1 + b + 1)
                        ac.wait_ge(s["out_ready"], b + 1)
                        nc.scalar.activation(mixed_t[0][:], ps_p[:, 0:DM].rearrange("p (k t) -> p k t", k=KT),
                                             ACT.Copy).then_inc(s["mixed_high"], 1)
                    if ahead(c, 3):
                        turned_high(t + 1)
                    if ahead(c, 5):
                        take(t + 1, (c // US + 1) % 2)
                    for half in range(2):
                        if ahead(c, 6 + half):
                            even_heads(t + 1, (c // US + 1) % 2, (2 * half, 2 * half + 1))

                run(ac, front, step)

            @block.vector
            def _(dve):
                chain = Chain(dve, s["chain"])
                link = chain.link
                variance(core, dve, chain, s["variance_ready"])
                if masked:
                    dve.sem_inc(s["scores_taken"], 2)
                dve.sem_inc(s["shift_ready"], 2)
                dve.sem_inc(s["mixed_ready"], 1)
                dve.sem_inc(s["x_updated"], 1)

                def layer_norm(t):
                    for b in range(UB):
                        last = nc.vector.tensor_scalar(xn[:, b, :], x[:, bass.ds(t * UB + b, 1), :].squeeze(1),
                                                       core.ln[:, 0, bass.ds(t * UB + b, 1)],
                                                       core.ln[:, 3, bass.ds(t * UB + b, 1)],
                                                       ALU.subtract, ALU.mult)
                    last.then_inc(s["xn_ready"], 1)

                def turned_low(t):
                    for bank, (high, low), ready, done in ((ps_f[0], cnt, "cn_high", "cn_low"),
                                                           (ps_f[1], xnt, "xn_high", "xn_low")):
                        dve.wait_ge(s[ready], t + 1)
                        nc.vector.tensor_tensor(low[:].rearrange("p k t -> p (k t)"), bank[:],
                                                high[:].rearrange("p k t -> p (k t)").bitcast(F32),
                                                ALU.subtract).then_inc(s[done], 1)

                def take_k(t, i):
                    dve.wait_ge(s["k_ready"], t + 1)
                    kept = keep[:, bass.ds(t * UB, UB), :].rearrange("p b t -> p (b t)")
                    for m in range(KT):
                        last = nc.vector.scalar_tensor_tensor(out=k_t[i][:, m, :], in0=ps_f[0][:, m * UT:(m + 1) * UT],
                                                              scalar=b_k[:, m:m + 1], in1=kept, op0=ALU.add,
                                                              op1=ALU.mult)
                    last.then_inc(s["k_taken"], 1)

                def odd_heads(t, i, pairs):
                    dve.wait_ge(s["q_scaled"], t + 1)
                    for r in pairs:
                        nc.vector.tensor_scalar(q[i][2 * r + 1][:], q_all[:], side[:, 2 * r + 1:2 * r + 2], None,
                                                ALU.mult).then_inc(s["q_odd"], 1)

                def take_v(t, i):
                    dve.wait_ge(s["v_ready"], t + 1)
                    for b in range(UB):
                        last = nc.vector.tensor_tensor(
                            v[:, i, b, :, 0:HD], ps_f[0][:, b * DM:(b + 1) * DM].rearrange("p (h d) -> p h d", d=HD),
                            b_v[:].rearrange("p (h d) -> p h d", d=HD), ALU.add)
                    last.then_inc(s["v_taken"], 1)

                def front(t):
                    dve.wait_ge(s["scale_ready"], 1)
                    layer_norm(t)
                    dve.wait_ge(s["scale_ready"], 2)
                    dve.wait_ge(s["w_loaded"], 16 * LOADS)
                    split_low(core, dve, [t[:] for t in raw], split, s["w_high"], s["w_low"])
                    nc.vector.tensor_scalar(b_scaled[:], b_q[:], HD ** -0.5, None, ALU.mult).then_inc(s["side_set"], 1)
                    turned_low(t)
                    if masked:
                        nc.vector.tensor_scalar(keep[:], padded[:], -1.0, 1.0, ALU.mult, ALU.add)
                        nc.vector.tensor_scalar(mask[:], padded[:], NEG, None, ALU.mult).then_inc(s["mask_ready"], 1)
                        dve.wait_ge(s["mask_ready"], 1)
                        nc.vector.tensor_tensor(mask[:], mask[:], causal[:].unsqueeze(1).to_broadcast([P, TILES, SEQ]),
                                                ALU.add).then_inc(s["mask_ready"], 1)
                        dve.wait_ge(s["mask_ready"], 2)
                        take_k(t, 0)
                    odd_heads(t, 0, range(ROWS))
                    dve.wait_ge(s["ones_set"], 1)
                    take_v(t, 0)

                def step(k, c):
                    n, t, b, there = at(k, c, 0)
                    if ahead(c, 3):
                        layer_norm(t + 1)
                    if ahead(c, 7):
                        take_v(t + 1, (c // US + 1) % 2)
                    if ends(c, SCALE):
                        e = at(k, c, SCALE)[2]
                        dve.wait_ge(s["heads_ready"], 2 + ROWS * e + ROWS)
                        dve.wait_ge(s["mixed_turned"], e + 1)
                        heads = ps_o[:, 0:HEADS * VW].rearrange("p (h d) -> p h d", d=VW)
                        link(nc.vector.reciprocal(inv_sum[:], heads[:, :, HD]))
                        nc.vector.tensor_tensor(mixed[:].rearrange("p (h d) -> p h d", d=HD), heads[:, :, 0:HD],
                                                inv_sum[:].unsqueeze(2).to_broadcast([P, HEADS, HD]),
                                                ALU.mult).then_inc(s["mixed_ready"], 1)
                    if there:
                        r = c % ROWS
                        scores = ps_s[c % 2][:].rearrange("p (j t) -> p j t", t=SEQ)
                        dve.wait_ge(s["scores_ready"], n + 1)
                        if masked:
                            dve.wait_ge(s["shift_ready"], n + 1)
                            mask_b = mask[:, bass.ds(b, 1), :].to_broadcast([P, 4, SEQ])
                            nc.vector.tensor_tensor(masked_s[:, c % 2], scores, mask_b,
                                                    ALU.add).then_inc(s["scores_taken"], 1)
                            dve.wait_ge(s["scores_taken"], 2 + n + 1)
                            nc.vector.tensor_reduce(top[:, r], masked_s[:, c % 2], AX.X,
                                                    ALU.max).then_inc(s["scores_masked"], 1)
                        else:
                            link(nc.vector.tensor_reduce(top[:, r], scores, AX.X, ALU.max))
                            dve.wait_ge(s["probs_turned"], n + 1)
                            nc.vector.tensor_tensor(shifted[:, r], scores,
                                                    top[:, r].unsqueeze(2).to_broadcast([P, 4, SEQ]),
                                                    ALU.subtract).then_inc(s["shift_ready"], 1)
                    if ends(c, PROJECT):
                        dve.wait_ge(s["mixed_high"], at(k, c, PROJECT)[2] + 1)
                        nc.vector.tensor_tensor(mixed_t[1][:], ps_p[:, 0:DM].rearrange("p (k t) -> p k t", k=KT),
                                                mixed_t[0][:].bitcast(F32), ALU.subtract).then_inc(s["mixed_low"], 1)
                    if ends(c, ADD):
                        _, u, e, _ = at(k, c, ADD)
                        xb = x[:, bass.ds(e, 1), :].squeeze(1)
                        dve.wait_ge(s["out_ready"], 1 + e + 1)
                        dve.wait_ge(s["bias_added"], u + 1)
                        nc.vector.tensor_tensor(xb, xb, ps_p[:, DM:2 * DM], ALU.add).then_inc(s["x_updated"], 1)
                        dve.wait_ge(s["x_updated"], 1 + e + 1)
                        nc.vector.bn_stats(core.stats[:, bass.ds(e, 1), :].squeeze(1), xb)
                    if ahead(c, 4):
                        turned_low(t + 1)
                    if masked and ahead(c, 5):
                        take_k(t + 1, (c // US + 1) % 2)
                    for half in range(2):
                        if ahead(c, 6 + half):
                            odd_heads(t + 1, (c // US + 1) % 2, (2 * half, 2 * half + 1))

                run(dve, front, step, chain, BODY // ROWS + (0 if masked else BODY))
        core.retire(s)


def experts(core, w, name, shared, routed, softmax_first):
    nc, x, ident = core.nc, core.x, core.ident
    E, PAIRS = shared + routed, (shared + routed) // 2
    FF = w[f"{name}_W1"].shape[3]
    FT = FF // P
    STEPS = 2 * GROUPS * FT
    UP, HID, RING = 3, 3, 4
    LAG = 3
    TOP = 2

    with ExitStack() as ctx:
        def sb(n, shape, dt=F32):
            return ctx.enter_context(nc.sbuf_tensor(f"{name}_{n}", shape, dt))

        def ps(n):
            return ctx.enter_context(nc.psum_tensor(f"{name}_{n}", [P, GT], F32))

        w_r, w_r_hi, w_r_lo = (sb(f"w_r{i}", [P, KT, P], F32R if i else F32) for i in range(3))
        logits_t = sb("logits_t", [routed, TILES * SEQ])
        b_r, b_1, b_2 = sb("b_r", [P, routed]), sb("b_1", [P, E, FT]), sb("b_2", [P, E, DM])
        before = sb("before", [P, routed, routed])
        raw = sb("raw_1", [P, KT, FF]), sb("raw_2", [P, FT, DM])
        w_1 = [(sb(f"w1_hi{j}", [P, KT, FF], F32R), sb(f"w1_lo{j}", [P, KT, FF], F32R)) for j in range(2)]
        w_2 = [(sb(f"w2_hi{j}", [P, FT, DM], F32R), sb(f"w2_lo{j}", [P, FT, DM], F32R)) for j in range(2)]
        zero = sb("zero", [P, 1, 1])
        b_now = sb("b_now", [P, 2, FT])
        xnt = (sb("xnt_hi", [P, KT, TILES * SEQ], F32R), sb("xnt_lo", [P, KT, TILES * SEQ], F32R))
        normal = [sb(f"xn{g}", [P, GB, DM]) for g in range(2)] * 2
        hid = sb("hid", [P, HID, GT])
        hid_hi, hid_lo = sb("hid_hi", [P, RING, GT], F32R), sb("hid_lo", [P, RING, GT], F32R)
        gates = sb("gates", [P, TILES, E])
        score, excess = sb("score", [P, TILES, routed]), sb("excess", [P, TILES, routed])
        rank, best = sb("rank", [P, TILES, routed]), sb("best", [P, TILES])
        above, equal = (sb(n, [P, TILES, routed, routed]) for n in ("above", "equal"))

        ps_u = [ps(f"u{i}") for i in range(UP)]
        ps_a = [[ps(f"a{i}{j}") for j in range(2)] for i in range(2)]
        ps_r = ps("r")
        ps_x = [ps_u[0:2], ps_a[0]] * 2

        names = ("small_loaded w_loaded w_high w_split router_ready variance_ready scale_ready xn_ready xn_turned "
                 "xn_high xn_low columns_set logits_turned logits_copied logits_ready excess_ready exp_ready "
                 "up_ready hid_ready hid_high hid_low down_done acc_taken bias_copied chain")
        s = core.stage_sems(name + "_", names)
        SMALL = 5

        def group_of(step):
            return step // (GROUPS * FT), step // FT % GROUPS, step % FT

        with nc.Block() as block:
            @block.sync
            def _(sp):
                sp.dma_start(w_r[:, :, 0:routed], w[f"{name}_Wr"]).then_inc(s["small_loaded"], 16)
                for t, n in ((b_1, "b1"), (before, "before")):
                    sp.dma_start(t[:], w[f"{name}_{n}"]).then_inc(s["small_loaded"], 16)
                for t, n in ((b_r, "br"), (b_2, "b2")):
                    sp.dma_start(t[:], w[f"{name}_{n}"].partition_broadcast(P)).then_inc(s["small_loaded"], 16)
                with sp.Fori(0, E) as e:
                    sp.wait_ge(s["w_split"], 2 * e + 2)
                    for t, n in zip(raw, ("W1", "W2")):
                        sp.dma_start(t[:], w[f"{name}_{n}"][bass.ds(e, 1)].squeeze(0)).then_inc(s["w_loaded"], 16)

            @block.gpsimd
            def _(pool):
                pool.sem_inc(s["w_split"], 2)
                nc.gpsimd.memset(zero[:], 0.0)
                nc.gpsimd.memset(w_r[:, :, routed:], 0.0).then_inc(s["columns_set"], 1)
                inverse_deviation(core, pool, s["variance_ready"], s["scale_ready"])
                pool.wait_ge(s["columns_set"], 1)
                pool.wait_ge(s["small_loaded"], 16 * SMALL)
                nc.gpsimd.tensor_copy(w_r_hi[:], w_r[:]).then_inc(s["router_ready"], 1)
                pool.wait_ge(s["router_ready"], 1)
                nc.gpsimd.tensor_tensor(w_r_lo[:], w_r[:], w_r_hi[:].bitcast(F32),
                                        ALU.subtract).then_inc(s["router_ready"], 1)
                if shared:
                    nc.gpsimd.memset(gates[:, :, 0:shared], 1.0 / shared).then_inc(s["router_ready"], 1)
                with pool.Fori(0, PAIRS) as e2:
                    for j in range(2):
                        e = 2 * e2 + j
                        pool.wait_ge(s["w_loaded"], 32 * e + 32)
                        pool.wait_ge(s["down_done"], RING + GROUPS * FT * e)
                        for i, (t, (hi, lo)) in enumerate(zip(raw, (w_1[j], w_2[j]))):
                            nc.gpsimd.tensor_tensor(hi[:], t[:], zero[:].to_broadcast(t.shape),
                                                    ALU.add).then_inc(s["w_high"], 1)
                            pool.wait_ge(s["w_high"], 2 * e + i + 1)
                            nc.gpsimd.tensor_tensor(lo[:], t[:], hi[:].bitcast(F32),
                                                    ALU.subtract).then_inc(s["w_split"], 1)

            @block.tensor
            def _(pe):
                pe.sem_inc(s["down_done"], RING + GROUPS * FT)
                pe.wait_ge(s["router_ready"], 2 + bool(shared))

                def turn(g):
                    pe.wait_ge(s["xn_ready"], g + 1)
                    if g >= 2:
                        pe.wait_ge(s["xn_low"], KT * (g - 1))
                    for k in range(KT):
                        for t in range(GB):
                            last = nc.tensor.transpose(ps_x[g][k][:, t * P:(t + 1) * P],
                                                       normal[g][:, t, k * P:(k + 1) * P], ident[:])
                        last.then_inc(s["xn_turned"], 1)

                def route(g):
                    pe.wait_ge(s["xn_low"], KT * g + KT)
                    if g >= 2:
                        pe.wait_ge(s["logits_copied"], g - 1)
                    for k in range(KT):
                        last = product(nc, ps_a[1][g % 2][:], [a[:, k, :] for a in (w_r_hi, w_r_lo)],
                                       [a[:, k, g * GT:(g + 1) * GT] for a in xnt], k == 0, k == KT - 1)
                    last.then_inc(s["logits_turned"], 1)

                def turn_back(g):
                    pe.wait_ge(s["logits_copied"], g + 1)
                    for t in range(GB * g, GB * g + GB):
                        last = nc.tensor.transpose(ps_r[:, t * routed:(t + 1) * routed],
                                                   logits_t[:, t * P:(t + 1) * P], ident[0:routed, 0:routed])
                    return last

                turn(0)
                turn(1)
                for g in range(GROUPS):
                    route(g)
                    if g + 2 < GROUPS:
                        turn(g + 2)
                    if g:
                        turn_back(g - 1)
                turn_back(GROUPS - 1).then_inc(s["logits_ready"], 1)
                with pe.Fori(0, PAIRS) as e2:
                    for n in range(STEPS + LAG):
                        if n < STEPS:
                            j, g, f = group_of(n)
                            if n % (GROUPS * FT) == 0:
                                pe.wait_ge(s["w_split"], 2 + 4 * e2 + 2 * j + 1)
                            pe.wait_ge(s["hid_ready"], e2 * STEPS + n + 1)
                            for k in range(KT):
                                last = product(nc, ps_u[n % UP][:], [a[:, k, f * P:(f + 1) * P] for a in w_1[j]],
                                               [a[:, k, g * GT:(g + 1) * GT] for a in xnt], k == 0, k == KT - 1)
                            last.then_inc(s["up_ready"], 1)
                        d = n - LAG
                        if d >= 0:
                            j, g, f = group_of(d)
                            if d % (GROUPS * FT) == 0:
                                pe.wait_ge(s["w_split"], 2 + 4 * e2 + 2 * j + 2)
                            pe.wait_ge(s["hid_low"], HID + e2 * STEPS + d + 1)
                            if f == 0:
                                pe.wait_ge(s["acc_taken"], e2 * STEPS // FT + d // FT + 1)
                            for t in range(GB):
                                out = ps_a[d // FT % 2][t // 2][:, (t % 2) * DM:(t % 2 + 1) * DM]
                                last = product(nc, out, [a[:, d % RING, t * P:(t + 1) * P] for a in (hid_hi, hid_lo)],
                                               [a[:, f, :] for a in w_2[j]], f == 0 and t % 2 == 0, f == FT - 1,
                                               skip=True)
                            last.then_inc(s["down_done"], 1)

            @block.scalar
            def _(ac):
                nc.scalar.preload_act_table(ACT.Exp)

                def copy_logits(g):
                    ac.wait_ge(s["logits_turned"], g + 1)
                    nc.scalar.activation(logits_t[:, g * GT:(g + 1) * GT], ps_a[1][g % 2][0:routed, :],
                                         ACT.Copy).then_inc(s["logits_copied"], 1)

                for g in range(GROUPS):
                    if g >= 2:
                        copy_logits(g - 2)
                    for k in range(KT):
                        ac.wait_ge(s["xn_turned"], KT * g + k + 1)
                        nc.scalar.activation(xnt[0][:, k, g * GT:(g + 1) * GT], ps_x[g][k][:],
                                             ACT.Copy).then_inc(s["xn_high"], 1)
                copy_logits(GROUPS - 2)
                copy_logits(GROUPS - 1)
                ac.wait_ge(s["excess_ready"], 1)
                nc.scalar.activation(excess[:], excess[:], ACT.Exp).then_inc(s["exp_ready"], 1)
                ac.sem_inc(s["hid_ready"], UP)
                ac.sem_inc(s["hid_high"], HID)
                nc.scalar.preload_act_table(ACT.Relu)
                with ac.Fori(0, PAIRS) as e2:
                    nc.scalar.activation(b_now[:], b_1[:, bass.ds(2 * e2, 2), :], ACT.Copy).then_inc(s["bias_copied"], 1)
                    ac.wait_ge(s["bias_copied"], e2 + 1)
                    for n in range(STEPS + 1):
                        i = e2 * STEPS + n
                        if n < STEPS:
                            j, g, f = group_of(n)
                            ac.wait_ge(s["up_ready"], i + 1)
                            ac.wait_ge(s["hid_low"], i + 1)
                            nc.scalar.activation(hid[:, n % HID, :], ps_u[n % UP][:], ACT.Relu,
                                                 bias=b_now[:, j, f:f + 1]).then_inc(s["hid_ready"], 1)
                        if n:
                            m = n - 1
                            ac.wait_ge(s["hid_ready"], UP + i)
                            ac.wait_ge(s["down_done"], GROUPS * FT + i)
                            nc.scalar.activation(hid_hi[:, m % RING, :], hid[:, m % HID, :],
                                                 ACT.Copy).then_inc(s["hid_high"], 1)

            @block.vector
            def _(dve):
                chain = Chain(dve, s["chain"])
                link = chain.link
                variance(core, dve, chain, s["variance_ready"])
                dve.wait_ge(s["scale_ready"], 1)

                def layer_norm(g):
                    if g >= 2:
                        dve.wait_ge(s["xn_turned"], KT * (g - 1))
                    for t in range(GB):
                        last = normalise(core, normal[g][:, t, :], GB * g + t)
                    last.then_inc(s["xn_ready"], 1)

                layer_norm(0)
                dve.wait_ge(s["scale_ready"], 2)
                for g in range(GROUPS):
                    if g + 1 < GROUPS:
                        layer_norm(g + 1)
                    for k in range(KT):
                        dve.wait_ge(s["xn_high"], KT * g + k + 1)
                        cols = slice(g * GT, (g + 1) * GT)
                        nc.vector.tensor_tensor(xnt[1][:, k, cols], ps_x[g][k][:], xnt[0][:, k, cols].bitcast(F32),
                                                ALU.subtract).then_inc(s["xn_low"], 1)
                dve.wait_ge(s["small_loaded"], 16 * SMALL)
                dve.wait_ge(s["logits_ready"], 1)
                wide = [P, TILES, routed]
                link(nc.vector.tensor_tensor(score[:], ps_r[:, 0:TILES * routed].rearrange("p (t e) -> p t e", e=routed),
                                             b_r[:].unsqueeze(1).to_broadcast(wide), ALU.add))
                link(nc.vector.tensor_reduce(best[:], score[:], AX.X, ALU.max))
                nc.vector.tensor_tensor(excess[:], score[:], best[:].unsqueeze(2).to_broadcast(wide),
                                        ALU.subtract).then_inc(s["excess_ready"], 1)
                dve.wait_ge(s["exp_ready"], 1)
                g_out = gates[:, :, shared:E]

                def over_sum(out, value):
                    link(nc.vector.tensor_reduce(best[:], value, AX.X, ALU.add))
                    link(nc.vector.reciprocal(best[:], best[:]))
                    link(nc.vector.tensor_tensor(out, value, best[:].unsqueeze(2).to_broadcast(wide), ALU.mult))

                if softmax_first:
                    over_sum(score[:], excess[:])
                square = [P, TILES, routed, routed]
                other = score[:].unsqueeze(2).to_broadcast(square)
                own = score[:].unsqueeze(3).to_broadcast(square)
                nc.vector.tensor_tensor(above[:], other, own, ALU.is_gt)
                link(nc.vector.tensor_tensor(equal[:], other, own, ALU.is_equal))
                link(nc.vector.tensor_tensor(equal[:], equal[:], before[:].unsqueeze(1).to_broadcast(square), ALU.mult))
                link(nc.vector.tensor_tensor(above[:], above[:], equal[:], ALU.add))
                link(nc.vector.tensor_reduce(rank[:], above[:], AX.X, ALU.add))
                link(nc.vector.tensor_scalar(rank[:], rank[:], float(TOP), None, ALU.is_lt))
                if softmax_first:
                    link(nc.vector.tensor_tensor(g_out, rank[:], score[:], ALU.mult))
                else:
                    link(nc.vector.tensor_tensor(excess[:], rank[:], excess[:], ALU.mult))
                    over_sum(g_out, excess[:])
                dve.sem_inc(s["hid_low"], HID)
                dve.sem_inc(s["acc_taken"], 2)
                FIRST_ACC = FT - 1 + LAG + 1
                BIAS_LEAD = 4

                def two_experts(e2, finish):
                    for n in range(STEPS - FT + FIRST_ACC + 1):
                        if n < STEPS:
                            dve.wait_ge(s["hid_high"], HID + e2 * STEPS + n + 1)
                            nc.vector.tensor_tensor(hid_lo[:, n % RING, :], hid[:, n % HID, :],
                                                    hid_hi[:, n % RING, :].bitcast(F32),
                                                    ALU.subtract).then_inc(s["hid_low"], 1)
                        r, late = divmod(n + BIAS_LEAD - FIRST_ACC, FT)
                        if late == 0 and 0 <= r < STEPS // FT:
                            j, g, _ = group_of(r * FT)
                            for t in range(GB * g, GB * g + GB):
                                last = nc.vector.scalar_tensor_tensor(
                                    out=x[:, t, :], in0=b_2[:, bass.ds(2 * e2 + j, 1), :].squeeze(1),
                                    scalar=gates[:, t, bass.ds(2 * e2 + j, 1)], in1=x[:, t, :],
                                    op0=ALU.mult, op1=ALU.add)
                            link(last)
                        r, late = divmod(n - FIRST_ACC, FT)
                        if late == 0 and 0 <= r < STEPS // FT:
                            q = e2 * (STEPS // FT) + r
                            j, g, _ = group_of(r * FT)
                            dve.wait_ge(s["down_done"], RING + GROUPS * FT + FT * q + FT)
                            for t in range(GB):
                                xt = x[:, g * GB + t, :]
                                last = nc.vector.scalar_tensor_tensor(
                                    out=xt, in0=ps_a[r % 2][t // 2][:, (t % 2) * DM:(t % 2 + 1) * DM],
                                    scalar=gates[:, g * GB + t, bass.ds(2 * e2 + j, 1)], in1=xt,
                                    op0=ALU.mult, op1=ALU.add)
                            last.then_inc(s["acc_taken"], 1)
                            dve.wait_ge(s["acc_taken"], 2 + q + 1)
                            if finish and j == 1:
                                statistics(g)

                def statistics(g):
                    for t in range(g * GB, (g + 1) * GB):
                        nc.vector.bn_stats(core.stats[:, t, :], x[:, t, :])

                with dve.Fori(0, PAIRS - 1) as e2:
                    chain.enter(e2, STEPS // FT)
                    two_experts(e2, False)
                    chain.leave(PAIRS - 1)
                two_experts(PAIRS - 1, True)
        core.retire(s)


def routed_experts(core, w, name, out):
    nc, x, ident = core.nc, core.x, core.ident
    E, TOP = w[f"{name}_W1"].shape[0], 2
    FF = w[f"{name}_W1"].shape[3]
    FT = FF // P
    BT, NB = core.block_rows, core.blocks
    LEVELS = TILES * SEQ // BT
    UP, HID, RING = 3, 3, 4
    LAG = 3
    BODY = 4
    LOOPS, REST = divmod(NB, BODY)
    FIRST_OUT = FT - 1 + LAG + 1
    STORE_OUT = FIRST_OUT + 2

    with ExitStack() as ctx:
        def sb(n, shape, dt=F32):
            return ctx.enter_context(nc.sbuf_tensor(f"{name}_{n}", shape, dt))

        def ps(n):
            return ctx.enter_context(nc.psum_tensor(f"{name}_{n}", [P, GT], F32))

        routed = E
        w_r, w_r_hi, w_r_lo = (sb(f"w_r{i}", [P, KT, P], F32R if i else F32) for i in range(3))
        logits_t = sb("logits_t", [routed, TILES * SEQ])
        b_r = sb("b_r", [P, routed])
        before = sb("before", [P, routed, routed])
        upper = sb("upper", [P, P])
        levels = sb("levels", [P, E, LEVELS])
        numbers = sb("numbers", [P, NB, E])
        gamma, beta = sb("gamma", [P, DM]), sb("beta", [P, DM])
        b_1, b_2 = sb("b_1", [P, BODY, FT]), sb("b_2", [P, BODY, DM])
        raw = sb("raw_1", [P, KT, FF]), sb("raw_2", [P, FT, DM])
        fetched = [raw[0][:].rearrange("p k (t d) -> p (k t) d", d=DM), raw[1][:]]
        w_1 = [(sb(f"w1_hi{j}", [P, KT, FF], F32R), sb(f"w1_lo{j}", [P, KT, FF], F32R)) for j in range(2)]
        w_2 = [(sb(f"w2_hi{j}", [P, FT, DM], F32R), sb(f"w2_lo{j}", [P, FT, DM], F32R)) for j in range(2)]
        xnt = [(sb(f"xnt_hi{j}", [P, KT, GT], F32R), sb(f"xnt_lo{j}", [P, KT, GT], F32R)) for j in range(2)]
        y = sb("y", [P, TILES, DM])
        normal = [y[:, g * GB:(g + 1) * GB, :] for g in range(GROUPS)]
        block_in = sb("block_in", [P, 2, GB, DM])
        block_out = sb("block_out", [P, 2, GB, DM])
        hid = sb("hid", [P, HID, GT])
        hid_hi, hid_lo = sb("hid_hi", [P, RING, GT], F32R), sb("hid_lo", [P, RING, GT], F32R)
        score, excess, rank = (sb(n, [P, TILES, E]) for n in ("score", "excess", "rank"))
        best = sb("best", [P, TILES])
        above, equal = (hid[:, i:i + 2, :].rearrange("p a (t e f) -> p (a t) e f", e=E, f=E) for i in (0, 0))
        upper_h, ones = sb("upper_h", [P, P], BF16), sb("ones", [P, P], BF16)
        chosen = sb("chosen", [P, TILES + 1, E], BF16)
        choice = sb("choice", [P, TOP, TILES, E])
        gates = sb("gates", [P, TILES, E])
        gate = sb("gate", [P, TOP, TILES])
        used, start, end = (sb(n, [P, E]) for n in ("used", "start", "end"))
        place = sb("place", [P, TILES, E])
        full = sb("full", [P, E, LEVELS])
        earlier = sb("earlier", [P, E, E])
        past = sb("past", [P, NB, E])
        row_f, row = sb("row_f", [P, TOP, TILES]), sb("row", [P, TOP, TILES], U32)
        owner_f, owner = sb("owner_f", [P, NB]), sb("owner", [P, NB], U32)

        ps_u = [ps(f"u{i}") for i in range(UP)]
        ps_a = [[ps(f"a{i}{j}") for j in range(2)] for i in range(2)]
        ps_r = ps("r")
        ps_x = [ps_u[0:2], ps_a[0]] * 2
        counts = ps_u[2][:, 0:(TILES + 1) * E].rearrange("p (t e) -> p t e", e=E)

        names = ("small_loaded w1_loaded w2_loaded w_high w_split router_ready variance_ready scale_ready xn_ready "
                 "xn_turned xn_high xn_low columns_set logits_turned logits_copied logits_ready excess_ready exp_ready "
                 "chosen_ready counts_ready rows_ready table_ready sorted_ready block_loaded_0 block_loaded_1 "
                 "block_turned block_high block_low up_ready hid_ready hid_high hid_low down_done out_ready "
                 "out_stored out_free fetched_0 fetched_1 mixed variance2_ready scale2_ready beta_added x_updated "
                 "stored chain")
        s = core.stage_sems(name + "_", names)
        SMALL = 7

        def rows_of(dram, n):
            return dram.rearrange("(b p) d -> p b d", p=P)[:, bass.ds(n * GB, GB), :]

        def run(engine, body, chain=None, links=0):
            with engine.Fori(0, LOOPS) as k:
                if chain:
                    chain.enter(k, links)
                body(k, BODY)
                if chain:
                    chain.leave(LOOPS)
            body(LOOPS, REST)

        def steps(k, size):
            return [(i, k * (BODY * FT) + i) for i in range(size * FT + STORE_OUT - FT + 1)]

        def more(k, size, j):
            return size == BODY or j + 1 < size

        with nc.Block() as block:
            @block.sync
            def _(sp):
                sp.dma_start(w_r[:, :, 0:routed], w[f"{name}_Wr"]).then_inc(s["small_loaded"], 16)
                for t, n in ((before, "before"), (upper, "upper"), (levels, "levels"), (numbers, "numbers")):
                    sp.dma_start(t[:], w[f"{name}_{n}"]).then_inc(s["small_loaded"], 16)
                for t, n in ((b_r, "br"), (beta, "beta")):
                    sp.dma_start(t[:], w[f"{name}_{n}"].partition_broadcast(P)).then_inc(s["small_loaded"], 16)
                sp.wait_ge(s["table_ready"], 1)

                def load_weights(n, j):
                    e = sp.value_load(owner[0:1, bass.ds(n, 1)], min_val=0, max_val=E - 1)
                    sp.wait_ge(s["w_split"], 4 * n + 2)
                    sp.dma_start(raw[0][:], w[f"{name}_W1"][bass.ds(e, 1)].squeeze(0)).then_inc(s["w1_loaded"], 16)
                    sp.dma_start(b_1[:, j, :], w[f"{name}_b1"][:, bass.ds(e, 1), :].squeeze(1)
                                 ).then_inc(s["w1_loaded"], 16)
                    sp.wait_ge(s["w_split"], 4 * n + 4)
                    sp.dma_start(raw[1][:], w[f"{name}_W2"][bass.ds(e, 1)].squeeze(0)).then_inc(s["w2_loaded"], 16)
                    sp.dma_start(b_2[:, j, :], w[f"{name}_b2"][bass.ds(e, 1)].squeeze(0).partition_broadcast(P)
                                 ).then_inc(s["w2_loaded"], 16)

                def load_rows(n, j):
                    sp.wait_ge(s["block_turned"], KT * n + KT)
                    sp.dma_start(block_in[:, j % 2], rows_of(core.sorted_in, n)).then_inc(
                        s[f"block_loaded_{j % 2}"], 16)

                def body(k, size):
                    for j in range(size):
                        if more(k, size, j):
                            load_rows(k * BODY + j + 1, (j + 1) % BODY)
                            load_weights(k * BODY + j + 1, (j + 1) % BODY)

                load_weights(0, 0)
                sp.wait_ge(s["sorted_ready"], 16 * TOP * TILES)
                load_rows(0, 0)
                run(sp, body)
                for g in range(GROUPS):
                    sp.wait_ge(s["x_updated"], g + 1)
                    sp.dma_start(out[:, g * GB:(g + 1) * GB, :],
                                 x[:, g * GB:(g + 1) * GB, :]).then_inc(s["stored"], 16)
                sp.wait_ge(s["stored"], 16 * GROUPS)

            @block.gpsimd
            def _(pool):
                nc.gpsimd.memset(ones[:], 1.0)
                nc.gpsimd.memset(chosen[:, TILES:, :], 0.0)
                nc.gpsimd.memset(w_r[:, :, routed:], 0.0).then_inc(s["columns_set"], 1)
                inverse_deviation(core, pool, s["variance_ready"], s["scale_ready"])
                pool.wait_ge(s["columns_set"], 1)
                pool.wait_ge(s["small_loaded"], 16 * SMALL)
                nc.gpsimd.tensor_copy(w_r_hi[:], w_r[:]).then_inc(s["router_ready"], 1)
                pool.wait_ge(s["router_ready"], 1)
                nc.gpsimd.tensor_tensor(w_r_lo[:], w_r[:], w_r_hi[:].bitcast(F32),
                                        ALU.subtract).then_inc(s["router_ready"], 1)
                nc.gpsimd.tensor_copy(upper_h[:], upper[:]).then_inc(s["router_ready"], 1)
                pool.wait_ge(core.blocks_cleared, 16)
                pool.wait_ge(s["rows_ready"], 1)
                for t in range(TILES):
                    for c in range(TOP):
                        nc.gpsimd.indirect_dma_start(core.sorted_in, bass.IndirectOffsetOnAxis(ap=row[:, c, t:t + 1], axis=0),
                                                     y[:, t, :], None).then_inc(s["sorted_ready"], 16)
                nc.gpsimd.tensor_tensor(x[:], x[:], beta[:].unsqueeze(1).to_broadcast([P, TILES, DM]),
                                        ALU.add).then_inc(s["beta_added"], 1)
                pool.wait_ge(s["out_stored"], 16 * NB + 16)
                pool.wait_ge(s["w_split"], 4 + 4 * NB)
                for g in range(GROUPS):
                    if g >= 2:
                        pool.wait_ge(s["mixed"], g - 1)
                    for t in range(GB):
                        for c in range(TOP):
                            nc.gpsimd.indirect_dma_start(
                                fetched[g % 2][:, TOP * t + c, :], None, core.sorted_out,
                                bass.IndirectOffsetOnAxis(ap=row[:, c, g * GB + t:g * GB + t + 1], axis=0)
                            ).then_inc(s[f"fetched_{g % 2}"], 16)
                    if g:
                        inverse_deviation(core, pool, s["variance2_ready"], s["scale2_ready"],
                                          (((g - 1) * GB, g * GB),), g)
                inverse_deviation(core, pool, s["variance2_ready"], s["scale2_ready"],
                                  ((TILES - GB, TILES),), GROUPS)

            @block.tensor
            def _(pe):
                pe.sem_inc(s["down_done"], RING)
                pe.sem_inc(s["block_turned"], 2 * KT)
                pe.wait_ge(s["router_ready"], 2)

                def turn(g):
                    pe.wait_ge(s["xn_ready"], g + 1)
                    if g >= 2:
                        pe.wait_ge(s["xn_low"], KT * (g - 1))
                    for k in range(KT):
                        for t in range(GB):
                            last = nc.tensor.transpose(ps_x[g][k][:, t * P:(t + 1) * P],
                                                       normal[g][:, t, k * P:(k + 1) * P], ident[:])
                        last.then_inc(s["xn_turned"], 1)

                def route(g):
                    pe.wait_ge(s["xn_low"], KT * g + KT)
                    if g >= 2:
                        pe.wait_ge(s["logits_copied"], g - 1)
                    for k in range(KT):
                        last = product(nc, ps_a[1][g % 2][:], [a[:, k, :] for a in (w_r_hi, w_r_lo)],
                                       [a[:, k, :] for a in xnt[g % 2]], k == 0, k == KT - 1)
                    last.then_inc(s["logits_turned"], 1)

                def turn_back(g):
                    pe.wait_ge(s["logits_copied"], g + 1)
                    for t in range(GB * g, GB * g + GB):
                        last = nc.tensor.transpose(ps_r[:, t * routed:(t + 1) * routed],
                                                   logits_t[:, t * P:(t + 1) * P], ident[0:routed, 0:routed])
                    return last

                turn(0)
                turn(1)
                for g in range(GROUPS):
                    route(g)
                    if g + 2 < GROUPS:
                        turn(g + 2)
                    if g:
                        turn_back(g - 1)
                turn_back(GROUPS - 1).then_inc(s["logits_ready"], 1)
                pe.wait_ge(s["chosen_ready"], 1)
                pe.wait_ge(s["router_ready"], 3)
                nc.tensor.matmul(counts.rearrange("p t e -> p (t e)"), upper_h[:], chosen[:].rearrange("p t e -> p (t e)"),
                                 start=True, stop=False, skip_group_check=True)
                for t in range(TILES):
                    after = TILES - t
                    last = nc.tensor.matmul(counts[:, t + 1:, :], ones[:],
                                            chosen[:, t:t + 1, :].to_broadcast([P, after, E]),
                                            start=False, stop=t == TILES - 1, skip_group_check=True)
                last.then_inc(s["counts_ready"], 1)

                def turn_block(n, half_n, j, k, first=False):
                    if k == 0:
                        pe.wait_ge(s[f"block_loaded_{j % 2}"], 16 * half_n + 16)
                        if not first:
                            pe.wait_ge(s["block_low"], KT * n)
                    else:
                        pe.wait_ge(s["block_low"], KT * n + k)
                    for t in range(GB):
                        last = nc.tensor.transpose(ps_r[:, t * P:(t + 1) * P],
                                                   block_in[:, j % 2, t, k * P:(k + 1) * P], ident[:])
                    last.then_inc(s["block_turned"], 1)

                for k in range(KT):
                    turn_block(0, 0, 0, k, True)

                def body(b, size):
                    for i, m in steps(b, size):
                        j, f = divmod(i, FT)
                        n = b * BODY + j
                        if j < size:
                            if f == 0:
                                pe.wait_ge(s["w_split"], 4 + 4 * n + 2)
                                pe.wait_ge(s["block_low"], KT * n + KT)
                            pe.wait_ge(s["hid_ready"], m + 1)
                            for k in range(KT):
                                last = product(nc, ps_u[i % UP][:], [a[:, k, f * P:(f + 1) * P] for a in w_1[j % 2]],
                                               [a[:, k, :] for a in xnt[j % 2]], k == 0, k == KT - 1)
                            last.then_inc(s["up_ready"], 1)
                        d = i - LAG
                        if 0 <= d < size * FT:
                            j2, f2 = divmod(d, FT)
                            n2 = b * BODY + j2
                            if f2 == 0:
                                pe.wait_ge(s["w_split"], 4 + 4 * n2 + 4)
                                pe.wait_ge(s["out_ready"], n2 + 1)
                            pe.wait_ge(s["hid_low"], HID + m - LAG + 1)
                            for t in range(GB):
                                acc = ps_a[j2 % 2][t // 2][:, (t % 2) * DM:(t % 2 + 1) * DM]
                                last = product(nc, acc, [a[:, d % RING, t * P:(t + 1) * P] for a in (hid_hi, hid_lo)],
                                               [a[:, f2, :] for a in w_2[j2 % 2]], f2 == 0 and t % 2 == 0,
                                               f2 == FT - 1, skip=True)
                            last.then_inc(s["down_done"], 1)
                        if f in (1, 3) and j < size and more(b, size, j):
                            turn_block(n + 1, b * (BODY // 2) + (j + 1) // 2, j + 1, f // 2)

                run(pe, body)

            @block.scalar
            def _(ac):
                ac.dma_start(gamma[:], w[f"{name}_gamma"].partition_broadcast(P)).then_inc(s["out_stored"], 16)
                nc.scalar.preload_act_table(ACT.Exp)

                def copy_logits(g):
                    ac.wait_ge(s["logits_turned"], g + 1)
                    nc.scalar.activation(logits_t[:, g * GT:(g + 1) * GT], ps_a[1][g % 2][0:routed, :],
                                         ACT.Copy).then_inc(s["logits_copied"], 1)

                for g in range(GROUPS):
                    if g >= 2:
                        copy_logits(g - 2)
                    for k in range(KT):
                        ac.wait_ge(s["xn_turned"], KT * g + k + 1)
                        nc.scalar.activation(xnt[g % 2][0][:, k, :], ps_x[g][k][:], ACT.Copy).then_inc(s["xn_high"], 1)
                copy_logits(GROUPS - 2)
                copy_logits(GROUPS - 1)
                ac.wait_ge(s["excess_ready"], 1)
                nc.scalar.activation(excess[:], excess[:], ACT.Exp).then_inc(s["exp_ready"], 1)
                ac.sem_inc(s["hid_ready"], UP)
                ac.sem_inc(s["hid_high"], HID)
                ac.sem_inc(s["out_free"], 1)
                nc.scalar.preload_act_table(ACT.Relu)

                def weights_high(n, j, q):
                    loaded = s["w1_loaded"] if q < 2 else s["w2_loaded"]
                    ac.wait_ge(loaded, 32 * n + 32)
                    hi, whole = (w_1 if q < 2 else w_2)[j % 2][0][:], raw[q // 2][:]
                    a = q % 2
                    part = slice(a * (hi.shape[1] // 2), (a + 1) * (hi.shape[1] // 2))
                    nc.scalar.activation(hi[:, part], whole[:, part], ACT.Copy).then_inc(s["w_high"], 1)

                def block_high(n, j, k):
                    ac.wait_ge(s["block_turned"], 2 * KT + KT * n + k + 1)
                    nc.scalar.activation(xnt[j % 2][0][:, k, :], ps_r[:], ACT.Copy).then_inc(s["block_high"], 1)

                for q in range(4):
                    weights_high(0, 0, q)
                for k in range(KT):
                    block_high(0, 0, k)

                def body(b, size):
                    for i, m in steps(b, size):
                        j, f = divmod(i, FT)
                        n = b * BODY + j
                        if j < size:
                            ac.wait_ge(s["up_ready"], m + 1)
                            ac.wait_ge(s["hid_low"], m + 1)
                            nc.scalar.activation(hid[:, i % HID, :], ps_u[i % UP][:], ACT.Relu,
                                                 bias=b_1[:, j, f:f + 1]).then_inc(s["hid_ready"], 1)
                        if 0 <= i - 1 < size * FT:
                            ac.wait_ge(s["hid_ready"], UP + m)
                            ac.wait_ge(s["down_done"], m)
                            nc.scalar.activation(hid_hi[:, (i - 1) % RING, :], hid[:, (i - 1) % HID, :],
                                                 ACT.Copy).then_inc(s["hid_high"], 1)
                        if j < size and more(b, size, j):
                            if f in (2, 4):
                                block_high(n + 1, j + 1, f // 2 - 1)
                            if f >= 4:
                                weights_high(n + 1, j + 1, f - 4)
                        j2, late = divmod(i - STORE_OUT, FT)
                        if late == 0 and 0 <= j2 < size:
                            n2 = b * BODY + j2
                            ac.wait_ge(s["out_stored"], 16 * n2 + 16)
                            ac.sem_inc(s["out_free"], 1)
                            ac.wait_ge(s["out_ready"], 2 + n2 + 1)
                            ac.dma_start(rows_of(core.sorted_out, n2), block_out[:, j2 % 2]).then_inc(s["out_stored"], 16)

                run(ac, body)

            @block.vector
            def _(dve):
                chain = Chain(dve, s["chain"])
                link = chain.link
                variance(core, dve, chain, s["variance_ready"])
                dve.wait_ge(s["scale_ready"], 1)

                def layer_norm(g):
                    for t in range(GB):
                        last = normalise(core, normal[g][:, t, :], GB * g + t)
                    last.then_inc(s["xn_ready"], 1)

                layer_norm(0)
                dve.wait_ge(s["scale_ready"], 2)
                for g in range(GROUPS):
                    if g + 1 < GROUPS:
                        layer_norm(g + 1)
                    for k in range(KT):
                        dve.wait_ge(s["xn_high"], KT * g + k + 1)
                        nc.vector.tensor_tensor(xnt[g % 2][1][:, k, :], ps_x[g][k][:],
                                                xnt[g % 2][0][:, k, :].bitcast(F32), ALU.subtract).then_inc(s["xn_low"], 1)
                dve.wait_ge(s["small_loaded"], 16 * SMALL)
                dve.wait_ge(s["logits_ready"], 1)
                wide = [P, TILES, E]
                link(nc.vector.tensor_tensor(score[:], ps_r[:, 0:TILES * E].rearrange("p (t e) -> p t e", e=E),
                                             b_r[:].unsqueeze(1).to_broadcast(wide), ALU.add))
                link(nc.vector.tensor_reduce(best[:], score[:], AX.X, ALU.max))
                nc.vector.tensor_tensor(excess[:], score[:], best[:].unsqueeze(2).to_broadcast(wide),
                                        ALU.subtract).then_inc(s["excess_ready"], 1)
                square = [P, TILES, E, E]
                other = score[:].unsqueeze(2).to_broadcast(square)
                own = score[:].unsqueeze(3).to_broadcast(square)
                link(nc.vector.tensor_tensor(equal, other, own, ALU.is_equal))
                link(nc.vector.tensor_tensor(equal, equal, before[:].unsqueeze(1).to_broadcast(square), ALU.mult))
                link(nc.vector.tensor_reduce(rank[:], equal, AX.X, ALU.add))
                link(nc.vector.tensor_tensor(above, other, own, ALU.is_gt))
                link(nc.vector.tensor_reduce(place[:], above, AX.X, ALU.add))
                link(nc.vector.tensor_tensor(rank[:], rank[:], place[:], ALU.add))
                nc.vector.tensor_scalar(chosen[:, 0:TILES, :], rank[:], float(TOP), None,
                                        ALU.is_lt).then_inc(s["chosen_ready"], 1)
                dve.wait_ge(s["chosen_ready"], 1)
                for c in range(TOP):
                    last = nc.vector.tensor_scalar(choice[:, c], rank[:], float(c), None, ALU.is_equal)
                link(last)
                dve.wait_ge(s["counts_ready"], 1)
                link(nc.vector.tensor_tensor(full[:], counts[:, TILES, :].unsqueeze(2).to_broadcast([P, E, LEVELS]),
                                             levels[:], ALU.is_gt))
                link(nc.vector.tensor_reduce(used[:], full[:], AX.X, ALU.add))
                link(nc.vector.tensor_tensor(earlier[:], before[:], used[:].unsqueeze(1).to_broadcast([P, E, E]),
                                             ALU.mult))
                link(nc.vector.tensor_reduce(start[:], earlier[:], AX.X, ALU.add))
                link(nc.vector.tensor_tensor(end[:], start[:], used[:], ALU.add))
                link(nc.vector.tensor_scalar(start[:], start[:], float(BT), None, ALU.mult))
                link(nc.vector.tensor_tensor(place[:], counts[:, 0:TILES, :], start[:].unsqueeze(1).to_broadcast(wide),
                                             ALU.add))
                for c in range(TOP):
                    link(nc.vector.tensor_tensor(gates[:], choice[:, c], place[:], ALU.mult))
                    link(nc.vector.tensor_reduce(row_f[:, c], gates[:], AX.X, ALU.add))
                nc.vector.tensor_copy(row[:], row_f[:]).then_inc(s["rows_ready"], 1)
                link(nc.vector.tensor_tensor(past[:], numbers[:], end[:].unsqueeze(1).to_broadcast([P, NB, E]), ALU.is_ge))
                link(nc.vector.tensor_reduce(owner_f[:], past[:], AX.X, ALU.add))
                link(nc.vector.tensor_scalar(owner_f[:], owner_f[:], float(E - 1), None, ALU.min))
                nc.vector.tensor_copy(owner[:], owner_f[:]).then_inc(s["table_ready"], 1)
                dve.wait_ge(s["exp_ready"], 1)
                link(nc.vector.tensor_tensor(excess[:], chosen[:, 0:TILES, :], excess[:], ALU.mult))
                link(nc.vector.tensor_reduce(best[:], excess[:], AX.X, ALU.add))
                link(nc.vector.reciprocal(best[:], best[:]))
                link(nc.vector.tensor_tensor(gates[:], excess[:], best[:].unsqueeze(2).to_broadcast(wide), ALU.mult))
                for c in range(TOP):
                    link(nc.vector.tensor_tensor(excess[:], choice[:, c], gates[:], ALU.mult))
                    link(nc.vector.tensor_reduce(gate[:, c], excess[:], AX.X, ALU.add))
                dve.sem_inc(s["w_split"], 4)
                dve.sem_inc(s["hid_low"], HID)
                dve.sem_inc(s["out_ready"], 2)

                def weights_low(n, j, q):
                    dve.wait_ge(s["w_high"], 4 * n + q + 1)
                    high, low = (w_1 if q < 2 else w_2)[j % 2]
                    size = high.shape[1] // 2
                    part = slice(q % 2 * size, (q % 2 + 1) * size)
                    nc.vector.tensor_tensor(low[:, part], raw[q // 2][:, part], high[:, part].bitcast(F32),
                                            ALU.subtract).then_inc(s["w_split"], 1)

                def block_low(n, j, k):
                    dve.wait_ge(s["block_high"], KT * n + k + 1)
                    nc.vector.tensor_tensor(xnt[j % 2][1][:, k, :], ps_r[:], xnt[j % 2][0][:, k, :].bitcast(F32),
                                            ALU.subtract).then_inc(s["block_low"], 1)

                for q in range(4):
                    weights_low(0, 0, q)
                for k in range(KT):
                    block_low(0, 0, k)

                def body(b, size):
                    for i, m in steps(b, size):
                        j, f = divmod(i, FT)
                        n = b * BODY + j
                        if j < size:
                            dve.wait_ge(s["hid_high"], HID + m + 1)
                            nc.vector.tensor_tensor(hid_lo[:, i % RING, :], hid[:, i % HID, :],
                                                    hid_hi[:, i % RING, :].bitcast(F32),
                                                    ALU.subtract).then_inc(s["hid_low"], 1)
                        if j < size and more(b, size, j):
                            if f in (2, 4):
                                block_low(n + 1, j + 1, f // 2 - 1)
                            if f >= 4:
                                weights_low(n + 1, j + 1, f - 4)
                        j2, late = divmod(i - FIRST_OUT, FT)
                        if late == 0 and 0 <= j2 < size:
                            n2 = b * BODY + j2
                            dve.wait_ge(s["down_done"], RING + FT * n2 + FT)
                            dve.wait_ge(s["out_free"], n2 + 1)
                            for h in range(2):
                                last = nc.vector.tensor_tensor(
                                    block_out[:, j2 % 2, 2 * h:2 * h + 2, :],
                                    ps_a[j2 % 2][h][:].rearrange("p (t d) -> p t d", d=DM),
                                    b_2[:, j2, :].unsqueeze(1).to_broadcast([P, 2, DM]), ALU.add)
                            last.then_inc(s["out_ready"], 1)

                run(dve, body)

                def mix(g):
                    dve.wait_ge(s[f"fetched_{g % 2}"], 16 * TOP * GB * (g // 2 + 1))
                    for c in range(TOP):
                        for t in range(GB):
                            yt = y[:, g * GB + t, :]
                            last = nc.vector.scalar_tensor_tensor(
                                out=yt, in0=fetched[g % 2][:, TOP * t + c, :],
                                scalar=gate[:, c, g * GB + t:g * GB + t + 1], in1=yt, op0=ALU.mult, op1=ALU.add)
                        if c == 0:
                            link(last)
                    last.then_inc(s["mixed"], 1)
                    dve.wait_ge(s["mixed"], g + 1)
                    for t in range(g * GB, (g + 1) * GB):
                        last = nc.vector.bn_stats(core.stats[:, t, :], y[:, t, :])
                    link(last)
                    variance(core, dve, chain, s["variance2_ready"], slice(g * GB, (g + 1) * GB))

                def normalise_result(g):
                    dve.wait_ge(s["scale2_ready"], g + 1)
                    dve.wait_ge(s["beta_added"], 1)
                    for t in range(g * GB, (g + 1) * GB):
                        last = nc.vector.scalar_tensor_tensor(out=y[:, t, :], in0=y[:, t, :],
                                                              scalar=core.ln[:, 0, t:t + 1], in1=gamma[:],
                                                              op0=ALU.subtract, op1=ALU.mult)
                    link(last)
                    for t in range(g * GB, (g + 1) * GB):
                        last = nc.vector.scalar_tensor_tensor(out=x[:, t, :], in0=y[:, t, :],
                                                              scalar=core.ln[:, 3, t:t + 1], in1=x[:, t, :],
                                                              op0=ALU.mult, op1=ALU.add)
                    last.then_inc(s["x_updated"], 1)

                for g in range(GROUPS):
                    mix(g)
                    if g:
                        normalise_result(g - 1)
                normalise_result(GROUPS - 1)
        core.retire(s)


def self_attention(core, w):
    nc, x, ident = core.nc, core.x, core.ident
    HEADS, HD = 8, 64
    INNER = HEADS * HD
    SIDES = P // HD
    JT = INNER // P
    VW = HD + 1
    SCALE = 16.0
    LEAST_NORM, LEAST_SUM = 1e-12, 1e-6
    RING = 4

    with ExitStack() as ctx:
        def sb(n, shape, dt=F32):
            return ctx.enter_context(nc.sbuf_tensor(f"a_{n}", shape, dt))

        def ps(n):
            return ctx.enter_context(nc.psum_tensor(f"a_ps_{n}", [P, GT], F32))

        raw = [sb("w_q", [P, KT, INNER]), sb("w_kv", [P, KT, 2 * INNER]), sb("w_o", [P, JT, DM])]
        split = [(sb(f"hi{i}", t.shape, F32R), sb(f"lo{i}", t.shape, F32R)) for i, t in enumerate(raw)]
        s_q, s_kv, s_o = split
        minus_half = sb("minus_half", [P, 2 * HEADS])
        less_scale = sb("less_scale", [P, 1])
        xn = sb("xn", [P, RING, DM])
        xnt = (sb("xnt_hi", [P, KT, SEQ], F32R), sb("xnt_lo", [P, KT, SEQ], F32R))
        qk = sb("qk", [P, RING, 2, INNER])
        squares = sb("squares", [P, 2, INNER])
        norm = sb("norm", [P, RING, 2 * HEADS])
        v = sb("v", [P, RING, HEADS, VW])
        q_t, k_t = sb("q_t", [P, JT, SEQ]), sb("k_t", [P, JT, SEQ])
        probs = sb("probs", [P, SIDES, JT * SEQ])
        inv_sum = sb("inv_sum", [P, SIDES, JT])
        mixed = sb("mixed", [P, INNER])
        mixed_t = (sb("mixed_hi", [P, JT, SEQ], F32R), sb("mixed_lo", [P, JT, SEQ], F32R))

        ps_q, ps_k = ps("q"), ps("k")
        ps_v = ps("v")
        ps_x = ps("x")
        ps_s, ps_o = ([ps(f"{n}{i}") for i in range(2)] for n in "so")

        names = ("Wq_loaded Wkv_loaded Wo_loaded w_high w_low consts_set variance_ready scale_ready xn_ready xn_turned xn_high xn_low "
                 "q_ready k_ready v_ready q_copied k_copied v_copied squares_ready squares_summed norm_ready unit_ready "
                 "q_turned k_turned qt_ready kt_ready scores_ready probs_ready heads_ready mixed_ready mixed_turned "
                 "mixed_high mixed_low out_ready x_updated chain")
        s = core.stage_sems("a_", names)

        FIRST, PEELED, LAST = -2, 1, TILES + 1
        LOOPS = (TILES - 4) // RING

        def turns(engine, step, chain=None, links=0):
            def plain(t):
                step(t, t % RING, lambda n: 0 <= t + n < TILES)

            for t in range(FIRST, PEELED):
                plain(t)
            with engine.Fori(0, LOOPS) as g:
                if chain:
                    chain.enter(g, RING * links)
                for i in range(RING):
                    step(g * RING + PEELED + i, (PEELED + i) % RING, lambda n: True)
                if chain:
                    chain.leave(LOOPS)
            for t in range(PEELED + LOOPS * RING, LAST):
                plain(t)

        with nc.Block() as block:
            @block.sync
            def _(sp):
                for t, n in zip(raw, ("Wq", "Wkv", "Wo")):
                    sp.dma_start(t[:], w[f"a_{n}"]).then_inc(s[f"{n}_loaded"], 16)
                clear_blocks(core, sp)

            @block.gpsimd
            def _(pool):
                nc.gpsimd.memset(v[:, :, :, HD:VW], 1.0)
                nc.gpsimd.memset(less_scale[:], -SCALE)
                nc.gpsimd.memset(minus_half[:], -0.5).then_inc(s["consts_set"], 1)
                inverse_deviation(core, pool, s["variance_ready"], s["scale_ready"])
                pool.wait_ge(s["consts_set"], 1)

                def step(t, at, on):
                    if on(1):
                        pool.wait_ge(s["squares_summed"], t + 2)
                        n = norm[:, (at + 1) % RING, :]
                        nc.gpsimd.tensor_tensor(n, n, minus_half[:], ALU.pow).then_inc(s["norm_ready"], 1)
                    if on(2):
                        pool.wait_ge(s["q_copied"], t + 3)
                        pool.wait_ge(s["k_copied"], t + 3)
                        qk_at = qk[:, (at + 2) % RING]
                        nc.gpsimd.tensor_tensor(squares[:], qk_at, qk_at, ALU.mult).then_inc(s["squares_ready"], 1)

                turns(pool, step)

            @block.tensor
            def _(pe):
                pe.wait_ge(s["consts_set"], 1)

                def step(t, at, on):
                    if on(0):
                        pe.wait_ge(s["unit_ready"], t + 1)
                        if on(1):
                            pe.wait_ge(s["q_copied"], t + 2)
                            pe.wait_ge(s["k_copied"], t + 2)
                        for c in range(JT):
                            last = nc.tensor.transpose(ps_q[:, c * SEQ:(c + 1) * SEQ],
                                                       qk[:, at, 0, c * P:(c + 1) * P], ident[:])
                        last.then_inc(s["q_turned"], 1)
                        for c in range(JT):
                            last = nc.tensor.transpose(ps_k[:, c * SEQ:(c + 1) * SEQ],
                                                       qk[:, at, 1, c * P:(c + 1) * P], ident[:])
                        last.then_inc(s["k_turned"], 1)
                    if on(-1):
                        pe.wait_ge(s["mixed_ready"], t)
                        if on(1):
                            pe.wait_ge(s["v_copied"], t + 2)
                        for c in range(JT):
                            last = nc.tensor.transpose(ps_v[:, c * SEQ:(c + 1) * SEQ],
                                                       mixed[:, c * P:(c + 1) * P], ident[:])
                        last.then_inc(s["mixed_turned"], 1)
                    if on(2):
                        pe.wait_ge(s["xn_ready"], t + 3)
                        if on(-1):
                            pe.wait_ge(s["x_updated"], t)
                        for k in range(KT):
                            last = nc.tensor.transpose(ps_x[:, k * P:(k + 1) * P],
                                                       xn[:, (at + 2) % RING, k * P:(k + 1) * P], ident[:])
                        last.then_inc(s["xn_turned"], 1)
                    if on(0):
                        pe.wait_ge(s["qt_ready"], t + 1)
                        pe.wait_ge(s["kt_ready"], t + 1)
                        for o in range(SIDES):
                            part = slice(o * HD, (o + 1) * HD)
                            for c in range(JT):
                                last = nc.tensor.matmul(ps_s[o][:, c * SEQ:(c + 1) * SEQ], k_t[part, c, :],
                                                        q_t[part, c, :], start=True, stop=True)
                            last.then_inc(s["scores_ready"], 1)
                    if on(2):
                        pe.wait_ge(s["xn_low"], t + 3)
                    if on(-1):
                        pe.wait_ge(s["mixed_low"], t)
                        pe.wait_ge(s["w_low"], 3)
                        for c in range(JT):
                            last = product(nc, ps_x[:, DM:2 * DM], [a[:, c, :] for a in mixed_t],
                                           [a[:, c, :] for a in s_o], c == 0, c == JT - 1)
                        last.then_inc(s["out_ready"], 1)
                    if on(2):
                        pe.wait_ge(s["w_low"], 2)
                        for bank, weights, ready in ((ps_q, [a[:] for a in s_q], "q_ready"),
                                                     (ps_k, [a[:, :, 0:INNER] for a in s_kv], "k_ready"),
                                                     (ps_v, [a[:, :, INNER:] for a in s_kv], "v_ready")):
                            for k in range(KT):
                                last = product(nc, bank[:], [a[:, k, :] for a in xnt], [a[:, k, :] for a in weights],
                                               k == 0, k == KT - 1)
                            last.then_inc(s[ready], 1)
                    if on(0):
                        for o in range(SIDES):
                            pe.wait_ge(s["probs_ready"], SIDES * t + o + 1)
                            for c in range(JT):
                                last = nc.tensor.matmul(ps_o[o][:, c * VW:(c + 1) * VW],
                                                        probs[:, o, c * SEQ:(c + 1) * SEQ],
                                                        v[:, at, SIDES * c + o, :], start=True, stop=True)
                        last.then_inc(s["heads_ready"], 1)

                turns(pe, step)

            @block.scalar
            def _(ac):
                for t, (hi, _), n in zip(raw, split, ("Wq", "Wkv", "Wo")):
                    ac.wait_ge(s[f"{n}_loaded"], 16)
                    nc.scalar.activation(hi[:], t[:], ACT.Copy).then_inc(s["w_high"], 1)
                nc.scalar.preload_act_table(ACT.Exp)

                def step(t, at, on):
                    if on(0):
                        ac.wait_ge(s["q_turned"], t + 1)
                        nc.scalar.activation(q_t[:].rearrange("p c t -> p (c t)"), ps_q[:],
                                             ACT.Copy).then_inc(s["qt_ready"], 1)
                    if on(-1):
                        ac.wait_ge(s["mixed_turned"], t)
                        nc.scalar.activation(mixed_t[0][:].rearrange("p c t -> p (c t)"), ps_v[:],
                                             ACT.Copy).then_inc(s["mixed_high"], 1)
                    if on(2):
                        ac.wait_ge(s["xn_turned"], t + 3)
                        nc.scalar.activation(xnt[0][:].rearrange("p k t -> p (k t)"), ps_x[:, 0:DM],
                                             ACT.Copy).then_inc(s["xn_high"], 1)
                    if on(0):
                        if on(-1):
                            ac.wait_ge(s["heads_ready"], t)
                        for o in range(SIDES):
                            ac.wait_ge(s["scores_ready"], SIDES * t + o + 1)
                            nc.scalar.activation(probs[:, o, :], ps_s[o][:], ACT.Exp, bias=less_scale[:, 0:1],
                                                 scale=SCALE).then_inc(s["probs_ready"], 1)
                    if on(2):
                        ac.wait_ge(s["q_ready"], t + 3)
                        nc.scalar.activation(qk[:, (at + 2) % RING, 0, :], ps_q[:], ACT.Copy).then_inc(s["q_copied"], 1)
                        ac.wait_ge(s["k_ready"], t + 3)
                        nc.scalar.activation(qk[:, (at + 2) % RING, 1, :], ps_k[:], ACT.Copy).then_inc(s["k_copied"], 1)

                turns(ac, step)

            @block.vector
            def _(dve):
                chain = Chain(dve, s["chain"])
                link = chain.link
                variance(core, dve, chain, s["variance_ready"])
                dve.wait_ge(s["consts_set"], 1)
                dve.wait_ge(s["scale_ready"], 1)

                def entry(a, j):
                    return a[:, bass.ds(j, 1), :].squeeze(1)

                def layer_norm(j, at):
                    nc.vector.tensor_scalar(xn[:, at % RING, :], entry(x, j), core.ln[:, 0, bass.ds(j, 1)],
                                            core.ln[:, 3, bass.ds(j, 1)], ALU.subtract,
                                            ALU.mult).then_inc(s["xn_ready"], 1)

                layer_norm(0, 0)
                dve.wait_ge(s["scale_ready"], 2)
                split_low(core, dve, [t[:] for t in raw], split, s["w_high"], s["w_low"])
                dve.sem_inc(s["x_updated"], 1)

                def step(t, at, on):
                    if on(0):
                        dve.wait_ge(s["k_turned"], t + 1)
                        nc.vector.tensor_copy(k_t[:].rearrange("p c t -> p (c t)"), ps_k[:]).then_inc(s["kt_ready"], 1)
                    if on(-1):
                        dve.wait_ge(s["mixed_high"], t)
                        nc.vector.tensor_tensor(mixed_t[1][:].rearrange("p c t -> p (c t)"), ps_v[:],
                                                mixed_t[0][:].rearrange("p c t -> p (c t)").bitcast(F32),
                                                ALU.subtract).then_inc(s["mixed_low"], 1)
                    if on(2):
                        dve.wait_ge(s["xn_high"], t + 3)
                        nc.vector.tensor_tensor(xnt[1][:].rearrange("p k t -> p (k t)"), ps_x[:, 0:DM],
                                                xnt[0][:].rearrange("p k t -> p (k t)").bitcast(F32),
                                                ALU.subtract).then_inc(s["xn_low"], 1)
                    if on(1):
                        n = norm[:, (at + 1) % RING, :]
                        dve.wait_ge(s["squares_ready"], t + 2)
                        link(nc.vector.tensor_reduce(n, squares[:].rearrange("p a (h d) -> p (a h) d", d=HD),
                                                     AX.X, ALU.add))
                        nc.vector.tensor_scalar(n, n, LEAST_NORM ** 2, None, ALU.max).then_inc(s["squares_summed"], 1)
                    if on(3):
                        layer_norm(t + 3, at + 3)
                    if on(-1):
                        xb = entry(x, t - 1)
                        dve.wait_ge(s["out_ready"], t)
                        nc.vector.tensor_tensor(xb, xb, ps_x[:, DM:2 * DM], ALU.add).then_inc(s["x_updated"], 1)
                        dve.wait_ge(s["x_updated"], t + 1)
                        nc.vector.bn_stats(entry(core.stats, t - 1), xb)
                    if on(1):
                        dve.wait_ge(s["norm_ready"], t + 2)
                        qk_at = qk[:, (at + 1) % RING].rearrange("p a (h d) -> p (a h) d", d=HD)
                        nc.vector.tensor_tensor(qk_at, qk_at, norm[:, (at + 1) % RING].unsqueeze(2)
                                                .to_broadcast([P, 2 * HEADS, HD]), ALU.mult).then_inc(s["unit_ready"], 1)
                    if on(2):
                        dve.wait_ge(s["v_ready"], t + 3)
                        nc.vector.tensor_copy(v[:, (at + 2) % RING, :, 0:HD],
                                              ps_v[:].rearrange("p (h d) -> p h d", d=HD)).then_inc(s["v_copied"], 1)
                    if on(0):
                        dve.wait_ge(s["heads_ready"], t + 1)
                        for o in range(SIDES):
                            sums = ps_o[o][:, 0:JT * VW].rearrange("p (c d) -> p c d", d=VW)[:, :, HD]
                            last = nc.vector.tensor_scalar(inv_sum[:, o, :], sums, LEAST_SUM, None, ALU.max)
                        link(last)
                        link(nc.vector.reciprocal(inv_sum[:], inv_sum[:]))
                        for o in range(SIDES):
                            last = nc.vector.tensor_tensor(
                                mixed[:].rearrange("p (c o d) -> p c o d", o=SIDES, d=HD)[:, :, o, :],
                                ps_o[o][:, 0:JT * VW].rearrange("p (c d) -> p c d", d=VW)[:, :, 0:HD],
                                inv_sum[:, o, :].unsqueeze(2).to_broadcast([P, JT, HD]), ALU.mult)
                        last.then_inc(s["mixed_ready"], 1)

                turns(dve, step, chain, 3)
        core.retire(s)


def as_is(a):
    return a


def rows(a):
    return a.reshape(-1, P, *a.shape[1:]).swapaxes(0, 1)


def turned(a):
    return rows(a.T)


def cross_layout(name, prefix, underscore):
    at = {f"{name}_W{c}": (f"{prefix}_W{underscore}{c}", turned) for c in "qkvo"}
    at |= {f"{name}_b{c}": (f"{prefix}_b{underscore}{c}", rows) for c in "qk"}
    return at | {f"{name}_b{c}": (f"{prefix}_b{underscore}{c}", as_is) for c in "vo"}


def stacked(a):
    return a.reshape(a.shape[0], -1, P, a.shape[2]).swapaxes(1, 2)


def joined(lay):
    return lambda a, b: lay(np.concatenate([a, b]))


LAYOUT = {
    "x": ("x", lambda a: a.swapaxes(0, 1)),
    "W_in": ("L0_attn_W_in", rows),
    "conv_w": ("L0_attn_conv_w", lambda a: rows(a[:, 0])),
    "W_B": ("L0_attn_W_B", rows),
    "W_C": ("L0_attn_W_C", rows),
    "W_delta": ("L0_attn_W_delta", rows),
    "delta_base": ("L0_attn_delta_base", rows),
    "W_tau": ("L0_attn_W_tau", rows),
    "A_log": ("L0_attn_A_log", rows),
    "W_out": ("L0_attn_W_out", rows),
    "context": ("ctx_1024", lambda a: a.swapaxes(0, 1)),
    "causal": ("mask_SxS2_fk0", as_is),
    "padding": ("mask_BxS2_bf0", as_is),
    **cross_layout("x0", "L0_xattn", ""),
    **cross_layout("x1", "L1_xattn", "_"),
    "a_Wq": ("L1_attn_Wq", rows),
    "a_Wkv": ("L1_attn_Wkv", rows),
    "a_Wo": ("L1_attn_Wo", rows),
    "e0_Wr": ("L0_ffn_gate_w", rows),
    "e0_br": ("L0_ffn_gate_b", as_is),
    "e0_W1": (("L0_ffn_sw1", "L0_ffn_rw1"), joined(stacked)),
    "e0_b1": (("L0_ffn_sb1", "L0_ffn_rb1"), joined(lambda a: a.reshape(len(a), -1, P).transpose(2, 0, 1))),
    "e0_W2": (("L0_ffn_sw2", "L0_ffn_rw2"), joined(stacked)),
    "e0_b2": (("L0_ffn_sb2", "L0_ffn_rb2"), joined(as_is)),
    "e1_Wr": ("L1_ffn_Wr", turned),
    "e1_br": ("L1_ffn_br", as_is),
    "e1_W1": ("L1_ffn_W1", lambda a: stacked(a.swapaxes(1, 2))),
    "e1_b1": ("L1_ffn_b1", lambda a: a.reshape(len(a), -1, P).transpose(2, 0, 1)),
    "e1_W2": ("L1_ffn_W2", lambda a: stacked(a.swapaxes(1, 2))),
    "e1_b2": ("L1_ffn_b2", as_is),
    "e1_gamma": ("L1_ffn_gamma", as_is),
    "e1_beta": ("L1_ffn_beta", as_is),
}


def constants():
    at = {"side": np.kron(np.eye(P // 16), np.ones((16, 1))).astype(np.float32)}
    at["e1_upper"] = np.triu(np.ones((P, P), np.float32), 1)
    at["e1_levels"] = np.broadcast_to(np.arange(TILES * SEQ // GT, dtype=np.float32) * GT, (P, 8, TILES * SEQ // GT))
    blocks = (2 * TILES * SEQ + 8 * (GT - 1)) // GT
    at["e1_numbers"] = np.broadcast_to(np.arange(blocks, dtype=np.float32)[:, None], (P, blocks, 8))
    for name, n in (("e0", 4), ("e1", 8)):
        at[f"{name}_before"] = np.broadcast_to(np.tril(np.ones((n, n), np.float32), -1), (P, n, n))
    return at


def decoder(nc, w, out):
    with ExitStack() as ctx:
        core = Core(nc, ctx)
        core.x = core.keep("x_stream", [P, TILES, DM])
        core.stats = core.keep("stats", [P, TILES, 6])
        core.ln = core.keep("ln", [P, 4, TILES])
        core.minus_half = core.keep("minus_half", [P, TILES])
        core.ident = core.keep("ident", [P, P])
        experts_1, core.block_rows = w["e1_W1"].shape[0], GT
        core.blocks = (2 * TILES * SEQ + experts_1 * (GT - 1)) // GT
        core.sorted_in, core.sorted_out = (
            nc.dram_tensor(name, (core.blocks * GT, DM), F32, kind="Internal").ap()
            for name in ("sorted_in", "sorted_out"))
        core.zeros = core.keep("zeros", [P, DM])
        core.blocks_cleared = core.sem("blocks_cleared")
        load(core, w)
        state_space(core, w)
        cross_attention(core, w, "x0", masked=False)
        experts(core, w, "e0", shared=2, routed=4, softmax_first=True)
        self_attention(core, w)
        cross_attention(core, w, "x1", masked=True)
        routed_experts(core, w, "e1", out)


def kernel(**inputs):
    import concourse.bacc as bacc
    from concourse.bass_utils import run_bass_kernel_spmd

    nc = bacc.Bacc("TRN2", target_bir_lowering=False, num_devices=1)
    arrays, w = {}, {}
    for name, (source, lay) in LAYOUT.items():
        sources = (source,) if isinstance(source, str) else source
        arrays[name] = lay(*(np.asarray(inputs[n]) for n in sources))
    arrays = {"in_" + n: np.ascontiguousarray(a) for n, a in (arrays | constants()).items()}
    for name, a in arrays.items():
        w[name[3:]] = nc.dram_tensor(name, a.shape, mybir.dt.from_np(a.dtype), kind="ExternalInput").ap()
    out = nc.dram_tensor("out", (SEQ, BATCH, DM), F32, kind="ExternalOutput").ap()
    decoder(nc, w, out)
    r = run_bass_kernel_spmd(nc, [arrays], core_ids=[0])
    return r.results[0]["out"].swapaxes(0, 1)
```
